# Optimizing a Trainium2 kernel written in Bass

```python
import numpy as np
import jax
import jax.numpy as jnp

def _softmax(x, axis=-1):
    return jax.nn.softmax(x, axis=axis)

def _gelu(x):
    return jax.nn.gelu(x, approximate=True)

def _silu(x):
    return jax.nn.silu(x)

def _sigmoid(x):
    return jax.nn.sigmoid(x)

def _layernorm(x, axis=-1, eps=1e-05):
    m = jnp.mean(x, axis=axis, keepdims=True)
    v = jnp.var(x, axis=axis, keepdims=True)
    return (x - m) / jnp.sqrt(v + eps)

def _scatter_add(tgt, idx, src, axis=0):
    return tgt.at[idx].add(src)

def _segment_sum(src, seg, n):
    return jax.ops.segment_sum(src, seg, n)
kernel_name = 'mk_decoder_postln_d1_seqx_r4_565eb8'

def setup_inputs(seed: int=0):
    np.random.seed(seed)
    _w = jnp.asarray

    def _rec_inputs():
        import jax
        import jax.numpy as jnp
        _rk = jax.random.key(seed)
        x = -0.0002928 + 1 * jax.random.normal(jax.random.fold_in(_rk, 1), (8, 512, 256), jnp.float32)
        _lenS = 512 - jax.random.randint(jax.random.fold_in(_rk, 7), (8,), 0, max(1, 512 // 4) + 1, jnp.int32)
        _lenS2 = 512 - jax.random.randint(jax.random.fold_in(_rk, 8), (8,), 0, max(1, 512 // 4) + 1, jnp.int32)
        _ctx_1024P = jax.random.normal(jax.random.fold_in(_rk, 11), (8, 16, 256), jnp.float32)
        _ctx_1024c = jax.random.dirichlet(jax.random.fold_in(_rk, 511), 0.3 * jnp.ones((16,), jnp.float32), (8, 512))
        _ctx_1024t = jnp.einsum('bsk,bkd->bsd', _ctx_1024c, _ctx_1024P)
        _ctx_1024t = _ctx_1024t * jax.lax.rsqrt(jnp.mean(jnp.square(_ctx_1024t)) + 1e-12) * 0.953939
        ctx_1024 = -1.39393e-06 + 0.999914 * (_ctx_1024t + 0.3 * jax.random.normal(jax.random.fold_in(_rk, 611), (8, 512, 256), jnp.float32))
        return (x, ctx_1024)
    x, ctx_1024 = _rec_inputs()

    def _L0_attn_setup():
        import jax, jax.numpy as jnp
        import numpy as np
        HIDDEN = 256
        NUM_HEADS = 16
        NUM_KV = 4
        HEAD_DIM = HIDDEN // NUM_HEADS
        GROUPS = NUM_HEADS // NUM_KV
        SCALE = HEAD_DIM ** 0.5
        key = jax.random.key(seed)
        ks = jax.random.split(key, 9)
        s = 0.02
        B, N = (4, 512)
        return {'x': jax.random.normal(ks[0], (B, N, HIDDEN), dtype=jnp.float32), 'Wq': jax.random.normal(ks[1], (HIDDEN, NUM_HEADS * HEAD_DIM), dtype=jnp.float32) * s, 'bq': jnp.zeros((NUM_HEADS * HEAD_DIM,), dtype=jnp.float32), 'Wk': jax.random.normal(ks[2], (HIDDEN, NUM_KV * HEAD_DIM), dtype=jnp.float32) * s, 'bk': jnp.zeros((NUM_KV * HEAD_DIM,), dtype=jnp.float32), 'Wv': jax.random.normal(ks[3], (HIDDEN, NUM_KV * HEAD_DIM), dtype=jnp.float32) * s, 'bv': jnp.zeros((NUM_KV * HEAD_DIM,), dtype=jnp.float32), 'Wo': jax.random.normal(ks[4], (NUM_HEADS * HEAD_DIM, HIDDEN), dtype=jnp.float32) * s, 'bo': jnp.zeros((HIDDEN,), dtype=jnp.float32)}
    _L0_attn_all = _L0_attn_setup()
    _L0_attn_in = {k: v for k, v in _L0_attn_all.items() if k in ('Wq', 'bq', 'Wk', 'bk', 'Wv', 'bv', 'Wo', 'bo')}
    del _L0_attn_all

    def _L0_xattn_setup():
        import jax, jax.numpy as jnp
        import numpy as np
        B, S, D, H, DH = (2, 512, 256, 16, 64)
        ATTN_SCALE = 8.0
        key = jax.random.key(seed)
        ks = jax.random.split(key, 10)
        scale = 0.02
        return {'query_input': jax.random.normal(ks[0], (B, S, D), dtype=jnp.float32), 'key_input': jax.random.normal(ks[1], (B, S, D), dtype=jnp.float32), 'value_input': jax.random.normal(ks[2], (B, S, D), dtype=jnp.float32), 'W_Q': jax.random.normal(ks[3], (H, D, DH), dtype=jnp.float32) * scale, 'W_K': jax.random.normal(ks[4], (H, D, DH), dtype=jnp.float32) * scale, 'W_V': jax.random.normal(ks[5], (H, D, DH), dtype=jnp.float32) * scale, 'W_O': jax.random.normal(ks[6], (H, DH, D), dtype=jnp.float32) * scale, 'b_Q': jnp.zeros((H, DH), dtype=jnp.float32), 'b_K': jnp.zeros((H, DH), dtype=jnp.float32), 'b_V': jnp.zeros((H, DH), dtype=jnp.float32), 'b_O': jnp.zeros((D,), dtype=jnp.float32)}
    _L0_xattn_all = _L0_xattn_setup()
    _L0_xattn_in = {k: v for k, v in _L0_xattn_all.items() if k in ('W_Q', 'W_K', 'W_V', 'W_O', 'b_Q', 'b_K', 'b_V', 'b_O')}
    del _L0_xattn_all

    def _L0_ffn_setup():
        import jax, jax.numpy as jnp
        import numpy as np
        TOP_K = 8
        CAPACITY = 128

        def _silu(x):
            return x * jax.nn.sigmoid(x)
        key = jax.random.key(seed)
        ks = jax.random.split(key, 7)
        B, S, H, E, I, Is = (2, 256, 256, 64, 128, 512)
        s = 0.05
        return {'hidden_states': jax.random.normal(ks[0], (B, S, H), jnp.float32), 'gate_w': jax.random.normal(ks[1], (H, E), jnp.float32) * s, 'shared_gate_w': jax.random.normal(ks[2], (H, 1), jnp.float32) * s, 'shared_gate_up_w': jax.random.normal(ks[3], (H, 2 * Is), jnp.float32) * s, 'shared_down_w': jax.random.normal(ks[4], (Is, H), jnp.float32) * s, 'expert_gate_up_w': jax.random.normal(ks[5], (E, H, 2 * I), jnp.float32) * s, 'expert_down_w': jax.random.normal(ks[6], (E, I, H), jnp.float32) * s}
    _L0_ffn_all = _L0_ffn_setup()
    _L0_ffn_in = {k: v for k, v in _L0_ffn_all.items() if k in ('gate_w', 'shared_gate_w', 'shared_gate_up_w', 'shared_down_w', 'expert_gate_up_w', 'expert_down_w')}
    del _L0_ffn_all
    return {'x': x, 'ctx_1024': ctx_1024, 'L0_attn_Wq': _L0_attn_in['Wq'], 'L0_attn_bq': _L0_attn_in['bq'], 'L0_attn_Wk': _L0_attn_in['Wk'], 'L0_attn_bk': _L0_attn_in['bk'], 'L0_attn_Wv': _L0_attn_in['Wv'], 'L0_attn_bv': _L0_attn_in['bv'], 'L0_attn_Wo': _L0_attn_in['Wo'], 'L0_attn_bo': _L0_attn_in['bo'], 'L0_xattn_W_Q': _L0_xattn_in['W_Q'], 'L0_xattn_W_K': _L0_xattn_in['W_K'], 'L0_xattn_W_V': _L0_xattn_in['W_V'], 'L0_xattn_W_O': _L0_xattn_in['W_O'], 'L0_xattn_b_Q': _L0_xattn_in['b_Q'], 'L0_xattn_b_K': _L0_xattn_in['b_K'], 'L0_xattn_b_V': _L0_xattn_in['b_V'], 'L0_xattn_b_O': _L0_xattn_in['b_O'], 'L0_ffn_gate_w': _L0_ffn_in['gate_w'], 'L0_ffn_shared_gate_w': _L0_ffn_in['shared_gate_w'], 'L0_ffn_shared_gate_up_w': _L0_ffn_in['shared_gate_up_w'], 'L0_ffn_shared_down_w': _L0_ffn_in['shared_down_w'], 'L0_ffn_expert_gate_up_w': _L0_ffn_in['expert_gate_up_w'], 'L0_ffn_expert_down_w': _L0_ffn_in['expert_down_w']}

def reference(x, ctx_1024, L0_attn_Wq, L0_attn_bq, L0_attn_Wk, L0_attn_bk, L0_attn_Wv, L0_attn_bv, L0_attn_Wo, L0_attn_bo, L0_xattn_W_Q, L0_xattn_W_K, L0_xattn_W_V, L0_xattn_W_O, L0_xattn_b_Q, L0_xattn_b_K, L0_xattn_b_V, L0_xattn_b_O, L0_ffn_gate_w, L0_ffn_shared_gate_w, L0_ffn_shared_gate_up_w, L0_ffn_shared_down_w, L0_ffn_expert_gate_up_w, L0_ffn_expert_down_w):
    import jax
    import jax.numpy as jnp

    def _L0_attn_ref(x, Wq, bq, Wk, bk, Wv, bv, Wo, bo):
        import jax, jax.numpy as jnp
        import numpy as np
        HIDDEN = 256
        NUM_HEADS = 16
        NUM_KV = 4
        HEAD_DIM = HIDDEN // NUM_HEADS
        GROUPS = NUM_HEADS // NUM_KV
        SCALE = HEAD_DIM ** 0.5
        B, N, _ = x.shape
        q = x @ Wq + bq
        k = x @ Wk + bk
        v = x @ Wv + bv
        q = q.reshape(B, N, NUM_HEADS, HEAD_DIM).transpose(0, 2, 1, 3)
        q = q.reshape(B, NUM_KV, GROUPS, N, HEAD_DIM).transpose(0, 2, 1, 3, 4)
        k = k.reshape(B, N, NUM_KV, HEAD_DIM).transpose(0, 2, 1, 3)
        v = v.reshape(B, N, NUM_KV, HEAD_DIM).transpose(0, 2, 1, 3)
        scores = jnp.einsum('bghnd,bhsd->bghns', q, k)
        attn = jax.nn.softmax(scores / SCALE, axis=-1)
        out = jnp.einsum('bghns,bhsd->bghnd', attn, v)
        out = out.transpose(0, 3, 1, 2, 4).reshape(B, N, NUM_HEADS * HEAD_DIM)
        return out @ Wo + bo

    def _L0_xattn_ref(query_input, key_input, value_input, W_Q, W_K, W_V, W_O, b_Q, b_K, b_V, b_O):
        import jax, jax.numpy as jnp
        import numpy as np
        B, S, D, H, DH = (2, 512, 256, 16, 64)
        ATTN_SCALE = 8.0
        q = jnp.einsum('bsd,hde->bshe', query_input, W_Q) + b_Q
        k = jnp.einsum('bsd,hde->bshe', key_input, W_K) + b_K
        v = jnp.einsum('bsd,hde->bshe', value_input, W_V) + b_V
        scores = jnp.einsum('bqhe,bkhe->bhqk', q, k) / ATTN_SCALE
        causal = jnp.tril(jnp.ones((S, S), dtype=bool))
        scores = jnp.where(causal[None, None, :, :], scores, -jnp.inf)
        pattern = jax.nn.softmax(scores, axis=-1)
        pattern = jnp.where(jnp.isnan(pattern), jnp.zeros_like(pattern), pattern)
        z = jnp.einsum('bhqk,bkhe->bqhe', pattern, v)
        out = jnp.einsum('bqhe,hed->bqd', z, W_O) + b_O
        return out

    def _L0_ffn_ref(hidden_states, gate_w, shared_gate_w, shared_gate_up_w, shared_down_w, expert_gate_up_w, expert_down_w):
        import jax, jax.numpy as jnp
        import numpy as np
        TOP_K = 8
        CAPACITY = 128

        def _silu(x):
            return x * jax.nn.sigmoid(x)
        B, S, H = hidden_states.shape
        x = hidden_states.reshape(-1, H)
        T = x.shape[0]
        E = gate_w.shape[1]
        Is = shared_gate_up_w.shape[1] // 2
        I = expert_gate_up_w.shape[2] // 2
        gu = x @ shared_gate_up_w
        shared = _silu(gu[:, :Is]) * gu[:, Is:] @ shared_down_w
        shared = shared * jax.nn.sigmoid(x @ shared_gate_w)
        logits = x @ gate_w
        probs = jax.nn.softmax(logits.astype(jnp.float32), axis=-1)
        w, idx = jax.lax.top_k(probs, TOP_K)
        w = (w / jnp.sum(w, axis=-1, keepdims=True)).astype(x.dtype)
        e_flat = idx.reshape(-1)
        w_flat = w.reshape(-1)
        A = e_flat.shape[0]
        tok = jnp.arange(A) // TOP_K
        onehot = jax.nn.one_hot(e_flat, E, dtype=jnp.int32)
        pos = jnp.take_along_axis(jnp.cumsum(onehot, axis=0) - 1, e_flat[:, None], axis=1)[:, 0]
        slot = jnp.minimum(pos, CAPACITY)
        buf = jnp.zeros((E, CAPACITY + 1, H), x.dtype).at[e_flat, slot].set(x[tok])
        gu_e = jnp.einsum('ech,ehf->ecf', buf, expert_gate_up_w)
        act = _silu(gu_e[..., :I]) * gu_e[..., I:]
        out_e = jnp.einsum('eci,eih->ech', act, expert_down_w)
        y = out_e[e_flat, slot] * w_flat[:, None]
        y = jnp.where((pos < CAPACITY)[:, None], y, jnp.zeros_like(y))
        y = y.reshape(T, TOP_K, H).sum(axis=1)
        return (y + shared).reshape(B, S, H)
    x = _layernorm(x + _L0_attn_ref(x, L0_attn_Wq, L0_attn_bq, L0_attn_Wk, L0_attn_bk, L0_attn_Wv, L0_attn_bv, L0_attn_Wo, L0_attn_bo), axis=-1)
    x = _layernorm(x + _L0_xattn_ref(x, ctx_1024, ctx_1024, L0_xattn_W_Q, L0_xattn_W_K, L0_xattn_W_V, L0_xattn_W_O, L0_xattn_b_Q, L0_xattn_b_K, L0_xattn_b_V, L0_xattn_b_O), axis=-1)
    x = _layernorm(x + _L0_ffn_ref(x, L0_ffn_gate_w, L0_ffn_shared_gate_w, L0_ffn_shared_gate_up_w, L0_ffn_shared_down_w, L0_ffn_expert_gate_up_w, L0_ffn_expert_down_w), axis=-1)
    return x

_drawn_inputs = setup_inputs


def setup_inputs(seed=0):
    import zlib

    import numpy as np

    out = dict(_drawn_inputs(seed))
    spreads = {'L0_attn_bq': (0.0, 0.8),
     'L0_attn_bk': (0.0, 0.8),
     'L0_attn_bv': (0.0, 0.1),
     'L0_attn_bo': (0.0, 0.1),
     'L0_xattn_b_Q': (0.0, 0.8),
     'L0_xattn_b_K': (0.0, 0.8),
     'L0_xattn_b_V': (0.0, 0.1),
     'L0_xattn_b_O': (0.0, 0.1)}
    factors = {'L0_attn_Wq': 8.0,
     'L0_attn_Wk': 8.0,
     'L0_attn_Wv': 8.0,
     'L0_xattn_W_Q': 8.0,
     'L0_xattn_W_K': 8.0}
    for name, (base, spread) in spreads.items():
        noise = np.random.default_rng([zlib.crc32(name.encode()), seed]).standard_normal(out[name].shape)
        drawn = base * np.exp(spread * noise) if base else spread * noise
        out[name] = jnp.asarray(drawn.astype(out[name].dtype))
    for name, factor in factors.items():
        out[name] = (out[name] * factor).astype(out[name].dtype)
    return out
```

```python
from contextlib import ExitStack

import concourse.bass as bass
from concourse import mybir

F32 = mybir.dt.float32
F32R = mybir.dt.float32r
BF16 = mybir.dt.bfloat16
U32 = mybir.dt.uint32
ALU = mybir.AluOpType
ACT = mybir.ActivationFunctionType
AX_X = mybir.AxisListType.X

P = 128
B, SEQ, D = 8, 512, 256
TOK = B * SEQ
NT = SEQ // P
DC = D // P
H = 16
UNITS = H // 2
HD1, KV1 = 16, 4
HD2 = 64
STEPS = UNITS * NT
E, TOPK, CAP = 64, 8, 128
FS = 512
FI = 128
ROW = D + E
NROW = TOK + CAP
EPS = 1e-5
MASKED = -1e30
YS = 2
EU = 4


def attention_timeline(projections):
    order = [("P2", 0)] if projections else []
    for n in range(STEPS + 3):
        if n < STEPS:
            order.append(("S", n))
        if 0 <= n - 1 < STEPS:
            order.append(("R", n - 1))
        if projections and n < STEPS and n % NT == 1 and n // NT + 1 < UNITS:
            order.append(("P2", n // NT + 1))
        if 0 <= n - 2 < STEPS:
            order.append(("T", n - 2))
        if n >= 3 and (n - 3) % NT == NT - 1:
            order.append(("PV", (n - 3) // NT))
    return order


def batch_timeline():
    t = [("xT", c) for c in range(DC)] + [("q1", c) for c in range(DC)] + [("k1", 0), ("v1", 0)]
    t += [("cT", c) for c in range(DC)] + [("V2", i) for i in range(2 * NT)]
    t += [(k + "1" if k in ("S", "R", "T", "PV") else k, n) for k, n in attention_timeline(False)]
    t += [("o1", i) for i in range(2)] + [("ln1", 0)] + [("x1T", c) for c in range(DC)]
    t += [(k + "2" if k in ("S", "R", "T", "PV") else k, n) for k, n in attention_timeline(True)]
    t += [("o2", i) for i in range(2)] + [("ln2", 0)] + [("x2T", c) for c in range(DC)]
    t += [("gate", 0), ("keys", 0)] + [("up", f) for f in range(FS // P)] + [("down", i) for i in range(2)]
    return t


USES = {"xT": ["xT"], "q1": ["q1"], "k1": ["k1"], "v1": ["v1"], "cT": ["cT"], "V2": ["V2"], "PV1": ["PV1"],
        "o1": ["o1"], "x1T": ["x1T"], "P2": ["q2", "k2"], "PV2": ["PV2"], "o2": ["o2"], "x2T": ["x2T"],
        "gate": ["gate"], "keys": ["keys"], "up": ["sg", "su"], "down": ["down"]}


def build(nc, x, ctx, Wq1, bq1, Wk1, bk1, Wv1, bv1, Wo1, bo1, WQ, WK, WV, WO, bQ, bK, bV, bO,
          gate_w, sgate_w, sup_w, sdown_w, eup_w, edown_w, out):
    order = batch_timeline()
    g_index = {}
    for kind, n in order:
        for use in USES.get(kind, []):
            g_index[use, n] = len(g_index)
    NG = len(g_index)
    assert NG % 2 == 0

    with ExitStack() as stack:
        def sb(name, shape, dt=F32):
            return stack.enter_context(nc.sbuf_tensor(name, shape, dt))

        def psum(name, shape, dt=F32):
            return stack.enter_context(nc.psum_tensor(name, shape, dt))

        def sem(name):
            return stack.enter_context(nc.semaphore(name))

        q_parts = nc.dram_tensor("q_parts", (2, H * HD1, SEQ), F32).ap()
        k_parts = nc.dram_tensor("k_parts", (2, KV1 * HD1, SEQ), F32).ap()
        table = nc.dram_tensor("token_table", (NROW, ROW), F32).ap()
        key_rows = nc.dram_tensor("key_rows", (E, TOK), F32).ap()
        sums = [nc.dram_tensor(f"sum_{i}", (NROW, D), F32).ap() for i in range(YS)]

        S = psum("S", [P, 2, 2, 512])
        T = psum("T", [P, 2, 512])
        G = psum("G", [P, 2, 512])

        ident = sb("ident", [P, P])
        identb = sb("identb", [P, P], BF16)
        maskb = sb("maskb", [P, P], BF16)
        wq1 = sb("wq1", [P, DC, H * HD1])
        wk1 = sb("wk1", [P, DC, KV1 * HD1])
        wv1 = sb("wv1", [P, DC, KV1 * HD1])
        wo1 = sb("wo1", [P, UNITS, D])
        wq2 = sb("wq2", [P, DC, H * HD2])
        wk2 = sb("wk2", [P, DC, H * HD2])
        wv2 = sb("wv2", [P, DC, H * HD2])
        wo2 = sb("wo2", [P, UNITS, D])
        gw = sb("gw", [P, DC, E + 1])
        supw = sb("supw", [P, DC, 2 * FS])
        sdownw = sb("sdownw", [P, FS // P, D])
        bq1c = sb("bq1c", [P, DC])
        bk1c = sb("bk1c", [KV1 * HD1, 1])
        bv1c = sb("bv1c", [P, KV1])
        bqc = sb("bqc", [P, UNITS])
        bkc = sb("bkc", [P, UNITS])
        bvc = sb("bvc", [P, UNITS])
        bo1r = sb("bo1r", [P, D])
        bo2r = sb("bo2r", [P, D])
        token_key = sb("token_key", [P, NT])
        slot_no = sb("slot_no", [P, 1])

        xs = sb("xs", [P, NT, D])
        cs = sb("cs", [P, NT, D])
        xT = sb("xT", [P, DC, SEQ])
        cT = sb("cT", [P, DC, SEQ])
        x1s = sb("x1s", [P, NT, D])
        x2s = sb("x2s", [P, NT, ROW])
        parts = sb("parts", [P, 2, 2, SEQ], F32R)
        k1parts = sb("k1parts", [KV1 * HD1, 2, SEQ], F32R)
        q1st = sb("q1st", [P, 2, 2, SEQ], F32R)
        k1st = sb("k1st", [P, KV1, SEQ], F32R)
        k2z = sb("k2z", [P, 2, 2, 2, SEQ], F32R)
        v1s = sb("v1s", [P, NT, KV1, 32])
        v2s = sb("v2s", [P, NT, H * HD2])
        probs = sb("probs", [P, 2, 2, SEQ])
        pT = sb("pT", [P, 2, 2, NT, SEQ])
        zT = sb("zT", [P, UNITS, SEQ])
        stats = sb("stats", [P, NT, 6])
        mv = sb("mv", [P, NT, 2])
        varps = sb("varps", [P, NT])
        minus_half = sb("minus_half", [P, NT])
        rstd = sb("rstd", [P, NT])
        negmax = sb("negmax", [P, 4, 2])
        rowsum = sb("rowsum", [P, 4, 2])
        rrow = sb("rrow", [P, 4, 2])
        gneg = sb("gneg", [P, NT])
        gsum = sb("gsum", [P, NT])
        gexp = probs[:, 0, 0, 0:NT * E].rearrange("p (t e) -> p t e", t=NT)
        gprob = probs[:, 0, 1, 0:NT * E].rearrange("p (t e) -> p t e", t=NT)
        grest = probs[:, 1, 0, 0:NT * E].rearrange("p (t e) -> p t e", t=NT)
        top8 = sb("top8", [P, NT, TOPK])
        gtmp = sb("gtmp", [P, NT, 4])
        sig = sb("sig", [P, NT])
        keyT = sb("keyT", [E, SEQ])
        hid = v2s[:, 0:2, :].rearrange("p a (b n) -> p (a b) n", b=2)
        tnh = v2s[:, 2, 0:SEQ]
        y0s = v2s[:, 3, :].rearrange("p (t n) -> p t n", t=NT)

        keys = pT[:, 0, 0, :, :].rearrange("p a n -> p (a n)")
        found = pT[:, 0, 1, 0, 0:CAP]
        both = pT[0:E, 0, 1, 1, 0:2 * CAP]
        first = pT[0:E, 0, 1, 2, 0:CAP]
        idxf = pT[:, 0, 1, 3, 0:2 * E].rearrange("p (a e) -> p a e", a=2)
        idx = sb("idx", [P, E], U32)
        idx4 = sb("idx4", [P, 2, EU], U32)
        xg = v2s[:, :, :].rearrange("p a n -> p (a n)")[:, 0:EU * ROW].rearrange("p (s n) -> p s n", s=EU)
        wup = zT[:, :, :].rearrange("p u n -> p (u n)").rearrange("p (s c n) -> p s c n", s=EU * 2, c=DC)
        wdn = pT[:, 1, 0, :, :].rearrange("p a (b n) -> p (a b) n", b=2)
        xgT = pT[:, 1, 1, 0:2, :].rearrange("p a (s n) -> p (a s) n", s=2)
        act = pT[:, 1, 1, 2, :].rearrange("p (s n) -> p s n", s=EU)
        ath = probs[:, 0, 0, :].rearrange("p (s n) -> p s n", s=EU)
        yo = xT[:, :, :].rearrange("p c (b n) -> p (c b) n", b=2)
        fin = xs
        fin1 = cs
        zero = sb("zero", [P, ROW])

        w_in = sem("w_in")
        passed = sem("passed")
        x_in = sem("x_in")
        c_in = sem("c_in")
        consts = sem("consts")
        id_zero = sem("id_zero")
        wprep = sem("wprep")
        g_ready = sem("g_ready")
        g_done = [sem("g_done0"), sem("g_done1")]
        hi_done = sem("hi_done")
        base1 = sem("base1")
        base2 = sem("base2")
        parts_out = sem("parts_out")
        kparts_out = sem("kparts_out")
        k1_in = sem("k1_in")
        q1_in = [sem("q1_in0"), sem("q1_in1")]
        s_ready = sem("s_ready")
        nm_ready = sem("nm_ready")
        p_ready = sem("p_ready")
        rr_ready = sem("rr_ready")
        pn_ready = sem("pn_ready")
        t_ready = sem("t_ready")
        pt_ready = sem("pt_ready")
        res_done = sem("res_done")
        st_done = sem("st_done")
        ag_done = sem("ag_done")
        ve_done = sem("ve_done")
        rs_done = sem("rs_done")
        ln_done = sem("ln_done")
        gmax_done = sem("gmax_done")
        gexp_done = sem("gexp_done")
        gate_step = sem("gate_step")
        keyv_done = sem("keyv_done")
        tanh_done = sem("tanh_done")
        gated = sem("gated")
        table_out = sem("table_out")
        keys_out = sem("keys_out")
        y0_done = sem("y0_done")
        y0_out = sem("y0_out")
        batch_out = sem("batch_out")
        turn_out = sem("turn_out")
        zero_out = sem("zero_out")
        k_in = sem("k_in")
        pick = sem("pick")
        moved = sem("moved")
        first_done = sem("first_done")
        firstT = sem("firstT")
        idx_step = sem("idx_step")
        idx4_done = sem("idx4_done")
        xg_in = [sem(f"xg_in{i}") for i in range(EU)]
        we_in = [sem(f"we_in{i}") for i in range(EU)]
        e_tr = sem("e_tr")
        e_trs = sem("e_trs")
        e_up = sem("e_up")
        e_tanh = sem("e_tanh")
        e_act1 = sem("e_act1")
        e_act = sem("e_act")
        e_down = [sem(f"e_down{i}") for i in range(EU)]
        e_yo = sem("e_yo")
        y_add = [sem(f"y_add{i}") for i in range(EU)]
        f_in = sem("f_in")
        f_step = sem("f_step")
        f_out = sem("f_out")

        NW = 29

        def g_written(eng, b, use, n):
            eng.wait_ge(g_ready, b * NG + g_index[use, n] + 1)

        def g_landed(eng, b, use, n):
            g = g_index[use, n]
            eng.wait_ge(g_done[g % 2], 1 + b * (NG // 2) + g // 2 + 1)

        def g_bank(use, n):
            return G[:, g_index[use, n] % 2, :]

        def g_sem(use, n):
            return g_done[g_index[use, n] % 2]

        def alone(eng):
            eng.sem_inc(passed, 1)

        def step_no(b, phase, n):
            return b * (2 * STEPS) + phase * STEPS + n

        def turn(eng, copy, b, phase, n):
            u, qt = n // NT, n % NT
            nk = NT if phase == 0 else qt + 1
            eng.wait_ge(t_ready, step_no(b, phase, n) + 1)
            if u >= 2:
                g_written(eng, b, f"PV{phase + 1}", u - 2)
            copy(pT[:, u % 2, :, 0:nk, qt * P:(qt + 1) * P],
                 T[:, :, 0:nk * P].rearrange("p j (k n) -> p j k n", k=nk)).then_inc(pt_ready, 1)

        block = stack.enter_context(nc.Block())

        @block.sync
        def _(sp):
            loads = [
                (wq1[:], Wq1.rearrange("(c p) n -> p c n", p=P)),
                (wk1[:], Wk1.rearrange("(c p) n -> p c n", p=P)),
                (wv1[:], Wv1.rearrange("(c p) n -> p c n", p=P)),
                (bq1c[:], bq1.rearrange("(c p) -> p c", p=P)),
                (bk1c[:], bk1.rearrange("(p o) -> p o", o=1)),
                (bo1r[:], bo1.rearrange("(o n) -> o n", o=1).to_broadcast([P, D])),
                (bo2r[:], bO.rearrange("(o n) -> o n", o=1).to_broadcast([P, D])),
                (bqc[:], bQ.rearrange("(u j) e -> (j e) u", j=2)),
                (bkc[:], bK.rearrange("(u j) e -> (j e) u", j=2)),
                (bvc[:], bV.rearrange("(u j) e -> (j e) u", j=2)),
                (wo2[:], WO.rearrange("(u j) e d -> (j e) u d", j=2)),
                (gw[:, :, 0:E], gate_w.rearrange("(c p) n -> p c n", p=P)),
                (gw[:, :, E:E + 1], sgate_w.rearrange("(c p) n -> p c n", p=P)),
                (supw[:], sup_w.rearrange("(c p) n -> p c n", p=P)),
                (sdownw[:], sdown_w.rearrange("(c p) n -> p c n", p=P)),
            ]
            for w, src in ((wq2, WQ), (wk2, WK), (wv2, WV)):
                for c in range(DC):
                    loads.append((w[:, c, :].rearrange("p (h e) -> p h e", h=H),
                                  src[:, c * P:(c + 1) * P, :].rearrange("h p e -> p h e")))
            sp.wait_ge(id_zero, 3)
            for g in range(4):
                rows = Wo1[4 * g * HD1:4 * (g + 1) * HD1, :].rearrange("(kv d) n -> d kv n", kv=KV1)
                for half in range(2):
                    r = 64 * half + 32 * (g % 2)
                    loads.append((wo1[r:r + HD1, g // 2:UNITS:2, :], rows))
            for j in range(2):
                loads.append((bv1c[32 * j:32 * j + HD1, :], bv1.rearrange("(kv d) -> d kv", kv=KV1)))
            assert len(loads) == NW + 2, len(loads)
            for dst, src in loads:
                sp.dma_start(dst, src, allow_slow_non_contiguous=True).then_inc(w_in, 16)

            with sp.Fori(0, B) as b:
                sp.wait_ge(base1, 1 + b)
                sp.dma_start(xs[:], x[bass.ds(b, 1)].rearrange("o (t p) d -> p (o t) d", p=P)).then_inc(x_in, 16)
                sp.dma_start(cs[:], ctx[bass.ds(b, 1)].rearrange("o (t p) d -> p (o t) d", p=P)).then_inc(c_in, 16)
                for c in range(DC):
                    g_landed(sp, b, "q1", c)
                    for part in range(2):
                        sp.dma_start(q_parts[part, c * P:(c + 1) * P, :], parts[:, c, part, :].bitcast(F32)).then_inc(parts_out, 16)
                g_landed(sp, b, "k1", 0)
                sp.dma_start(k_parts.rearrange("s r n -> r s n"), k1parts[:].bitcast(F32)).then_inc(kparts_out, 16)
                sp.wait_ge(kparts_out, 16 * (b + 1))
                for blk, part in enumerate((0, 0, 1, 1)):
                    sp.dma_start(k1st[blk * HD1:(blk + 1) * HD1, :, :].bitcast(F32),
                                 k_parts[part].rearrange("(h d) n -> d h n", d=HD1)).then_inc(k1_in, 16)
                sp.wait_ge(parts_out, 1 + 64 * (b + 1))
                for u in range(UNITS):
                    if u >= 2:
                        sp.wait_ge(s_ready, step_no(b, 0, NT * (u - 1)))
                    for blk, part in enumerate((0, 1, 0, 1)):
                        sp.dma_start(q1st[blk * HD1:(blk + 1) * HD1, u % 2, :, :].bitcast(F32),
                                     q_parts[part, 2 * u * HD1:2 * (u + 1) * HD1, :].rearrange("(h d) n -> d h n", d=HD1)
                                     ).then_inc(q1_in[u % 2], 16)

            sp.wait_ge(keys_out, 16 * B)
            g_landed(sp, B - 1, "down", 1)
            for half in range(2):
                sp.dma_start(keys[half * E:(half + 1) * E, :],
                             key_rows[:, half * (TOK // 2):(half + 1) * (TOK // 2)]).then_inc(k_in, 16)
            sp.wait_ge(pick, 32)
            for half in range(2):
                sp.dma_start(both[:, half * CAP:(half + 1) * CAP], found[half * E:(half + 1) * E, :]).then_inc(moved, 16)
            with sp.Fori(0, E // EU) as r:
                for s in range(EU):
                    sp.wait_ge(e_down[s], 1 + r)
                    sp.dma_start(wup[:, s, :, :], eup_w[bass.ds(r * EU + s, 1)].rearrange("o (c p) n -> p (o c) n", p=P)).then_inc(we_in[s], 16)
                    sp.dma_start(wdn[:, s, :], edown_w[bass.ds(r * EU + s, 1)].rearrange("o p n -> p (o n)")).then_inc(we_in[s], 16)
            for s in range(EU):
                sp.wait_ge(y_add[s], 16 * (E // EU))
            with sp.Fori(0, B) as b:
                sp.wait_ge(f_out, 1 + 16 * b)
                sp.dma_start(fin[:], sums[0][bass.ds(b * SEQ, SEQ), :].rearrange("(t p) n -> p t n", p=P)).then_inc(f_in, 16)
                sp.dma_start(fin1[:], sums[1][bass.ds(b * SEQ, SEQ), :].rearrange("(t p) n -> p t n", p=P)).then_inc(f_in, 16)
                sp.wait_ge(ln_done, NT * (2 * B + b + 1))
                sp.dma_start(out[bass.ds(b, 1)].rearrange("o (t p) d -> p (o t) d", p=P), fin[:]).then_inc(f_out, 16)
            sp.wait_ge(f_out, 1 + 16 * B)

        start_at_1 = [base1, *g_done, pt_ready, parts_out, batch_out, gated, keyv_done,
                      *e_down, turn_out, e_yo, f_out]

        @block.gpsimd
        def _(pool):
            for counted in start_at_1:
                pool.sem_inc(counted, 1)
            nc.gpsimd.memset(wo1[:], 0.0).then_inc(id_zero, 1)
            nc.gpsimd.memset(bv1c[:], 0.0).then_inc(id_zero, 1)
            nc.gpsimd.memset(ident[:], 0.0).then_inc(id_zero, 1)
            nc.gpsimd.memset(maskb[:], 0.0).then_inc(consts, 1)
            nc.gpsimd.memset(zero[:], 0.0).then_inc(consts, 1)
            nc.gpsimd.memset(minus_half[:], -0.5).then_inc(consts, 1)
            pool.wait_ge(consts, 3)
            nc.gpsimd.memset(k1st[:].bitcast(F32), 0.0).then_inc(consts, 1)
            nc.gpsimd.memset(q1st[:].bitcast(F32), 0.0).then_inc(consts, 1)
            nc.gpsimd.memset(k2z[:].bitcast(F32), 0.0).then_inc(consts, 1)
            nc.gpsimd.memset(v1s[:], 0.0).then_inc(consts, 1)
            nc.gpsimd.iota(token_key[:], pattern=[[-P, NT]], base=TOK, channel_multiplier=-1,
                           allow_small_or_imprecise_dtypes=True).then_inc(consts, 1)
            nc.gpsimd.iota(slot_no[:], pattern=[[0, 1]], base=0, channel_multiplier=1,
                           allow_small_or_imprecise_dtypes=True).then_inc(consts, 1)
            pool.wait_ge(id_zero, 3)
            nc.gpsimd.affine_select(out=ident[:], in_=ident[:], compare_op=ALU.not_equal, fill=1.0, base=0,
                                    pattern=[[-1, P]], channel_multiplier=1).then_inc(consts, 1)
            nc.gpsimd.affine_select(out=maskb[:], in_=maskb[:], compare_op=ALU.is_ge, fill=MASKED, base=0,
                                    pattern=[[-1, P]], channel_multiplier=1).then_inc(consts, 1)
            pool.wait_ge(consts, 11)
            nc.gpsimd.tensor_copy(identb[:], ident[:]).then_inc(consts, 1)
            for i in range(4):
                pool.dma_start(sums[1][i * 1024:(i + 1) * 1024, :].rearrange("(a p) n -> p a n", p=P),
                               zero[:, 0:D].rearrange("p (o n) -> p o n", o=1).to_broadcast([P, 8, D])).then_inc(zero_out, 16)
            for i in range(2):
                pool.dma_start(sums[i][TOK:NROW, :], zero[:, 0:D]).then_inc(zero_out, 16)
            pool.dma_start(table[TOK:NROW, :], zero[:]).then_inc(zero_out, 16)
            pool.wait_ge(w_in, 16 * (NW + 2))
            nc.gpsimd.tensor_scalar(wq1[:], wq1[:], HD1 ** -0.5, None, ALU.mult).then_inc(wprep, 1)
            nc.gpsimd.tensor_scalar(bq1c[:], bq1c[:], HD1 ** -0.5, None, ALU.mult).then_inc(wprep, 1)
            nc.gpsimd.tensor_scalar(wq2[:], wq2[:], HD2 ** -0.5, None, ALU.mult).then_inc(wprep, 1)
            nc.gpsimd.tensor_scalar(bqc[:], bqc[:], HD2 ** -0.5, None, ALU.mult).then_inc(wprep, 1)

            def normalise(b, phase, n):
                w = SEQ if phase == 0 else (n % NT + 1) * P
                pool.wait_ge(rr_ready, step_no(b, phase, n) + 1)
                alone(pool)
                for j in range(2):
                    i = nc.gpsimd.tensor_scalar(probs[:, n % 2, j, 0:w], probs[:, n % 2, j, 0:w],
                                                rrow[:, n % 4, j:j + 1], None, ALU.mult)
                i.then_inc(pn_ready, 1)

            def inverse_deviation(k):
                pool.wait_ge(ag_done, NT * (k + 1))
                alone(pool)
                nc.gpsimd.tensor_scalar(varps[:], mv[:, :, 1], EPS, None, ALU.add).then_inc(ve_done, 1)
                pool.wait_ge(ve_done, k + 1)
                nc.gpsimd.tensor_tensor(rstd[:], varps[:], minus_half[:], ALU.pow).then_inc(rs_done, 1)

            with pool.Fori(0, B) as b:
                for kind, n in order:
                    if kind == "ln1":
                        inverse_deviation(2 * b)
                    elif kind == "ln2":
                        inverse_deviation(2 * b + 1)
                    if kind == "k1":
                        pool.wait_ge(x_in, 16 * (b + 1))
                        nc.gpsimd.tensor_tensor(x1s[:], xs[:], bo1r[:].rearrange("p (o n) -> p o n", o=1).to_broadcast([P, NT, D]),
                                                ALU.add).then_inc(base1, 1)
                    elif kind == "R1":
                        normalise(b, 0, n)
                    elif kind == "R2":
                        normalise(b, 1, n)
                    elif kind == "ln1":
                        pool.wait_ge(ln_done, (2 * b + 1) * NT)
                        nc.gpsimd.tensor_tensor(x2s[:, :, 0:D], x1s[:], bo2r[:].rearrange("p (o n) -> p o n", o=1).to_broadcast([P, NT, D]),
                                                ALU.add).then_inc(base2, 1)
                    elif kind == "keys":
                        pool.wait_ge(keyv_done, 1 + b + 1)
                        pool.dma_start(table[bass.ds(b * SEQ, SEQ), :].rearrange("(t p) n -> p t n", p=P), x2s[:]).then_inc(table_out, 16)
                        g_landed(pool, b, "keys", 0)
                        pool.dma_start(key_rows[:, bass.ds(b * SEQ, SEQ)], keyT[:]).then_inc(keys_out, 16)
                    elif kind == "down" and n == 1:
                        pool.wait_ge(y0_done, 2 * (b + 1))
                        pool.dma_start(sums[0][bass.ds(b * SEQ, SEQ), :].rearrange("(t p) n -> p t n", p=P), y0s).then_inc(y0_out, 16)
                        for stored in (table_out, keys_out, y0_out):
                            pool.wait_ge(stored, 16 * (b + 1))
                        pool.sem_inc(batch_out, 1)

            pool.wait_ge(zero_out, 16 * 7)
            with pool.Fori(0, E // EU) as r:
                for s in range(EU):
                    pool.wait_ge(idx4_done, r + 1)
                    alone(pool)
                    pool.indirect_dma_start(out=xg[:, s, :], out_offset=None, in_=table,
                                            in_offset=bass.IndirectOffsetOnAxis(ap=idx4[:, 0, s:s + 1], axis=0)).then_inc(xg_in[s], 16)
                for s in range(EU):
                    pool.wait_ge(e_yo, 1 + r * EU + s + 1)
                    if s >= YS:
                        pool.wait_ge(y_add[s - YS], 16 * (r + 1))
                    alone(pool)
                    pool.indirect_dma_start(out=sums[s % YS], out_offset=bass.IndirectOffsetOnAxis(ap=idx4[:, 1, s:s + 1], axis=0),
                                            in_=yo[:, s, :], in_offset=None, compute_op=ALU.add).then_inc(y_add[s], 16)
                for s in range(EU):
                    pool.wait_ge(y_add[s], 16 * (r + 1))
                pool.sem_inc(turn_out, 1)
            with pool.Fori(0, B) as b:
                inverse_deviation(2 * B + b)

        @block.tensor
        def _(pe):
            pe.wait_ge(consts, 12)
            pe.wait_ge(wprep, 4)

            def bank(b, use, n, *results):
                g = g_index[use, n]
                need = {g % 2: g // 2}
                for r in results:
                    k = g_index[r]
                    need[k % 2] = max(need.get(k % 2, 0), k // 2 + 1)
                for k, count in sorted(need.items()):
                    pe.wait_ge(g_done[k], 1 + b * (NG // 2) + count)
                return G[:, g % 2, :]

            def transposed(b, use, c, src):
                dst = bank(b, use, c)
                for t in range(NT):
                    i = nc.tensor.transpose(dst[:, t * P:(t + 1) * P], src[:, t, c * P:(c + 1) * P], ident[:])
                i.then_inc(g_ready, 1)

            def product(dst, lhs, rhs):
                n = len(lhs)
                for i, (a, m) in enumerate(zip(lhs, rhs)):
                    last = nc.tensor.matmul(dst, a, m, start=(i == 0), stop=(i == n - 1))
                return last

            def transposes(b, phase, n):
                pe.wait_ge(pn_ready, step_no(b, phase, n) + 1)
                pe.wait_ge(pt_ready, 1 + step_no(b, phase, n))
                for j in range(2):
                    for kt in range(NT if phase == 0 else n % NT + 1):
                        i = nc.tensor.transpose(T[:, j, kt * P:(kt + 1) * P], probs[:, n % 2, j, kt * P:(kt + 1) * P], ident[:])
                i.then_inc(t_ready, 1)

            with pe.Fori(0, B) as b:
                for kind, n in order:
                    if kind == "xT":
                        pe.wait_ge(x_in, 16 * (b + 1))
                        transposed(b, "xT", n, xs)
                    elif kind == "cT":
                        pe.wait_ge(c_in, 16 * (b + 1))
                        transposed(b, "cT", n, cs)
                    elif kind == "q1":
                        product(bank(b, "q1", n, ("xT", 0), ("xT", 1)), [wq1[:, c, n * P:(n + 1) * P] for c in range(DC)],
                                [xT[:, c, :] for c in range(DC)]).then_inc(g_ready, 1)
                    elif kind == "k1":
                        product(bank(b, "k1", 0)[0:KV1 * HD1, :], [wk1[:, c, :] for c in range(DC)],
                                [xT[:, c, :] for c in range(DC)]).then_inc(g_ready, 1)
                    elif kind == "v1":
                        dst = bank(b, "v1", 0)
                        for t in range(NT):
                            i = product(dst[:, t * 64:(t + 1) * 64], [xT[:, c, t * P:(t + 1) * P] for c in range(DC)],
                                        [wv1[:, c, :] for c in range(DC)])
                        i.then_inc(g_ready, 1)
                    elif kind == "V2":
                        t, half = n // 2, n % 2
                        product(bank(b, "V2", n, ("cT", 0), ("cT", 1)), [cT[:, c, t * P:(t + 1) * P] for c in range(DC)],
                                [wv2[:, c, half * 512:(half + 1) * 512] for c in range(DC)]).then_inc(g_ready, 1)
                    elif kind == "S1":
                        u, qt = n // NT, n % NT
                        if n == 0:
                            pe.wait_ge(k1_in, 64 * (b + 1))
                        if qt == 0:
                            pe.wait_ge(q1_in[u % 2], 64 * (b * (UNITS // 2) + u // 2 + 1))
                        if n >= 2:
                            pe.wait_ge(p_ready, step_no(b, 0, n - 1))
                        for j in range(2):
                            i = nc.tensor.matmul(S[:, n % 2, j, :], q1st[:, u % 2, j, qt * P:(qt + 1) * P], k1st[:, u // 2, :],
                                                 start=True, stop=True)
                        i.then_inc(s_ready, 1)
                    elif kind == "T1":
                        transposes(b, 0, n)
                    elif kind == "PV1":
                        pe.wait_ge(pt_ready, 1 + step_no(b, 0, NT * n + NT))
                        dst = bank(b, "PV1", n, ("v1", 0))
                        for kk in range(NT // 2):
                            for half in range(2):
                                for j in range(2):
                                    r, kt = 64 * half + 32 * j, 2 * half + kk
                                    i = nc.tensor.matmul(dst[r:r + 32, :], v1s[:, kt, n // 2, :], pT[:, n % 2, j, kt, :],
                                                         start=(kk == 0), stop=(kk == 1), skip_group_check=True)
                        i.then_inc(g_ready, 1)
                    elif kind in ("o1", "o2"):
                        phase = 1 if kind == "o1" else 2
                        w = wo1 if phase == 1 else wo2
                        dst = bank(b, kind, n, *((f"PV{phase}", u) for u in range(UNITS)))
                        for t in range(2):
                            tt = 2 * n + t
                            i = product(dst[:, t * D:(t + 1) * D], [zT[:, u, tt * P:(tt + 1) * P] for u in range(UNITS)],
                                        [w[:, u, :] for u in range(UNITS)])
                        i.then_inc(g_ready, 1)
                    elif kind == "x1T":
                        pe.wait_ge(ln_done, (2 * b + 1) * NT)
                        transposed(b, "x1T", n, x1s)
                    elif kind == "P2":
                        product(bank(b, "q2", n, ("x1T", 0), ("x1T", 1)), [wq2[:, c, n * P:(n + 1) * P] for c in range(DC)],
                                [xT[:, c, :] for c in range(DC)]).then_inc(g_ready, 1)
                        product(bank(b, "k2", n), [wk2[:, c, n * P:(n + 1) * P] for c in range(DC)],
                                [cT[:, c, :] for c in range(DC)]).then_inc(g_ready, 1)
                    elif kind == "S2":
                        u, qt = n // NT, n % NT
                        w = (qt + 1) * P
                        if qt == 0:
                            g_landed(pe, b, "q2", u)
                            g_landed(pe, b, "k2", u)
                        if n >= 2:
                            pe.wait_ge(p_ready, step_no(b, 1, n - 1))
                        for j in range(2):
                            dst = S[:, n % 2, j, 0:w]
                            hi = parts[:, u % 2, 0, qt * P:(qt + 1) * P]
                            lo = parts[:, u % 2, 1, qt * P:(qt + 1) * P]
                            nc.tensor.matmul(dst, hi, k2z[:, u % 2, 0, j, 0:w], start=True, stop=False)
                            nc.tensor.matmul(dst, lo, k2z[:, u % 2, 0, j, 0:w], start=False, stop=False)
                            nc.tensor.matmul(S[:, n % 2, j, qt * P:w], identb[:], maskb[:], start=False, stop=False,
                                             skip_group_check=True)
                            i = nc.tensor.matmul(dst, hi, k2z[:, u % 2, 1, j, 0:w], start=False, stop=True)
                        i.then_inc(s_ready, 1)
                    elif kind == "T2":
                        transposes(b, 1, n)
                    elif kind == "PV2":
                        pe.wait_ge(pt_ready, 1 + step_no(b, 1, NT * n + NT))
                        dst = bank(b, "PV2", n, *(("V2", i) for i in range(2 * NT)))
                        for kt in range(NT):
                            for j in range(2):
                                h = 2 * n + j
                                i = nc.tensor.matmul(dst[64 * j:64 * j + 64, kt * P:SEQ], v2s[:, kt, h * HD2:(h + 1) * HD2],
                                                     pT[:, n % 2, j, kt, kt * P:SEQ], start=(kt == 0), stop=(kt == NT - 1),
                                                     skip_group_check=True)
                        i.then_inc(g_ready, 1)
                    elif kind == "x2T":
                        pe.wait_ge(ln_done, (2 * b + 2) * NT)
                        transposed(b, "x2T", n, x2s)
                    elif kind == "gate":
                        dst = bank(b, "gate", 0, ("x2T", 0), ("x2T", 1))
                        for t in range(NT):
                            i = product(dst[:, t * (E + 1):(t + 1) * (E + 1)], [xT[:, c, t * P:(t + 1) * P] for c in range(DC)],
                                        [gw[:, c, :] for c in range(DC)])
                        i.then_inc(g_ready, 1)
                    elif kind == "keys":
                        pe.wait_ge(keyv_done, 1 + b + 1)
                        dst = bank(b, "keys", 0)
                        alone(pe)
                        for t in range(NT):
                            i = nc.tensor.transpose(dst[0:E, t * P:(t + 1) * P], grest[:, t, :], ident[:])
                        i.then_inc(g_ready, 1)
                    elif kind == "up":
                        for use, off in (("sg", 0), ("su", FS)):
                            product(bank(b, use, n), [supw[:, c, off + n * P:off + (n + 1) * P] for c in range(DC)],
                                    [xT[:, c, :] for c in range(DC)]).then_inc(g_ready, 1)
                    elif kind == "down":
                        dst = bank(b, "down", n, *(("su", f) for f in range(FS // P)))
                        for t in range(2):
                            tt = 2 * n + t
                            i = product(dst[:, t * D:(t + 1) * D], [hid[:, f, tt * P:(tt + 1) * P] for f in range(FS // P)],
                                        [sdownw[:, f, :] for f in range(FS // P)])
                        i.then_inc(g_ready, 1)

            pe.wait_ge(pick, 64)
            nc.tensor.transpose(T[:, 0, 0:E], first, ident[0:E, 0:E]).then_inc(firstT, 1)
            with pe.Fori(0, E // EU) as r:
                for s in range(EU):
                    pe.wait_ge(e_yo, 1 + r * EU)
                    pe.wait_ge(xg_in[s], 16 * (r + 1))
                    for c in range(DC):
                        i = nc.tensor.transpose(S[:, s // 2, s % 2, c * P:(c + 1) * P], xg[:, s, c * P:(c + 1) * P], ident[:])
                    i.then_inc(e_tr, 1)
                for s in range(EU):
                    pe.wait_ge(e_trs, r * EU + s + 1)
                    pe.wait_ge(we_in[s], 32 * (r + 1))
                    for half in range(2):
                        i = product(S[:, s // 2, s % 2, 256 + half * P:256 + (half + 1) * P],
                                    [wup[:, s, c, half * FI:(half + 1) * FI] for c in range(DC)],
                                    [xgT[:, s, c * P:(c + 1) * P] for c in range(DC)])
                    i.then_inc(e_up, 1)
                for s in range(EU):
                    pe.wait_ge(e_act, r * EU + s + 1)
                    nc.tensor.matmul([T, G][s // 2][:, s % 2, 0:D], act[:, s, :], wdn[:, s, :], start=True, stop=True).then_inc(e_down[s], 1)

        @block.scalar
        def _(a):
            def evac(b, use, n, dst, bias=None):
                g_written(a, b, use, n)
                if bias is None:
                    nc.scalar.copy(dst, g_bank(use, n)).then_inc(g_sem(use, n), 1)
                else:
                    nc.scalar.activation(dst, g_bank(use, n), ACT.Identity, bias=bias).then_inc(g_sem(use, n), 1)

            def softmax(b, phase, n):
                w = SEQ if phase == 0 else (n % NT + 1) * P
                a.wait_ge(nm_ready, step_no(b, phase, n) + 1)
                if n >= 2:
                    a.wait_ge(t_ready, step_no(b, phase, n - 1))
                for j in range(2):
                    i = nc.scalar.activation(probs[:, n % 2, j, 0:w], S[:, n % 2, j, 0:w], ACT.Exp, bias=negmax[:, n % 4, j:j + 1],
                                             accum_out=rowsum[:, n % 4, j:j + 1])
                i.then_inc(p_ready, 1)

            a.wait_ge(consts, 12)
            a.wait_ge(wprep, 4)
            with a.Fori(0, B) as b:
                for kind, n in order:
                    if kind in ("xT", "x1T", "x2T"):
                        evac(b, kind, n, xT[:, n, :])
                    elif kind == "cT":
                        evac(b, kind, n, cT[:, n, :])
                    elif kind == "q1":
                        g_written(a, b, "q1", n)
                        a.wait_ge(parts_out, 1 + 64 * b)
                        nc.scalar.activation(parts[:, n, 0, :], g_bank("q1", n), ACT.Identity, bias=bq1c[:, n:n + 1]).then_inc(hi_done, 1)
                    elif kind == "k1":
                        g_written(a, b, "k1", 0)
                        nc.scalar.activation(k1parts[:, 0, :], g_bank("k1", 0)[0:64, :], ACT.Identity, bias=bk1c[:]).then_inc(hi_done, 1)
                    elif kind == "V2":
                        if n % 2 == 0:
                            if n == 6:
                                a.wait_ge(batch_out, 1 + b)
                            evac(b, "V2", n, v2s[:, n // 2, 0:512])
                    elif kind == "P2":
                        g_written(a, b, "q2", n)
                        nc.scalar.activation(parts[:, n % 2, 0, :], g_bank("q2", n), ACT.Identity, bias=bqc[:, n:n + 1]).then_inc(hi_done, 1)
                        g_written(a, b, "k2", n)
                        for j in range(2):
                            r = slice(64 * j, 64 * j + 64)
                            i = nc.scalar.activation(k2z[r, n % 2, 0, j, :], g_bank("k2", n)[r, :], ACT.Identity, bias=bkc[r, n:n + 1])
                        i.then_inc(hi_done, 1)
                    elif kind == "S1":
                        softmax(b, 0, n)
                    elif kind == "S2":
                        softmax(b, 1, n)
                    elif kind == "T1" and n % 2 == 1:
                        turn(a, nc.scalar.copy, b, 0, n)
                    elif kind == "T2" and n % 2 == 1:
                        turn(a, nc.scalar.copy, b, 1, n)
                    elif kind == "PV1":
                        evac(b, "PV1", n, zT[:, n, :], bv1c[:, n // 2:n // 2 + 1])
                    elif kind == "PV2":
                        evac(b, "PV2", n, zT[:, n, :], bvc[:, n:n + 1])
                    elif kind == "gate":
                        a.wait_ge(gmax_done, b + 1)
                        for t in range(NT):
                            nc.scalar.activation(gexp[:, t, :], g_bank("gate", 0)[:, t * (E + 1):t * (E + 1) + E], ACT.Exp,
                                                 bias=gneg[:, t:t + 1], accum_out=gsum[:, t:t + 1])
                        nc.scalar.activation(gtmp[:, :, 0], g_bank("gate", 0)[:, 0:NT * (E + 1)].rearrange("p (t e) -> p t e", t=NT)[:, :, E],
                                             ACT.Tanh, scale=0.5).then_inc(g_sem("gate", 0), 1)
                    elif kind == "keys":
                        g_written(a, b, "keys", 0)
                        a.wait_ge(batch_out, 1 + b)
                        nc.scalar.copy(keyT[:], g_bank("keys", 0)[0:E, :]).then_inc(g_sem("keys", 0), 1)
                    elif kind == "up":
                        g_written(a, b, "sg", n)
                        a.wait_ge(gated, 1 + b * (FS // P) + n)
                        nc.scalar.activation(tnh, g_bank("sg", n), ACT.Tanh, scale=0.5).then_inc(tanh_done, 1)
            with a.Fori(0, E // EU) as r:
                for s in range(EU):
                    a.wait_ge(e_tr, r * EU + s + 1)
                    nc.scalar.copy(xgT[:, s, :], S[:, s // 2, s % 2, 0:D]).then_inc(e_trs, 1)
                for s in range(EU):
                    a.wait_ge(e_up, r * EU + s + 1)
                    nc.scalar.activation(ath[:, s, :], S[:, s // 2, s % 2, 256:256 + FI], ACT.Tanh, scale=0.5).then_inc(e_tanh, 1)

        @block.vector
        def _(v):
            def low_part(b, use, n, dst, src, bias, hi, count):
                v.wait_ge(hi_done, count)
                return nc.vector.scalar_tensor_tensor(out=dst, in0=src, scalar=bias, in1=hi.bitcast(F32), op0=ALU.add, op1=ALU.subtract)

            HI = DC + 1 + 2 * UNITS

            def maxima(b, phase, n):
                w = SEQ if phase == 0 else (n % NT + 1) * P
                v.wait_ge(s_ready, step_no(b, phase, n) + 1)
                nc.vector.tensor_reduce(negmax[:, n % 4, :], S[:, n % 2, :, 0:w], AX_X, ALU.max, negate=True).then_inc(nm_ready, 1)

            def recip(b, phase, n):
                v.wait_ge(p_ready, step_no(b, phase, n) + 1)
                nc.vector.reciprocal(rrow[:, n % 4, :], rowsum[:, n % 4, :]).then_inc(rr_ready, 1)

            def layernorm(k, tile):
                v.wait_ge(res_done, 2 * (k + 1))
                for t in range(NT):
                    nc.vector.bn_stats(stats[:, t, :], tile[:, t, 0:D]).then_inc(st_done, 1)
                v.wait_ge(st_done, NT * (k + 1))
                alone(v)
                for t in range(NT):
                    nc.vector.bn_aggr(mv[:, t, :], stats[:, t, :]).then_inc(ag_done, 1)
                v.wait_ge(rs_done, k + 1)
                for t in range(NT):
                    nc.vector.tensor_scalar(tile[:, t, 0:D], tile[:, t, 0:D], mv[:, t, 0:1], rstd[:, t:t + 1],
                                            ALU.subtract, ALU.mult).then_inc(ln_done, 1)

            v.wait_ge(consts, 12)
            v.wait_ge(wprep, 4)
            with v.Fori(0, B) as b:
                for kind, n in order:
                    if kind == "q1":
                        low_part(b, "q1", n, parts[:, n, 1, :], g_bank("q1", n), bq1c[:, n:n + 1], parts[:, n, 0, :],
                                 b * HI + n + 1).then_inc(g_sem("q1", n), 1)
                    elif kind == "k1":
                        low_part(b, "k1", 0, k1parts[:, 1, :], g_bank("k1", 0)[0:64, :], bk1c[:], k1parts[:, 0, :],
                                 b * HI + DC + 1).then_inc(g_sem("k1", 0), 1)
                    elif kind == "v1":
                        g_written(v, b, "v1", 0)
                        nc.vector.tensor_copy(v1s[:, :, :, 0:HD1], g_bank("v1", 0)[:, 0:NT * 64].rearrange("p (t h d) -> p t h d", t=NT, h=KV1)
                                              ).then_inc(g_sem("v1", 0), 1)
                    elif kind == "V2":
                        if n % 2 == 1:
                            if n == 7:
                                v.wait_ge(batch_out, 1 + b)
                            g_written(v, b, "V2", n)
                            nc.vector.tensor_copy(v2s[:, n // 2, 512:1024], g_bank("V2", n)).then_inc(g_sem("V2", n), 1)
                    elif kind == "P2":
                        at = b * HI + DC + 1 + 2 * n
                        low_part(b, "q2", n, parts[:, n % 2, 1, :], g_bank("q2", n), bqc[:, n:n + 1], parts[:, n % 2, 0, :],
                                 at + 1).then_inc(g_sem("q2", n), 1)
                        for j in range(2):
                            r = slice(64 * j, 64 * j + 64)
                            i = low_part(b, "k2", n, k2z[r, n % 2, 1, j, :], g_bank("k2", n)[r, :], bkc[r, n:n + 1],
                                         k2z[r, n % 2, 0, j, :], at + 2)
                        i.then_inc(g_sem("k2", n), 1)
                    elif kind == "S1":
                        maxima(b, 0, n)
                    elif kind == "S2":
                        maxima(b, 1, n)
                    elif kind == "R1":
                        recip(b, 0, n)
                    elif kind == "R2":
                        recip(b, 1, n)
                    elif kind == "T1" and n % 2 == 0:
                        turn(v, nc.vector.tensor_copy, b, 0, n)
                    elif kind == "T2" and n % 2 == 0:
                        turn(v, nc.vector.tensor_copy, b, 1, n)
                    elif kind in ("o1", "o2"):
                        tile = x1s if kind == "o1" else x2s
                        if n == 0:
                            v.wait_ge(*((base1, 1 + b + 1) if kind == "o1" else (base2, b + 1)))
                        g_written(v, b, kind, n)
                        dst = tile[:, 2 * n:2 * n + 2, 0:D]
                        nc.vector.tensor_tensor(dst, g_bank(kind, n).rearrange("p (t n) -> p t n", t=2), dst, ALU.add).then_inc(res_done, 1)
                        v.wait_ge(res_done, 4 * b + (0 if kind == "o1" else 2) + n + 1)
                        v.sem_inc(g_sem(kind, n), 1)
                    elif kind == "ln1":
                        layernorm(2 * b, x1s)
                    elif kind == "ln2":
                        layernorm(2 * b + 1, x2s)
                    elif kind == "gate":
                        g_written(v, b, "gate", 0)
                        logits = g_bank("gate", 0)[:, 0:NT * (E + 1)].rearrange("p (t e) -> p t e", t=NT)[:, :, 0:E]
                        nc.vector.tensor_reduce(gneg[:], logits, AX_X, ALU.max, negate=True).then_inc(gmax_done, 1)
                        g_landed(v, b, "gate", 0)
                        v.wait_ge(keyv_done, 1 + b)
                        GS = 10
                        at = [0]

                        def link(i):
                            at[0] += 1
                            i.then_inc(gate_step, 1)
                            v.wait_ge(gate_step, b * GS + at[0])
                            alone(v)

                        def wide(t):
                            return t.rearrange("p (t o) -> p t o", o=1).to_broadcast([P, NT, E])

                        link(nc.vector.tensor_scalar(sig[:], gtmp[:, :, 0], 1.0, 0.5, ALU.add, ALU.mult))
                        link(nc.vector.reciprocal(gtmp[:, :, 1], gsum[:]))
                        link(nc.vector.tensor_tensor(gprob[:], gexp[:], wide(gtmp[:, :, 1]), ALU.mult))
                        for t in range(NT):
                            i = nc.vector.max(top8[:, t, :], gprob[:, t, :])
                        link(i)
                        for t in range(NT):
                            i = nc.vector.match_replace(grest[:, t, :], top8[:, t, :], gprob[:, t, :], -1.0)
                        link(i)
                        link(nc.vector.reduce_sum(gtmp[:, :, 2], top8[:], AX_X))
                        link(nc.vector.reciprocal(gtmp[:, :, 3], gtmp[:, :, 2]))
                        link(nc.vector.tensor_tensor(gprob[:], gprob[:], wide(gtmp[:, :, 3]), ALU.mult))
                        link(nc.vector.scalar_tensor_tensor(out=x2s[:, :, D:ROW], in0=grest[:], scalar=0.0, in1=gprob[:],
                                                            op0=ALU.is_lt, op1=ALU.mult))
                        for t in range(NT):
                            i = nc.vector.tensor_scalar(grest[:, t, :], grest[:, t, :], 0.0, token_key[:, t:t + 1], ALU.is_lt, ALU.mult)
                        link(i)
                        nc.vector.tensor_scalar(token_key[:], token_key[:], -float(SEQ), None, ALU.add).then_inc(keyv_done, 1)
                        assert at[0] == GS, at
                    elif kind == "up":
                        v.wait_ge(tanh_done, b * (FS // P) + n + 1)
                        nc.vector.scalar_tensor_tensor(out=hid[:, n, :], in0=tnh, scalar=1.0, in1=g_bank("sg", n), op0=ALU.add,
                                                       op1=ALU.mult).then_inc(gated, 1)
                        v.wait_ge(gated, 1 + b * (FS // P) + n + 1)
                        v.sem_inc(g_sem("sg", n), 1)
                        g_written(v, b, "su", n)
                        nc.vector.scalar_tensor_tensor(out=hid[:, n, :], in0=hid[:, n, :], scalar=0.5, in1=g_bank("su", n), op0=ALU.mult,
                                                       op1=ALU.mult).then_inc(g_sem("su", n), 1)
                    elif kind == "down":
                        if n == 0:
                            v.wait_ge(batch_out, 1 + b)
                        g_written(v, b, "down", n)
                        for t in range(2):
                            tt = 2 * n + t
                            i = nc.vector.scalar_tensor_tensor(out=y0s[:, tt, :], in0=g_bank("down", n)[:, t * D:(t + 1) * D],
                                                               scalar=sig[:, tt:tt + 1], in1=x2s[:, tt, 0:D], op0=ALU.mult, op1=ALU.add)
                        i.then_inc(y0_done, 1)
                        v.wait_ge(y0_done, 2 * b + n + 1)
                        v.sem_inc(g_sem("down", n), 1)

            def largest(src, dst, at):
                for r in range(CAP // 8):
                    nc.vector.max(dst[:, 8 * r:8 * r + 8], src).then_inc(pick, 1)
                    v.wait_ge(pick, at + 2 * r + 1)
                    nc.vector.match_replace(src, dst[:, 8 * r:8 * r + 8], src, 0.0).then_inc(pick, 1)
                    v.wait_ge(pick, at + 2 * r + 2)

            v.wait_ge(k_in, 32)
            largest(keys, found, 0)
            v.wait_ge(moved, 32)
            largest(both, first, 32)
            v.wait_ge(firstT, 1)
            nc.vector.tensor_scalar(idxf[:, 0, :], T[:, 0, 0:E], 0.0, slot_no[:], ALU.is_equal, ALU.mult).then_inc(idx_step, 1)
            nc.vector.tensor_scalar(idxf[:, 1, :], T[:, 0, 0:E], -1.0, float(TOK), ALU.mult, ALU.add).then_inc(idx_step, 1)
            v.wait_ge(idx_step, 2)
            nc.vector.tensor_tensor(idx[:], idxf[:, 0, :], idxf[:, 1, :], ALU.add).then_inc(idx_step, 1)
            v.wait_ge(idx_step, 3)
            with v.Fori(0, E // EU) as r:
                v.wait_ge(turn_out, 1 + r)
                nc.vector.tensor_copy(idx4[:, 0, :], idx[:, bass.ds(r * EU, EU)])
                nc.vector.tensor_copy(idx4[:, 1, :], idx[:, bass.ds(r * EU, EU)]).then_inc(idx4_done, 1)
                for s in range(EU):
                    v.wait_ge(e_tanh, r * EU + s + 1)
                    nc.vector.scalar_tensor_tensor(out=act[:, s, :], in0=ath[:, s, :], scalar=1.0,
                                                   in1=S[:, s // 2, s % 2, 256:256 + FI], op0=ALU.add, op1=ALU.mult).then_inc(e_act1, 1)
                    v.wait_ge(e_act1, r * EU + s + 1)
                    nc.vector.scalar_tensor_tensor(out=act[:, s, :], in0=act[:, s, :], scalar=0.5,
                                                   in1=S[:, s // 2, s % 2, 256 + FI:256 + 2 * FI], op0=ALU.mult, op1=ALU.mult).then_inc(e_act, 1)
                for s in range(EU):
                    v.wait_ge(e_down[s], 1 + r + 1)
                    nc.vector.tensor_scalar(yo[:, s, :], [T, G][s // 2][:, s % 2, 0:D], xg[:, s, bass.ds(r * EU + s + D, 1)], None,
                                            ALU.mult).then_inc(e_yo, 1)
            with v.Fori(0, B) as b:
                v.wait_ge(f_in, 32 * (b + 1))
                for t in range(2):
                    nc.vector.tensor_tensor(fin[:, 2 * t:2 * t + 2, :], fin[:, 2 * t:2 * t + 2, :], fin1[:, 2 * t:2 * t + 2, :],
                                            ALU.add).then_inc(res_done, 1)
                layernorm(2 * B + b, fin)


_INS = ["x", "ctx_1024", "L0_attn_Wq", "L0_attn_bq", "L0_attn_Wk", "L0_attn_bk", "L0_attn_Wv", "L0_attn_bv",
        "L0_attn_Wo", "L0_attn_bo", "L0_xattn_W_Q", "L0_xattn_W_K", "L0_xattn_W_V", "L0_xattn_W_O",
        "L0_xattn_b_Q", "L0_xattn_b_K", "L0_xattn_b_V", "L0_xattn_b_O", "L0_ffn_gate_w", "L0_ffn_shared_gate_w",
        "L0_ffn_shared_gate_up_w", "L0_ffn_shared_down_w", "L0_ffn_expert_gate_up_w", "L0_ffn_expert_down_w"]


def kernel(**inputs):
    import numpy as _np
    import concourse.bacc as _bacc
    from concourse import mybir as _mybir
    from concourse.bass_utils import run_bass_kernel_spmd as _run

    nc = _bacc.Bacc("TRN2", target_bir_lowering=False, num_devices=1)
    arrays, args = {}, []
    for name in _INS:
        a = _np.ascontiguousarray(inputs[name])
        arrays[f"in_{name}_dram"] = a
        args.append(nc.dram_tensor(f"in_{name}_dram", a.shape, _mybir.dt.from_np(a.dtype), kind="ExternalInput").ap())
    out = nc.dram_tensor("out_0_dram", (B, SEQ, D), F32, kind="ExternalOutput").ap()
    build(nc, *args, out)
    r = _run(nc, [arrays], core_ids=[0])
    return r.results[0]["out_0_dram"]
```

```python
from contextlib import ExitStack

import concourse.bass as bass
from concourse import mybir

F32 = mybir.dt.float32
F32R = mybir.dt.float32r
BF16 = mybir.dt.bfloat16
U32 = mybir.dt.uint32
ALU = mybir.AluOpType
ACT = mybir.ActivationFunctionType
AX_X = mybir.AxisListType.X

P = 128
B, SEQ, D = 8, 512, 256
TOK = B * SEQ
NT = SEQ // P
DC = D // P
H = 16
UNITS = H // 2
HD1, KV1 = 16, 4
HD2 = 64
STEPS = UNITS * NT
E, TOPK, CAP = 64, 8, 128
FS = 512
FI = 128
ROW = D + E
NROW = TOK + CAP
EPS = 1e-5
MASKED = -1e30
YS = 2
EU = 8
AHEAD = 12
PU = 4
TURNS = E // EU


def self_attention_timeline():
    pairs = [(g, i) for g in range(KV1) for i in range(2 * NT)]
    order, later = [], []
    for m in range(AHEAD):
        order.append(("M", pairs[m]))
        if m % 3 == 0:
            order.append(("V2", 1 + m // 3))
        if m == 2 * NT:
            order.append(("NT", 0))
    for x, (g, i) in enumerate(pairs):
        if x + AHEAD < len(pairs):
            order.append(("M", pairs[x + AHEAD]))
            if pairs[x + AHEAD][1] == 2 * NT - 1:
                later.append((x + 2, ("NT", pairs[x + AHEAD][0])))
        order.append(("X", (g, i)))
        for due in [d for d in later if d[0] <= x]:
            order.append(due[1])
            later.remove(due)
        if i % 2 == 1:
            later.append((x + 1, ("PV1", (g, i // 2))))
        if i == 2 * NT - 1:
            later += [(x + 2, ("E1", g)), (x + 3, ("SM", g)), (x + 5, ("RS", g))]
    order += [("PV1", (KV1 - 1, NT - 1)), ("E1", KV1 - 1), ("V2", 5), ("SM", KV1 - 1), ("V2", 6), ("RS", KV1 - 1)]
    return order


def cross_attention_timeline(engine):
    order = [("Q2", 0)]
    for n in range(STEPS + 3):
        score = [("S2", n)] if n < STEPS else []
        transposes = [("T2", n - 2)] if 0 <= n - 2 < STEPS else []
        division = [("R2", n - 1)] if 0 <= n - 1 < STEPS else []
        order += transposes + score if engine == "scalar" else score + division + transposes
        if n < STEPS and n // NT + 1 < UNITS:
            if n % NT == 1:
                order.append(("K2", n // NT + 1))
            if n % NT == 2:
                order.append(("Q2", n // NT + 1))
        if n < STEPS and n % 2 == 0:
            order.append(("pick", n // 2))
        if n >= 3 and (n - 3) % NT == NT - 1:
            order.append(("PV2", (n - 3) // NT))
    return order


def batch_timeline(engine):
    t = [("xT", c) for c in range(DC)] + [("q1", c) for c in range(DC)] + [("k1", 0), ("v1", 0)]
    t += [("cT", c) for c in range(DC)] + [("V2", 0)]
    t += self_attention_timeline()
    t += [("o1", i) for i in range(2)] + [("V2", 7), ("K2", 0), ("ln1", 0)] + [("x1T", c) for c in range(DC)]
    t += cross_attention_timeline(engine)
    t += [("o2", i) for i in range(2)] + [("ln2", 0)] + [("x2T", c) for c in range(DC)]
    t += [("gate", 0), ("up", 0), ("up", 1), ("keys", 0), ("up", 2), ("up", 3)] + [("down", i) for i in range(2)]
    return t


USES = {"xT": ["xT"], "q1": ["q1"], "k1": ["k1"], "v1": ["v1"], "cT": ["cT"], "V2": ["V2"], "NT": ["nt"],
        "SM": ["sm"], "RS": ["rs"],
        "o1": ["o1"], "x1T": ["x1T"], "Q2": ["q2"], "K2": ["k2"], "PV2": ["PV2"], "o2": ["o2"], "x2T": ["x2T"],
        "gate": ["gate"], "keys": ["keys"], "down": ["down"]}


def build(nc, x, ctx, Wq1, bq1, Wk1, bk1, Wv1, bv1, Wo1, bo1, WQ, WK, WV, WO, bQ, bK, bV, bO,
          gate_w, sgate_w, sup_w, sdown_w, eup_w, edown_w, out):
    order = batch_timeline("tensor")
    g_index = {}
    for kind, n in order:
        for use in USES.get(kind, []):
            g_index[use, n] = len(g_index)
    NG = len(g_index)
    assert NG % 2 == 0
    s_index = {}
    for kind, n in order:
        if kind in ("M", "X", "S2", "up"):
            s_index[kind, n] = len(s_index)
    NS = len(s_index)
    assert NS % 2 == 0

    with ExitStack() as stack:
        def sb(name, shape, dt=F32):
            return stack.enter_context(nc.sbuf_tensor(name, shape, dt))

        def psum(name, shape, dt=F32):
            return stack.enter_context(nc.psum_tensor(name, shape, dt))

        def sem(name):
            return stack.enter_context(nc.semaphore(name))

        q_parts = nc.dram_tensor("q_parts", (2, H * HD1, SEQ), F32).ap()
        k_parts = nc.dram_tensor("k_parts", (2, KV1 * HD1, SEQ), F32).ap()
        table = nc.dram_tensor("token_table", (NROW, ROW), F32).ap()
        sums = [nc.dram_tensor(f"sum_{i}", (NROW, D), F32).ap() for i in range(YS)]

        S = psum("S", [P, 2, 2, 512])
        T = psum("T", [P, 2, 512])
        G = psum("G", [P, 2, 512])

        ident = sb("ident", [P, P])
        identb = sb("identb", [P, P], BF16)
        maskb = sb("maskb", [P, P], BF16)
        wq1 = sb("wq1", [P, DC, H * HD1])
        wk1 = sb("wk1", [P, DC, KV1 * HD1])
        wv1 = sb("wv1", [P, DC, KV1 * HD1])
        wo1 = sb("wo1", [P, KV1, D])
        wq2 = sb("wq2", [P, DC, H * HD2])
        wk2 = sb("wk2", [P, DC, H * HD2])
        wv2 = sb("wv2", [P, DC, H * HD2])
        wo2 = sb("wo2", [P, UNITS, D])
        gw = sb("gw", [P, DC, E + 1])
        supw = sb("supw", [P, DC, 2 * FS])
        sdownw = sb("sdownw", [P, FS // P, D])
        bq1c = sb("bq1c", [P, DC])
        bk1c = sb("bk1c", [KV1 * HD1, 1])
        bv1r = sb("bv1r", [P, KV1 * HD1])
        bqc = sb("bqc", [P, UNITS])
        bkc = sb("bkc", [P, UNITS])
        bvc = sb("bvc", [P, UNITS])
        bo1r = sb("bo1r", [P, D])
        bo2r = sb("bo2r", [P, D])
        token_key = sb("token_key", [P, NT])
        slot_no = sb("slot_no", [P, 1])
        sum_rows = sb("sum_rows", [P, 4])

        xs = sb("xs", [P, NT, D])
        cs = sb("cs", [P, NT, D])
        xT = sb("xT", [P, DC, SEQ])
        cT = sb("cT", [P, DC, SEQ])
        x1s = sb("x1s", [P, NT, D])
        x2s = sb("x2s", [P, NT, ROW])
        parts = sb("parts", [P, 2, 2, SEQ], F32R)
        k1parts = sb("k1parts", [KV1 * HD1, 2, SEQ], F32R)
        q1st = sb("q1st", [P, 4, SEQ], F32R)
        k1st = sb("k1st", [P, KV1, SEQ], F32R)
        k2z = sb("k2z", [P, 2, 2, 2, SEQ], F32R)
        q_slots = [q1st[:, :, :], parts[:, :, :, :].rearrange("p a b n -> p (a b) n"),
                   k2z[:, 0, :, :, :].rearrange("p a b n -> p (a b) n")]
        KQ = 4 * HD1 + 1
        v1s = sb("v1s", [P, NT, KV1, 32])
        v2s = sb("v2s", [P, NT, H * HD2])
        negmax1 = sb("negmax1", [P, 2, 4, NT])
        negrow = sb("negrow", [4 * NT, P], F32R)
        rsum1 = sb("rsum1", [P, 4 * NT])
        probs = sb("probs", [P, 2, 2, SEQ])
        rwide = probs[:, 0, 0, :]
        pT = sb("pT", [P, 2, 2, NT, SEQ])
        p1 = pT[:, :, :, :, :].rearrange("p a b k n -> p (a b k) n").rearrange("p (k h) n -> p k h n", k=NT)
        zT = sb("zT", [P, UNITS, SEQ])
        stats = sb("stats", [P, NT, 6])
        mv = sb("mv", [P, NT, 2])
        varps = sb("varps", [P, NT])
        minus_half = sb("minus_half", [P, NT])
        rstd = sb("rstd", [P, NT])
        negmax = sb("negmax", [P, 4, 2])
        rowsum = sb("rowsum", [P, 4, 2])
        rrow = sb("rrow", [P, 4, 2])
        gneg = sb("gneg", [P, NT])
        gsum = sb("gsum", [P, NT])
        gexp = probs[:, 0, 0, 0:NT * E].rearrange("p (t e) -> p t e", t=NT)
        gprob = probs[:, 0, 1, 0:NT * E].rearrange("p (t e) -> p t e", t=NT)
        grest = probs[:, 1, 0, 0:NT * E].rearrange("p (t e) -> p t e", t=NT)
        keyv = probs[:, 1, 1, 0:NT * E].rearrange("p (t h e) -> p t h e", t=2, h=2)
        top8 = sb("top8", [P, NT, TOPK])
        gtmp = sb("gtmp", [P, NT, 4])
        sig = sb("sig", [P, NT])
        keys = sb("keys", [P, CAP + SEQ // 2])
        found = sb("found", [P, CAP])
        hid = v2s[:, 0:2, :].rearrange("p a (b n) -> p (a b) n", b=2)
        tnh = v2s[:, 2, :].rearrange("p (s n) -> p s n", s=2)
        y0s = v2s[:, 3, :].rearrange("p (t n) -> p t n", t=NT)

        both = pT[0:E, 0, 1, 1, 0:2 * CAP]
        first = pT[0:E, 0, 1, 2, 0:CAP]
        idxf = pT[:, 0, 1, 3, 0:2 * E].rearrange("p (a e) -> p a e", a=2)
        idx = sb("idx", [P, E], U32)
        idx_gather = sb("idx_gather", [P, EU], U32)
        idx_add = sb("idx_add", [P, EU], U32)
        xg = v2s[:, :, :].rearrange("p a n -> p (a n)")[:, 0:EU * ROW].rearrange("p (s n) -> p s n", s=EU)
        wup = zT[:, :, :].rearrange("p u n -> p (u n)").rearrange("p (s c n) -> p s c n", s=EU, c=DC)
        wdn = pT[:, 1, 0, :, :].rearrange("p a (b n) -> p (a b) n", b=2)
        xgT = pT[:, 1, 1, 0:2, :].rearrange("p a (s n) -> p (a s) n", s=2)
        act = pT[:, 1, 1, 2, :].rearrange("p (s n) -> p s n", s=PU)
        ath = probs[:, 0, 0, :].rearrange("p (s n) -> p s n", s=PU)
        yo = xT[:, :, :].rearrange("p c (b n) -> p (c b) n", b=2)
        fin = [xs[:], x1s[:]]
        fin1 = [cs[:], x2s[:, :, 0:D]]
        zero = sb("zero", [P, SEQ])
        zero_row = zero[0:1, :].rearrange("p (o n) -> p o n", o=1).to_broadcast([1, 4, SEQ])

        w_in = sem("w_in")
        passed = sem("passed")
        x_in = sem("x_in")
        c_in = sem("c_in")
        consts = sem("consts")
        id_zero = sem("id_zero")
        ones_done = sem("ones_done")
        wprep = sem("wprep")
        g_ready = sem("g_ready")
        g_done = [sem("g_done0"), sem("g_done1")]
        hi_done = sem("hi_done")
        base1 = sem("base1")
        base2 = sem("base2")
        parts_out = sem("parts_out")
        kparts_out = sem("kparts_out")
        k1_in = sem("k1_in")
        q1_in = [sem(f"q1_in{i}") for i in range(3)]
        nm_in = [sem(f"nm_in{i}") for i in range(3)]
        zero_in = sem("zero_in")
        z_copied = sem("z_copied")
        rsum1_done = sem("rsum1_done")
        z_divided = sem("z_divided")
        z_ready = sem("z_ready")
        s_ready = sem("s_ready")
        s_done = [sem("s_done0"), sem("s_done1")]
        nm_ready = sem("nm_ready")
        rr_ready = sem("rr_ready")
        pn_ready = sem("pn_ready")
        t_ready = sem("t_ready")
        pt_ready = sem("pt_ready")
        res_done = sem("res_done")
        st_done = sem("st_done")
        ag_done = sem("ag_done")
        ve_done = sem("ve_done")
        rs_done = sem("rs_done")
        ln_done = sem("ln_done")
        gmax_done = sem("gmax_done")
        gexp_done = sem("gexp_done")
        gate_step = sem("gate_step")
        keyv_done = sem("keyv_done")
        tanh_done = sem("tanh_done")
        gated = sem("gated")
        table_out = sem("table_out")
        keys_in = sem("keys_in")
        y0_done = sem("y0_done")
        y0_out = sem("y0_out")
        batch_out = sem("batch_out")
        zero_out = sem("zero_out")
        pick = sem("pick")
        kept = sem("kept")
        moved = sem("moved")
        first_done = sem("first_done")
        firstT = sem("firstT")
        idx_step = sem("idx_step")
        idx0_done = sem("idx0_done")
        xg_in = [sem(f"xg_in{i}") for i in range(EU)]
        we_in = [sem(f"we_in{i}") for i in range(EU)]
        e_tr = sem("e_tr")
        e_trs = sem("e_trs")
        e_up = sem("e_up")
        e_tanh = sem("e_tanh")
        e_act1 = sem("e_act1")
        e_act = sem("e_act")
        e_down = sem("e_down")
        e_yo = sem("e_yo")
        y_add = [sem(f"y_add{i}") for i in range(EU)]
        f_in = [sem(f"f_in{i}") for i in range(2)]
        f_out = [sem(f"f_out{i}") for i in range(2)]

        NW = 26

        def g_written(eng, b, use, n):
            eng.wait_ge(g_ready, b * NG + g_index[use, n] + 1)

        def g_landed(eng, b, use, n):
            g = g_index[use, n]
            eng.wait_ge(g_done[g % 2], 1 + b * (NG // 2) + g // 2 + 1)

        def g_bank(use, n):
            return G[:, g_index[use, n] % 2, :]

        def g_sem(use, n):
            return g_done[g_index[use, n] % 2]

        def s_written(eng, b, kind, n):
            eng.wait_ge(s_ready, b * NS + s_index[kind, n] + 1)

        def s_landed(eng, b, *steps):
            need = {}
            for step in steps:
                k = s_index[step]
                need[k % 2] = max(need.get(k % 2, 0), k // 2 + 1)
            for k, count in sorted(need.items()):
                eng.wait_ge(s_done[k], 1 + b * (NS // 2) + count)

        def s_slot(kind, n):
            return S[:, s_index[kind, n] % 2, :, :]

        def s_sem(kind, n):
            return s_done[s_index[kind, n] % 2]

        def alone(eng):
            eng.sem_inc(passed, 1)

        def out_of(s):
            return [T, G][s % PU // 2][:, s % 2, :]

        ROUND_STEPS = 2 * CAP // 8

        def step_no(b, n):
            return b * STEPS + n

        def turn(eng, copy, b, n):
            u, qt = n // NT, n % NT
            nk = qt + 1
            eng.wait_ge(t_ready, step_no(b, n) + 1)
            if u >= 2:
                g_written(eng, b, "PV2", u - 2)
            copy(pT[:, u % 2, :, 0:nk, qt * P:(qt + 1) * P],
                 T[:, :, 0:nk * P].rearrange("p j (k n) -> p j k n", k=nk)).then_inc(pt_ready, 1)

        block = stack.enter_context(nc.Block())

        @block.sync
        def _(sp):
            loads = [
                (wq1[:], Wq1.rearrange("(c p) n -> p c n", p=P)),
                (wk1[:], Wk1.rearrange("(c p) n -> p c n", p=P)),
                (wv1[:], Wv1.rearrange("(c p) n -> p c n", p=P)),
                (bq1c[:], bq1.rearrange("(c p) -> p c", p=P)),
                (bv1r[:], bv1.rearrange("(o n) -> o n", o=1).to_broadcast([P, KV1 * HD1])),
                (bk1c[:], bk1.rearrange("(p o) -> p o", o=1)),
                (bo1r[:], bo1.rearrange("(o n) -> o n", o=1).to_broadcast([P, D])),
                (bo2r[:], bO.rearrange("(o n) -> o n", o=1).to_broadcast([P, D])),
                (bqc[:], bQ.rearrange("(u j) e -> (j e) u", j=2)),
                (bkc[:], bK.rearrange("(u j) e -> (j e) u", j=2)),
                (bvc[:], bV.rearrange("(u j) e -> (j e) u", j=2)),
                (wo2[:], WO.rearrange("(u j) e d -> (j e) u d", j=2)),
                (gw[:, :, 0:E], gate_w.rearrange("(c p) n -> p c n", p=P)),
                (gw[:, :, E:E + 1], sgate_w.rearrange("(c p) n -> p c n", p=P)),
                (supw[:], sup_w.rearrange("(c p) n -> p c n", p=P)),
                (sdownw[:], sdown_w.rearrange("(c p) n -> p c n", p=P)),
            ]
            for w, src in ((wq2, WQ), (wk2, WK), (wv2, WV)):
                for c in range(DC):
                    loads.append((w[:, c, :].rearrange("p (h e) -> p h e", h=H),
                                  src[:, c * P:(c + 1) * P, :].rearrange("h p e -> p h e")))
            sp.wait_ge(id_zero, 2)
            for g in range(4):
                loads.append((wo1[32 * g:32 * g + HD1, :, :],
                              Wo1[4 * g * HD1:4 * (g + 1) * HD1, :].rearrange("(kv d) n -> d kv n", kv=KV1)))
            assert len(loads) == NW, len(loads)
            for dst, src in loads:
                sp.dma_start(dst, src, allow_slow_non_contiguous=True).then_inc(w_in, 16)

            with sp.Fori(0, B) as b:
                sp.wait_ge(base1, 1 + b)
                sp.dma_start(xs[:], x[bass.ds(b, 1)].rearrange("o (t p) d -> p (o t) d", p=P)).then_inc(x_in, 16)
                sp.dma_start(cs[:], ctx[bass.ds(b, 1)].rearrange("o (t p) d -> p (o t) d", p=P)).then_inc(c_in, 16)
                for c in range(DC):
                    g_landed(sp, b, "q1", c)
                    for part in range(2):
                        sp.dma_start(q_parts[part, c * P:(c + 1) * P, :], parts[:, c, part, :].bitcast(F32)).then_inc(parts_out, 16)
                g_landed(sp, b, "k1", 0)
                sp.dma_start(k_parts.rearrange("s r n -> r s n"), k1parts[:].bitcast(F32)).then_inc(kparts_out, 16)
                sp.wait_ge(kparts_out, 16 * (b + 1))
                for blk, part in enumerate((0, 0, 1, 1)):
                    sp.dma_start(k1st[blk * HD1:(blk + 1) * HD1, :, :].bitcast(F32),
                                 k_parts[part].rearrange("(h d) n -> d h n", d=HD1)).then_inc(k1_in, 16)
                sp.wait_ge(parts_out, 1 + 64 * (b + 1))

                def load_group(g):
                    dst = q_slots[g % 3]
                    for blk, part in enumerate((0, 1, 0, 1)):
                        sp.dma_start(dst[blk * HD1:(blk + 1) * HD1, :, :].bitcast(F32),
                                     q_parts[part, 4 * g * HD1:4 * (g + 1) * HD1, :].rearrange("(h d) n -> d h n", d=HD1)
                                     ).then_inc(q1_in[g % 3], 16)
                    sp.dma_start(dst[KQ - 1:KQ, :, :].bitcast(F32), zero_row[:, :, :]).then_inc(q1_in[g % 3], 16)

                def place_maxima(g):
                    g_landed(sp, b, "nt", g)
                    sp.dma_start(q_slots[g % 3][KQ - 1:KQ, :, :].bitcast(F32),
                                 negrow[:].bitcast(F32)).then_inc(nm_in[g % 3], 16)

                for g in range(3):
                    load_group(g)
                place_maxima(0)
                place_maxima(1)
                s_written(sp, b, "X", (0, 2 * NT - 1))
                load_group(3)
                place_maxima(2)
                place_maxima(3)
                s_written(sp, b, "X", (2, 2 * NT - 1))
                sp.dma_start(q_slots[2][KQ - 1:KQ, :, :].bitcast(F32), zero_row[:, :, :]).then_inc(zero_in, 16)

            def weights(r, first_turn=False):
                for s in range(EU):
                    n = r * EU + s
                    if not first_turn:
                        sp.wait_ge(e_down, n + 1 - EU)
                    sp.dma_start(wup[:, s, :, :], eup_w[bass.ds(n, 1)].rearrange("o (c p) n -> p (o c) n", p=P)).then_inc(we_in[s], 16)
                    sp.dma_start(wdn[:, s, :], edown_w[bass.ds(n, 1)].rearrange("o p n -> p (o n)")).then_inc(we_in[s], 16)

            g_landed(sp, B - 1, "down", 1)
            weights(0, first_turn=True)
            sp.wait_ge(pick, (B + 1) * ROUND_STEPS)
            for half in range(2):
                sp.dma_start(both[:, half * CAP:(half + 1) * CAP], found[half * E:(half + 1) * E, :]).then_inc(moved, 16)

            with sp.Fori(1, TURNS) as r:
                weights(r)
            for s in range(EU):
                sp.wait_ge(y_add[s], 16 * TURNS)

            def load_sums(k, half):
                rows = bass.ds((2 * k + half) * SEQ, SEQ)
                for dst, src in ((fin, sums[0]), (fin1, sums[1])):
                    sp.dma_start(dst[half], src[rows, :].rearrange("(t p) n -> p t n", p=P)).then_inc(f_in[half], 16)

            for half in range(2):
                load_sums(0, half)
            def store_pair(k):
                for half in range(2):
                    sp.wait_ge(ln_done, NT * (2 * B + 2 * k + half + 1))
                    sp.dma_start(out[bass.ds(2 * k + half, 1)].rearrange("o (t p) d -> p (o t) d", p=P), fin[half]).then_inc(f_out[half], 16)

            with sp.Fori(0, B // 2 - 1) as k:
                store_pair(k)
                for half in range(2):
                    sp.wait_ge(f_out[half], 16 * (k + 1))
                    load_sums(k + 1, half)
            store_pair(B // 2 - 1)
            for half in range(2):
                sp.wait_ge(f_out[half], 16 * (B // 2))

        start_at_1 = [base1, *g_done, *s_done, pt_ready, parts_out, batch_out, keyv_done, keys_in, kept]

        @block.gpsimd
        def _(pool):
            for counted in start_at_1:
                pool.sem_inc(counted, 1)
            nc.gpsimd.memset(wo1[:], 0.0).then_inc(id_zero, 1)
            nc.gpsimd.memset(ident[:], 0.0).then_inc(id_zero, 1)
            nc.gpsimd.memset(maskb[:], 0.0).then_inc(consts, 1)
            nc.gpsimd.memset(zero[:], 0.0).then_inc(consts, 1)
            nc.gpsimd.memset(minus_half[:], -0.5).then_inc(consts, 1)
            pool.wait_ge(consts, 3)
            nc.gpsimd.memset(sum_rows[:], 0.0).then_inc(consts, 1)
            nc.gpsimd.memset(k2z[:].bitcast(F32), 0.0).then_inc(consts, 1)
            nc.gpsimd.memset(v1s[:], 0.0).then_inc(consts, 1)
            nc.gpsimd.memset(keys[:], 0.0).then_inc(consts, 1)
            pool.wait_ge(consts, 7)
            nc.gpsimd.memset(v1s[:, :, :, HD1:HD1 + 1], 1.0).then_inc(consts, 1)
            nc.gpsimd.affine_select(out=sum_rows[:], in_=sum_rows[:], compare_op=ALU.not_equal, fill=1.0, base=-HD1,
                                    pattern=[[-32, 4]], channel_multiplier=1).then_inc(consts, 1)
            nc.gpsimd.iota(token_key[:], pattern=[[-P, NT]], base=TOK, channel_multiplier=-1,
                           allow_small_or_imprecise_dtypes=True).then_inc(consts, 1)
            nc.gpsimd.iota(slot_no[:], pattern=[[0, 1]], base=0, channel_multiplier=1,
                           allow_small_or_imprecise_dtypes=True).then_inc(consts, 1)
            pool.wait_ge(id_zero, 2)
            nc.gpsimd.affine_select(out=ident[:], in_=ident[:], compare_op=ALU.not_equal, fill=1.0, base=0,
                                    pattern=[[-1, P]], channel_multiplier=1).then_inc(consts, 1)
            nc.gpsimd.affine_select(out=maskb[:], in_=maskb[:], compare_op=ALU.is_ge, fill=MASKED, base=0,
                                    pattern=[[-1, P]], channel_multiplier=1).then_inc(consts, 1)
            pool.wait_ge(consts, 13)
            nc.gpsimd.tensor_copy(identb[:], ident[:]).then_inc(consts, 1)
            for i in range(4):
                pool.dma_start(sums[1][i * 1024:(i + 1) * 1024, :].rearrange("(a p) n -> p a n", p=P),
                               zero[:, 0:D].rearrange("p (o n) -> p o n", o=1).to_broadcast([P, 8, D])).then_inc(zero_out, 16)
            for i in range(2):
                pool.dma_start(sums[i][TOK:NROW, :], zero[:, 0:D]).then_inc(zero_out, 16)
            pool.dma_start(table[TOK:NROW, :], zero[:, 0:ROW]).then_inc(zero_out, 16)
            pool.wait_ge(w_in, 16 * (NW))
            nc.gpsimd.tensor_scalar(wq1[:], wq1[:], HD1 ** -0.5, None, ALU.mult).then_inc(wprep, 1)
            nc.gpsimd.tensor_scalar(bq1c[:], bq1c[:], HD1 ** -0.5, None, ALU.mult).then_inc(wprep, 1)
            nc.gpsimd.tensor_scalar(wq2[:], wq2[:], HD2 ** -0.5, None, ALU.mult).then_inc(wprep, 1)
            nc.gpsimd.tensor_scalar(bqc[:], bqc[:], HD2 ** -0.5, None, ALU.mult).then_inc(wprep, 1)

            def inverse_deviation(k):
                pool.wait_ge(ag_done, NT * (k + 1))
                alone(pool)
                nc.gpsimd.tensor_scalar(varps[:], mv[:, :, 1], EPS, None, ALU.add).then_inc(ve_done, 1)
                pool.wait_ge(ve_done, k + 1)
                nc.gpsimd.tensor_tensor(rstd[:], varps[:], minus_half[:], ALU.pow).then_inc(rs_done, 1)

            with pool.Fori(0, B) as b:
                for kind, n in order:
                    if kind == "ln1":
                        inverse_deviation(2 * b)
                    elif kind == "ln2":
                        inverse_deviation(2 * b + 1)
                    if kind == "k1":
                        pool.wait_ge(x_in, 16 * (b + 1))
                        nc.gpsimd.tensor_tensor(x1s[:], xs[:], bo1r[:].rearrange("p (o n) -> p o n", o=1).to_broadcast([P, NT, D]),
                                                ALU.add).then_inc(base1, 1)
                    elif kind == "ln1":
                        pool.wait_ge(ln_done, (2 * b + 1) * NT)
                        nc.gpsimd.tensor_tensor(x2s[:, :, 0:D], x1s[:], bo2r[:].rearrange("p (o n) -> p o n", o=1).to_broadcast([P, NT, D]),
                                                ALU.add).then_inc(base2, 1)
                    elif kind == "keys":
                        pool.wait_ge(keyv_done, 1 + b + 1)
                        pool.dma_start(table[bass.ds(b * SEQ, SEQ), :].rearrange("(t p) n -> p t n", p=P), x2s[:]).then_inc(table_out, 16)
                    elif kind == "down" and n == 1:
                        pool.wait_ge(y0_done, 2 * (b + 1))
                        pool.dma_start(sums[0][bass.ds(b * SEQ, SEQ), :].rearrange("(t p) n -> p t n", p=P), y0s).then_inc(y0_out, 16)
                        for stored in (table_out, y0_out):
                            pool.wait_ge(stored, 16 * (b + 1))
                        pool.sem_inc(batch_out, 1)

            pool.wait_ge(zero_out, 16 * 7)
            def gather(s):
                alone(pool)
                pool.indirect_dma_start(out=xg[:, s, :], out_offset=None, in_=table,
                                        in_offset=bass.IndirectOffsetOnAxis(ap=idx_gather[:, s:s + 1], axis=0)).then_inc(xg_in[s], 16)

            def add_and_gather(r, first_turn=False, last_turn=False):
                for s in range(EU):
                    pool.wait_ge(e_yo, r * EU + s + 1)
                    if s >= YS:
                        pool.wait_ge(y_add[s - YS], 16 * (r + 1))
                    elif not first_turn:
                        pool.wait_ge(y_add[s - YS], 16 * r)
                    alone(pool)
                    pool.indirect_dma_start(out=sums[s % YS], out_offset=bass.IndirectOffsetOnAxis(ap=idx_add[:, s:s + 1], axis=0),
                                            in_=yo[:, s % PU, :], in_offset=None, compute_op=ALU.add).then_inc(y_add[s], 16)
                    if not last_turn:
                        gather(s)

            pool.wait_ge(idx0_done, 1)
            for s in range(EU):
                gather(s)
            add_and_gather(0, first_turn=True)
            with pool.Fori(1, TURNS - 1) as r:
                add_and_gather(r)
            add_and_gather(TURNS - 1, last_turn=True)
            with pool.Fori(0, B) as b:
                inverse_deviation(2 * B + b)

        @block.tensor
        def _(pe):
            pe.wait_ge(consts, 14)
            pe.wait_ge(ones_done, 1)
            pe.wait_ge(wprep, 4)

            def bank(b, use, n, *results):
                g = g_index[use, n]
                need = {g % 2: g // 2}
                for r in results:
                    k = g_index[r]
                    need[k % 2] = max(need.get(k % 2, 0), k // 2 + 1)
                for k, count in sorted(need.items()):
                    pe.wait_ge(g_done[k], 1 + b * (NG // 2) + count)
                return G[:, g % 2, :]

            def transposed(b, use, c, src):
                dst = bank(b, use, c)
                for t in range(NT):
                    i = nc.tensor.transpose(dst[:, t * P:(t + 1) * P], src[:, t, c * P:(c + 1) * P], ident[:])
                i.then_inc(g_ready, 1)

            def product(dst, lhs, rhs):
                n = len(lhs)
                for i, (a, m) in enumerate(zip(lhs, rhs)):
                    last = nc.tensor.matmul(dst, a, m, start=(i == 0), stop=(i == n - 1))
                return last

            def scores(b, kind, n):
                k = s_index[kind, n]
                pe.wait_ge(s_done[k % 2], 1 + b * (NS // 2) + k // 2)
                return S[:, k % 2, :, :]

            with pe.Fori(0, B) as b:
                for kind, n in order:
                    if kind == "xT":
                        pe.wait_ge(x_in, 16 * (b + 1))
                        transposed(b, "xT", n, xs)
                    elif kind == "cT":
                        pe.wait_ge(c_in, 16 * (b + 1))
                        transposed(b, "cT", n, cs)
                    elif kind == "q1":
                        product(bank(b, "q1", n, ("xT", 0), ("xT", 1)), [wq1[:, c, n * P:(n + 1) * P] for c in range(DC)],
                                [xT[:, c, :] for c in range(DC)]).then_inc(g_ready, 1)
                    elif kind == "k1":
                        product(bank(b, "k1", 0)[0:KV1 * HD1, :], [wk1[:, c, :] for c in range(DC)],
                                [xT[:, c, :] for c in range(DC)]).then_inc(g_ready, 1)
                    elif kind == "v1":
                        dst = bank(b, "v1", 0)
                        for t in range(NT):
                            i = product(dst[:, t * 64:(t + 1) * 64], [xT[:, c, t * P:(t + 1) * P] for c in range(DC)],
                                        [wv1[:, c, :] for c in range(DC)])
                        i.then_inc(g_ready, 1)
                    elif kind == "V2":
                        t, half = n // 2, n % 2
                        product(bank(b, "V2", n, ("cT", 0), ("cT", 1)), [cT[:, c, t * P:(t + 1) * P] for c in range(DC)],
                                [wv2[:, c, half * 512:(half + 1) * 512] for c in range(DC)]).then_inc(g_ready, 1)
                    elif kind == "M":
                        g, i = n
                        if n == (0, 0):
                            pe.wait_ge(k1_in, 64 * (b + 1))
                        if i == 0:
                            pe.wait_ge(q1_in[g % 3], 80 * (b * (2 if g % 3 == 0 else 1) + g // 3 + 1))
                        dst = scores(b, "M", n)
                        for j in range(2):
                            at = nc.tensor.matmul(dst[:, j, :], q_slots[g % 3][0:KQ, 2 * (i % 2) + j, (i // 2) * P:(i // 2 + 1) * P],
                                                  k1st[0:KQ, g, :], start=True, stop=True)
                        at.then_inc(s_ready, 1)
                    elif kind == "NT":
                        s_landed(pe, b, ("M", (n, 2 * NT - 1)))
                        dst = bank(b, "nt", n)
                        alone(pe)
                        nc.tensor.transpose(dst[0:4 * NT, 0:P], negmax1[:, n % 2, :, :].rearrange("p h t -> p (h t)"), ident[:]).then_inc(g_ready, 1)
                    elif kind == "X":
                        g, i = n
                        if i == 0:
                            pe.wait_ge(nm_in[g % 3], 16 * (b * (2 if g % 3 == 0 else 1) + g // 3 + 1))
                        dst = scores(b, "X", n)
                        for j in range(2):
                            at = nc.tensor.matmul(dst[:, j, :], k1st[0:KQ, g, (i // 2) * P:(i // 2 + 1) * P],
                                                  q_slots[g % 3][0:KQ, 2 * (i % 2) + j, :], start=True, stop=True)
                        at.then_inc(s_ready, 1)
                    elif kind == "PV1":
                        g, kt = n
                        s_landed(pe, b, ("X", (g, 2 * kt)), ("X", (g, 2 * kt + 1)))
                        if kt == 0 and g >= 2:
                            pe.wait_ge(z_copied, b * KV1 + g - 1)
                        if kt == 0:
                            g_landed(pe, b, "v1", 0) if g == 0 else None
                        for h in range(4):
                            at = nc.tensor.matmul(T[32 * h:32 * h + 32, g % 2, :], v1s[:, kt, g, :], p1[:, kt, h, :],
                                                  start=(kt == 0), stop=(kt == NT - 1), skip_group_check=True)
                        if kt == NT - 1:
                            at.then_inc(z_ready, 1)
                    elif kind == "SM":
                        pe.wait_ge(z_copied, b * KV1 + n + 1)
                        dst = bank(b, "sm", n)
                        for t in range(NT):
                            at = nc.tensor.matmul(dst[:, 4 * t:4 * t + 4], zT[:, n, t * P:(t + 1) * P], sum_rows[:], start=True, stop=True)
                        at.then_inc(g_ready, 1)
                    elif kind == "RS":
                        dst = bank(b, "rs", n, ("sm", n))
                        for t in range(NT):
                            at = nc.tensor.matmul(dst[:, t * P:(t + 1) * P],
                                                  rwide[:, t * P:(t + 1) * P],
                                                  ident[:], start=True, stop=True)
                        at.then_inc(g_ready, 1)
                    elif kind in ("o1", "o2"):
                        w, chunks = (wo1, KV1) if kind == "o1" else (wo2, UNITS)
                        if kind == "o1":
                            pe.wait_ge(z_divided, KV1 * (b + 1))
                            dst = bank(b, "o1", n)
                        else:
                            dst = bank(b, "o2", n, *(("PV2", u) for u in range(UNITS)))
                        for t in range(2):
                            tt = 2 * n + t
                            i = product(dst[:, t * D:(t + 1) * D], [zT[:, u, tt * P:(tt + 1) * P] for u in range(chunks)],
                                        [w[:, u, :] for u in range(chunks)])
                        i.then_inc(g_ready, 1)
                    elif kind == "x1T":
                        pe.wait_ge(ln_done, (2 * b + 1) * NT)
                        transposed(b, "x1T", n, x1s)
                    elif kind == "Q2":
                        product(bank(b, "q2", n, ("x1T", 0), ("x1T", 1)), [wq2[:, c, n * P:(n + 1) * P] for c in range(DC)],
                                [xT[:, c, :] for c in range(DC)]).then_inc(g_ready, 1)
                    elif kind == "K2":
                        product(bank(b, "k2", n, ("cT", 0), ("cT", 1)), [wk2[:, c, n * P:(n + 1) * P] for c in range(DC)],
                                [cT[:, c, :] for c in range(DC)]).then_inc(g_ready, 1)
                    elif kind == "S2":
                        u, qt = n // NT, n % NT
                        w = (qt + 1) * P
                        if qt == 0:
                            g_landed(pe, b, "q2", u)
                            g_landed(pe, b, "k2", u)
                        if n == 0:
                            pe.wait_ge(zero_in, 16 * (b + 1))
                        bank2 = scores(b, "S2", n)
                        for j in range(2):
                            dst = bank2[:, j, 0:w]
                            hi = parts[:, u % 2, 0, qt * P:(qt + 1) * P]
                            lo = parts[:, u % 2, 1, qt * P:(qt + 1) * P]
                            nc.tensor.matmul(dst, hi, k2z[:, j, u % 2, 0, 0:w], start=True, stop=False)
                            nc.tensor.matmul(dst, lo, k2z[:, j, u % 2, 0, 0:w], start=False, stop=False)
                            nc.tensor.matmul(bank2[:, j, qt * P:w], identb[:], maskb[:], start=False, stop=False,
                                             skip_group_check=True)
                            i = nc.tensor.matmul(dst, hi, k2z[:, j, u % 2, 1, 0:w], start=False, stop=True)
                        i.then_inc(s_ready, 1)
                    elif kind == "T2":
                        pe.wait_ge(pn_ready, step_no(b, n) + 1)
                        pe.wait_ge(pt_ready, 1 + step_no(b, n))
                        for j in range(2):
                            for kt in range(n % NT + 1):
                                i = nc.tensor.transpose(T[:, j, kt * P:(kt + 1) * P], probs[:, n % 2, j, kt * P:(kt + 1) * P], ident[:])
                        i.then_inc(t_ready, 1)
                    elif kind == "PV2":
                        pe.wait_ge(pt_ready, 1 + step_no(b, NT * n + NT))
                        dst = bank(b, "PV2", n, *(("V2", i) for i in range(2 * NT)))
                        for kt in range(NT):
                            for j in range(2):
                                h = 2 * n + j
                                i = nc.tensor.matmul(dst[64 * j:64 * j + 64, kt * P:SEQ], v2s[:, kt, h * HD2:(h + 1) * HD2],
                                                     pT[:, n % 2, j, kt, kt * P:SEQ], start=(kt == 0), stop=(kt == NT - 1),
                                                     skip_group_check=True)
                        i.then_inc(g_ready, 1)
                    elif kind == "x2T":
                        pe.wait_ge(ln_done, (2 * b + 2) * NT)
                        transposed(b, "x2T", n, x2s)
                    elif kind == "gate":
                        dst = bank(b, "gate", 0, ("x2T", 0), ("x2T", 1))
                        for t in range(NT):
                            i = product(dst[:, t * (E + 1):(t + 1) * (E + 1)], [xT[:, c, t * P:(t + 1) * P] for c in range(DC)],
                                        [gw[:, c, :] for c in range(DC)])
                        i.then_inc(g_ready, 1)
                    elif kind == "keys":
                        pe.wait_ge(keyv_done, 1 + b + 1)
                        dst = bank(b, "keys", 0)
                        alone(pe)
                        for t in range(2):
                            i = nc.tensor.transpose(dst[:, t * P:(t + 1) * P], keyv[:, t, :, :].rearrange("p h e -> p (h e)"), ident[:])
                        i.then_inc(g_ready, 1)
                    elif kind == "up":
                        dst = scores(b, "up", n)
                        for j in range(2):
                            at = product(dst[:, j, :], [supw[:, c, j * FS + n * P:j * FS + (n + 1) * P] for c in range(DC)],
                                         [xT[:, c, :] for c in range(DC)])
                        at.then_inc(s_ready, 1)
                    elif kind == "down":
                        s_landed(pe, b, *(("up", f) for f in range(FS // P)))
                        dst = bank(b, "down", n)
                        for t in range(2):
                            tt = 2 * n + t
                            i = product(dst[:, t * D:(t + 1) * D], [hid[:, f, tt * P:(tt + 1) * P] for f in range(FS // P)],
                                        [sdownw[:, f, :] for f in range(FS // P)])
                        i.then_inc(g_ready, 1)

            pe.wait_ge(pick, (B + 2) * ROUND_STEPS)
            nc.tensor.transpose(T[:, 0, 0:E], first, ident[0:E, 0:E]).then_inc(firstT, 1)

            def bank_of(s):
                return S[:, s % PU // 2, s % 2, :]

            def tokens(r, s, first_turn):
                if s >= PU or not first_turn:
                    pe.wait_ge(e_act, r * EU + s + 1 - PU)
                pe.wait_ge(xg_in[s], 16 * (r + 1))
                for c in range(DC):
                    i = nc.tensor.transpose(bank_of(s)[:, c * P:(c + 1) * P], xg[:, s, c * P:(c + 1) * P], ident[:])
                i.then_inc(e_tr, 1)

            def up(r, s):
                pe.wait_ge(e_trs, r * EU + s + 1)
                pe.wait_ge(we_in[s % EU], 32 * (r + 1 if s >= 0 else r))
                for half in range(2):
                    i = product(bank_of(s % EU)[:, 256 + half * P:256 + (half + 1) * P],
                                [wup[:, s % EU, c, half * FI:(half + 1) * FI] for c in range(DC)],
                                [xgT[:, s % PU, c * P:(c + 1) * P] for c in range(DC)])
                i.then_inc(e_up, 1)

            def down(r, s, first_turn):
                pe.wait_ge(e_act, r * EU + s + 1)
                if s >= PU or not first_turn:
                    pe.wait_ge(e_yo, r * EU + s + 1 - PU)
                nc.tensor.matmul(out_of(s)[:, 0:D], act[:, s % PU, :], wdn[:, s % EU, :], start=True, stop=True).then_inc(e_down, 1)

            def experts(r, first_turn=False):
                for s in range(EU):
                    tokens(r, s, first_turn)
                    if s >= 1 or not first_turn:
                        up(r, s - 1)
                    if s >= 2 or not first_turn:
                        down(r, s - 2, first_turn)

            experts(0, first_turn=True)
            with pe.Fori(1, TURNS) as r:
                experts(r)
            down(TURNS, -2, False)
            up(TURNS, -1)
            down(TURNS, -1, False)

        @block.scalar
        def _(a):
            def evac(b, use, n, dst, bias=None):
                g_written(a, b, use, n)
                if bias is None:
                    nc.scalar.copy(dst, g_bank(use, n)).then_inc(g_sem(use, n), 1)
                else:
                    nc.scalar.activation(dst, g_bank(use, n), ACT.Identity, bias=bias).then_inc(g_sem(use, n), 1)

            def softmax(b, n):
                w = (n % NT + 1) * P
                a.wait_ge(nm_ready, step_no(b, n) + 1)
                if n >= 2:
                    a.wait_ge(t_ready, step_no(b, n - 1))
                for j in range(2):
                    i = nc.scalar.activation(probs[:, n % 2, j, 0:w], s_slot("S2", n)[:, j, 0:w], ACT.Exp, bias=negmax[:, n % 4, j:j + 1],
                                             accum_out=rowsum[:, n % 4, j:j + 1])
                i.then_inc(s_sem("S2", n), 1)

            a.wait_ge(consts, 14)
            a.wait_ge(wprep, 4)
            with a.Fori(0, B) as b:
                for kind, n in batch_timeline("scalar"):
                    if kind in ("xT", "x1T", "x2T"):
                        evac(b, kind, n, xT[:, n, :])
                    elif kind == "cT":
                        evac(b, kind, n, cT[:, n, :])
                    elif kind == "q1":
                        g_written(a, b, "q1", n)
                        a.wait_ge(parts_out, 1 + 64 * b)
                        nc.scalar.activation(parts[:, n, 0, :], g_bank("q1", n), ACT.Identity, bias=bq1c[:, n:n + 1]).then_inc(hi_done, 1)
                    elif kind == "k1":
                        g_written(a, b, "k1", 0)
                        nc.scalar.activation(k1parts[:, 0, :], g_bank("k1", 0)[0:64, :], ACT.Identity, bias=bk1c[:]).then_inc(hi_done, 1)
                    elif kind == "V2":
                        if n >= NT or n % 2 == 0:
                            if n == 6:
                                a.wait_ge(batch_out, 1 + b)
                            evac(b, "V2", n, v2s[:, n // 2, n % 2 * 512:(n % 2 + 1) * 512])
                    elif kind == "Q2":
                        g_written(a, b, "q2", n)
                        nc.scalar.activation(parts[:, n % 2, 0, :], g_bank("q2", n), ACT.Identity, bias=bqc[:, n:n + 1]).then_inc(hi_done, 1)
                    elif kind == "K2":
                        g_written(a, b, "k2", n)
                        for j in range(2):
                            r = slice(64 * j, 64 * j + 64)
                            i = nc.scalar.activation(k2z[r, j, n % 2, 0, :], g_bank("k2", n)[r, :], ACT.Identity, bias=bkc[r, n:n + 1])
                        i.then_inc(hi_done, 1)
                    elif kind == "NT":
                        g_written(a, b, "nt", n)
                        if n >= 1:
                            a.wait_ge(nm_in[(n - 1) % 3], 16 * (b * (2 if (n - 1) % 3 == 0 else 1) + (n - 1) // 3 + 1))
                        nc.scalar.copy(negrow[:], g_bank("nt", n)[0:4 * NT, 0:P]).then_inc(g_sem("nt", n), 1)
                    elif kind == "X":
                        g, i = n
                        s_written(a, b, "X", n)
                        nc.scalar.activation(p1[:, i // 2, 2 * (i % 2):2 * (i % 2) + 2, :], s_slot("X", n), ACT.Exp).then_inc(s_sem("X", n), 1)
                    elif kind == "E1":
                        a.wait_ge(z_ready, b * KV1 + n + 1)
                        nc.scalar.copy(zT[:, n, :], T[:, n % 2, :]).then_inc(z_copied, 1)
                    elif kind == "S2":
                        softmax(b, n)
                    elif kind == "T2" and n % 2 == 1:
                        turn(a, nc.scalar.copy, b, n)
                    elif kind == "PV2":
                        evac(b, "PV2", n, zT[:, n, :], bvc[:, n:n + 1])
                    elif kind == "gate":
                        a.wait_ge(gmax_done, b + 1)
                        for t in range(NT):
                            nc.scalar.activation(gexp[:, t, :], g_bank("gate", 0)[:, t * (E + 1):t * (E + 1) + E], ACT.Exp,
                                                 bias=gneg[:, t:t + 1], accum_out=gsum[:, t:t + 1])
                        nc.scalar.activation(gtmp[:, :, 0], g_bank("gate", 0)[:, 0:NT * (E + 1)].rearrange("p (t e) -> p t e", t=NT)[:, :, E],
                                             ACT.Tanh, scale=0.5).then_inc(g_sem("gate", 0), 1)
                    elif kind == "keys":
                        g_written(a, b, "keys", 0)
                        nc.scalar.copy(keys[:, CAP:], g_bank("keys", 0)[:, 0:SEQ // 2]).then_inc(keys_in, 1)
                        a.wait_ge(keys_in, 1 + b + 1)
                        a.sem_inc(g_sem("keys", 0), 1)
                    elif kind == "up":
                        s_written(a, b, "up", n)
                        if n >= 2:
                            a.wait_ge(gated, b * (FS // P) + n - 1)
                        nc.scalar.activation(tnh[:, n % 2, :], s_slot("up", n)[:, 0, :], ACT.Tanh, scale=0.5).then_inc(tanh_done, 1)

            def hidden(r, s):
                a.wait_ge(e_up, r * EU + s + 1)
                nc.scalar.activation(ath[:, s % PU, :], S[:, s % PU // 2, s % 2, 256:256 + FI], ACT.Tanh, scale=0.5).then_inc(e_tanh, 1)

            def experts(r, first_turn=False):
                for s in range(EU):
                    a.wait_ge(e_tr, r * EU + s + 1)
                    if s >= PU or not first_turn:
                        a.wait_ge(e_up, r * EU + s + 1 - PU)
                    nc.scalar.copy(xgT[:, s % PU, :], S[:, s % PU // 2, s % 2, 0:D]).then_inc(e_trs, 1)
                    if s >= 1 or not first_turn:
                        hidden(r, s - 1)

            experts(0, first_turn=True)
            with a.Fori(1, TURNS) as r:
                experts(r)
            hidden(TURNS, -1)

        @block.vector
        def _(v):
            def low_part(b, use, n, dst, src, bias, hi, count):
                v.wait_ge(hi_done, count)
                return nc.vector.scalar_tensor_tensor(out=dst, in0=src, scalar=bias, in1=hi.bitcast(F32), op0=ALU.add, op1=ALU.subtract)

            HI = DC + 1 + 2 * UNITS

            def maxima(b, n):
                w = (n % NT + 1) * P
                s_written(v, b, "S2", n)
                nc.vector.tensor_reduce(negmax[:, n % 4, :], s_slot("S2", n)[:, :, 0:w], AX_X, ALU.max, negate=True).then_inc(nm_ready, 1)

            def divide(b, n):
                w = (n % NT + 1) * P
                s_landed(v, b, ("S2", n))
                nc.vector.reciprocal(rrow[:, n % 4, :], rowsum[:, n % 4, :]).then_inc(rr_ready, 1)
                v.wait_ge(rr_ready, step_no(b, n) + 1)
                for j in range(2):
                    i = nc.vector.tensor_scalar(probs[:, n % 2, j, 0:w], probs[:, n % 2, j, 0:w], rrow[:, n % 4, j:j + 1], None, ALU.mult)
                i.then_inc(pn_ready, 1)

            def layernorm(k, tile):
                v.wait_ge(res_done, 2 * (k + 1))
                for t in range(NT):
                    nc.vector.bn_stats(stats[:, t, :], tile[:, t, 0:D]).then_inc(st_done, 1)
                v.wait_ge(st_done, NT * (k + 1))
                alone(v)
                for t in range(NT):
                    nc.vector.bn_aggr(mv[:, t, :], stats[:, t, :]).then_inc(ag_done, 1)
                v.wait_ge(rs_done, k + 1)
                for t in range(NT):
                    nc.vector.tensor_scalar(tile[:, t, 0:D], tile[:, t, 0:D], mv[:, t, 0:1], rstd[:, t:t + 1],
                                            ALU.subtract, ALU.mult).then_inc(ln_done, 1)

            def search(src, dst, r, at):
                if r >= 1:
                    v.wait_ge(pick, at + 2 * r)
                alone(v)
                nc.vector.max(dst[:, 8 * r:8 * r + 8], src).then_inc(pick, 1)
                v.wait_ge(pick, at + 2 * r + 1)
                alone(v)
                nc.vector.match_replace(src, dst[:, 8 * r:8 * r + 8], src, 0.0).then_inc(pick, 1)

            nc.vector.memset(k1st[KQ - 1:KQ, :, :].bitcast(F32), 1.0).then_inc(ones_done, 1)
            v.wait_ge(consts, 14)
            v.wait_ge(wprep, 4)
            with v.Fori(0, B) as b:
                for kind, n in batch_timeline("vector"):
                    if kind == "q1":
                        low_part(b, "q1", n, parts[:, n, 1, :], g_bank("q1", n), bq1c[:, n:n + 1], parts[:, n, 0, :],
                                 b * HI + n + 1).then_inc(g_sem("q1", n), 1)
                    elif kind == "k1":
                        low_part(b, "k1", 0, k1parts[:, 1, :], g_bank("k1", 0)[0:64, :], bk1c[:], k1parts[:, 0, :],
                                 b * HI + DC + 1).then_inc(g_sem("k1", 0), 1)
                    elif kind == "v1":
                        g_written(v, b, "v1", 0)
                        for t in range(NT):
                            i = nc.vector.tensor_tensor(v1s[:, t, :, 0:HD1], g_bank("v1", 0)[:, t * 64:(t + 1) * 64].rearrange("p (h d) -> p h d", h=KV1),
                                                        bv1r[:].rearrange("p (h d) -> p h d", h=KV1), ALU.add)
                        i.then_inc(g_sem("v1", 0), 1)
                    elif kind == "V2":
                        if n < NT and n % 2 == 1:
                            g_written(v, b, "V2", n)
                            nc.vector.tensor_copy(v2s[:, n // 2, 512:1024], g_bank("V2", n)).then_inc(g_sem("V2", n), 1)
                    elif kind == "K2":
                        for j in range(2):
                            r = slice(64 * j, 64 * j + 64)
                            i = low_part(b, "k2", n, k2z[r, j, n % 2, 1, :], g_bank("k2", n)[r, :], bkc[r, n:n + 1],
                                         k2z[r, j, n % 2, 0, :], b * HI + DC + 1 + 2 * n + 1)
                        i.then_inc(g_sem("k2", n), 1)
                    elif kind == "Q2":
                        low_part(b, "q2", n, parts[:, n % 2, 1, :], g_bank("q2", n), bqc[:, n:n + 1], parts[:, n % 2, 0, :],
                                 b * HI + DC + 1 + 2 * n + 2).then_inc(g_sem("q2", n), 1)
                    elif kind == "pick":
                        if n == 0:
                            v.wait_ge(keys_in, 1 + b)
                            v.wait_ge(kept, 1 + b)
                        search(keys[:], found, n, b * ROUND_STEPS)
                        if n == CAP // 8 - 1:
                            v.wait_ge(pick, (b + 1) * ROUND_STEPS)
                            nc.vector.tensor_copy(keys[:, 0:CAP], found[:]).then_inc(kept, 1)
                    elif kind == "M":
                        g, i = n
                        s_written(v, b, "M", n)
                        nc.vector.tensor_reduce(negmax1[:, g % 2, 2 * (i % 2):2 * (i % 2) + 2, i // 2], s_slot("M", n), AX_X, ALU.max,
                                                negate=True).then_inc(s_sem("M", n), 1)
                    elif kind == "SM":
                        g_written(v, b, "sm", n)
                        nc.vector.reciprocal(rsum1[:], g_bank("sm", n)[:, 0:4 * NT]).then_inc(rsum1_done, 1)
                        v.wait_ge(rsum1_done, b * KV1 + n + 1)
                        nc.vector.tensor_copy(rwide.rearrange("p (s o) -> p s o", o=32),
                                              rsum1[:].rearrange("p (s o) -> p s o", o=1).to_broadcast([P, 4 * NT, 32])).then_inc(g_sem("sm", n), 1)
                    elif kind == "RS":
                        g_written(v, b, "rs", n)
                        nc.vector.tensor_tensor(zT[:, n, :], g_bank("rs", n), zT[:, n, :], ALU.mult).then_inc(z_divided, 1)
                        v.wait_ge(z_divided, b * KV1 + n + 1)
                        v.sem_inc(g_sem("rs", n), 1)
                    elif kind == "S2":
                        maxima(b, n)
                    elif kind == "R2":
                        divide(b, n)
                    elif kind == "T2" and n % 2 == 0:
                        turn(v, nc.vector.tensor_copy, b, n)
                    elif kind in ("o1", "o2"):
                        tile = x1s if kind == "o1" else x2s
                        if n == 0:
                            v.wait_ge(*((base1, 1 + b + 1) if kind == "o1" else (base2, b + 1)))
                        g_written(v, b, kind, n)
                        dst = tile[:, 2 * n:2 * n + 2, 0:D]
                        nc.vector.tensor_tensor(dst, g_bank(kind, n).rearrange("p (t n) -> p t n", t=2), dst, ALU.add).then_inc(res_done, 1)
                        v.wait_ge(res_done, 4 * b + (0 if kind == "o1" else 2) + n + 1)
                        v.sem_inc(g_sem(kind, n), 1)
                    elif kind == "ln1":
                        layernorm(2 * b, x1s)
                    elif kind == "ln2":
                        layernorm(2 * b + 1, x2s)
                    elif kind == "gate":
                        g_written(v, b, "gate", 0)
                        logits = g_bank("gate", 0)[:, 0:NT * (E + 1)].rearrange("p (t e) -> p t e", t=NT)[:, :, 0:E]
                        nc.vector.tensor_reduce(gneg[:], logits, AX_X, ALU.max, negate=True).then_inc(gmax_done, 1)
                        g_landed(v, b, "gate", 0)
                        v.wait_ge(keyv_done, 1 + b)
                        GS = 10
                        at = [0]

                        def link(i):
                            at[0] += 1
                            i.then_inc(gate_step, 1)
                            v.wait_ge(gate_step, b * GS + at[0])
                            alone(v)

                        def wide(t):
                            return t.rearrange("p (t o) -> p t o", o=1).to_broadcast([P, NT, E])

                        link(nc.vector.tensor_scalar(sig[:], gtmp[:, :, 0], 1.0, 0.5, ALU.add, ALU.mult))
                        link(nc.vector.reciprocal(gtmp[:, :, 1], gsum[:]))
                        link(nc.vector.tensor_tensor(gprob[:], gexp[:], wide(gtmp[:, :, 1]), ALU.mult))
                        for t in range(NT):
                            i = nc.vector.max(top8[:, t, :], gprob[:, t, :])
                        link(i)
                        for t in range(NT):
                            i = nc.vector.match_replace(grest[:, t, :], top8[:, t, :], gprob[:, t, :], -1.0)
                        link(i)
                        link(nc.vector.reduce_sum(gtmp[:, :, 2], top8[:], AX_X))
                        link(nc.vector.reciprocal(gtmp[:, :, 3], gtmp[:, :, 2]))
                        link(nc.vector.tensor_tensor(gprob[:], gprob[:], wide(gtmp[:, :, 3]), ALU.mult))
                        link(nc.vector.scalar_tensor_tensor(out=x2s[:, :, D:ROW], in0=grest[:], scalar=0.0, in1=gprob[:],
                                                            op0=ALU.is_lt, op1=ALU.mult))
                        for t in range(NT):
                            i = nc.vector.tensor_scalar(keyv[:, t % 2, t // 2, :], grest[:, t, :], 0.0, token_key[:, t:t + 1], ALU.is_lt, ALU.mult)
                        link(i)
                        nc.vector.tensor_scalar(token_key[:], token_key[:], -float(SEQ), None, ALU.add).then_inc(keyv_done, 1)
                        assert at[0] == GS, at
                    elif kind == "up":
                        v.wait_ge(tanh_done, b * (FS // P) + n + 1)
                        nc.vector.scalar_tensor_tensor(out=hid[:, n, :], in0=tnh[:, n % 2, :], scalar=1.0, in1=s_slot("up", n)[:, 0, :],
                                                       op0=ALU.add, op1=ALU.mult).then_inc(gated, 1)
                        v.wait_ge(gated, b * (FS // P) + n + 1)
                        nc.vector.scalar_tensor_tensor(out=hid[:, n, :], in0=hid[:, n, :], scalar=0.5, in1=s_slot("up", n)[:, 1, :],
                                                       op0=ALU.mult, op1=ALU.mult).then_inc(s_sem("up", n), 1)
                    elif kind == "down":
                        if n == 0:
                            v.wait_ge(batch_out, 1 + b)
                        g_written(v, b, "down", n)
                        for t in range(2):
                            tt = 2 * n + t
                            i = nc.vector.scalar_tensor_tensor(out=y0s[:, tt, :], in0=g_bank("down", n)[:, t * D:(t + 1) * D],
                                                               scalar=sig[:, tt:tt + 1], in1=x2s[:, tt, 0:D], op0=ALU.mult, op1=ALU.add)
                        i.then_inc(y0_done, 1)
                        v.wait_ge(y0_done, 2 * b + n + 1)
                        v.sem_inc(g_sem("down", n), 1)

            def search_all(src, dst, at):
                for r in range(CAP // 8):
                    search(src, dst, r, at)

            v.wait_ge(keys_in, 1 + B)
            v.wait_ge(kept, 1 + B)
            search_all(keys[:], found, B * ROUND_STEPS)
            v.wait_ge(moved, 32)
            search_all(both, first, (B + 1) * ROUND_STEPS)
            v.wait_ge(firstT, 1)
            nc.vector.tensor_scalar(idxf[:, 0, :], T[:, 0, 0:E], 0.0, slot_no[:], ALU.is_equal, ALU.mult).then_inc(idx_step, 1)
            nc.vector.tensor_scalar(idxf[:, 1, :], T[:, 0, 0:E], -1.0, float(TOK), ALU.mult, ALU.add).then_inc(idx_step, 1)
            v.wait_ge(idx_step, 2)
            nc.vector.tensor_tensor(idx[:], idxf[:, 0, :], idxf[:, 1, :], ALU.add).then_inc(idx_step, 1)
            v.wait_ge(idx_step, 3)
            nc.vector.tensor_copy(idx_gather[:], idx[:, 0:EU]).then_inc(idx0_done, 1)

            def hidden(r, s, first_turn):
                v.wait_ge(e_tanh, r * EU + s + 1)
                if s >= PU or not first_turn:
                    v.wait_ge(e_down, r * EU + s + 1 - PU)
                up = S[:, s % PU // 2, s % 2, 256:512]
                nc.vector.scalar_tensor_tensor(out=act[:, s % PU, :], in0=ath[:, s % PU, :], scalar=1.0, in1=up[:, 0:FI],
                                               op0=ALU.add, op1=ALU.mult).then_inc(e_act1, 1)
                v.wait_ge(e_act1, r * EU + s + 1)
                nc.vector.scalar_tensor_tensor(out=act[:, s % PU, :], in0=act[:, s % PU, :], scalar=0.5, in1=up[:, FI:2 * FI],
                                               op0=ALU.mult, op1=ALU.mult).then_inc(e_act, 1)

            def output(r, s, first_turn, last_turn):
                slot, n = s % EU, r * EU + s
                v.wait_ge(e_down, n + 1)
                if s >= PU or not first_turn:
                    v.wait_ge(y_add[(s - PU) % EU], 16 * (r + 1 if s >= PU else r))
                nc.vector.tensor_copy(idx_add[:, slot:slot + 1], idx[:, bass.ds(n, 1)])
                if not last_turn:
                    nc.vector.tensor_copy(idx_gather[:, slot:slot + 1], idx[:, bass.ds(n + EU, 1)])
                nc.vector.tensor_scalar(yo[:, s % PU, :], out_of(s)[:, 0:D], xg[:, slot, bass.ds(n + D, 1)], None,
                                        ALU.mult).then_inc(e_yo, 1)

            def experts(r, first_turn=False, last_turn=False):
                for s in range(EU):
                    if s >= 1 or not first_turn:
                        hidden(r, s - 1, first_turn)
                    if s >= 2 or not first_turn:
                        output(r, s - 2, first_turn, last_turn and s >= 2)

            experts(0, first_turn=True)
            with v.Fori(1, TURNS - 1) as r:
                experts(r)
            experts(TURNS - 1, last_turn=True)
            output(TURNS, -2, False, True)
            hidden(TURNS, -1, False)
            output(TURNS, -1, False, True)

            with v.Fori(0, B // 2) as k:
                for half in range(2):
                    v.wait_ge(f_in[half], 32 * (k + 1))
                    for t in range(2):
                        part = slice(2 * t, 2 * t + 2)
                        nc.vector.tensor_tensor(fin[half][:, part, :], fin[half][:, part, :], fin1[half][:, part, :],
                                                ALU.add).then_inc(res_done, 1)
                    layernorm(2 * B + 2 * k + half, fin[half])


_INS = ["x", "ctx_1024", "L0_attn_Wq", "L0_attn_bq", "L0_attn_Wk", "L0_attn_bk", "L0_attn_Wv", "L0_attn_bv",
        "L0_attn_Wo", "L0_attn_bo", "L0_xattn_W_Q", "L0_xattn_W_K", "L0_xattn_W_V", "L0_xattn_W_O",
        "L0_xattn_b_Q", "L0_xattn_b_K", "L0_xattn_b_V", "L0_xattn_b_O", "L0_ffn_gate_w", "L0_ffn_shared_gate_w",
        "L0_ffn_shared_gate_up_w", "L0_ffn_shared_down_w", "L0_ffn_expert_gate_up_w", "L0_ffn_expert_down_w"]


def kernel(**inputs):
    import numpy as _np
    import concourse.bacc as _bacc
    from concourse import mybir as _mybir
    from concourse.bass_utils import run_bass_kernel_spmd as _run

    nc = _bacc.Bacc("TRN2", target_bir_lowering=False, num_devices=1)
    arrays, args = {}, []
    for name in _INS:
        a = _np.ascontiguousarray(inputs[name])
        arrays[f"in_{name}_dram"] = a
        args.append(nc.dram_tensor(f"in_{name}_dram", a.shape, _mybir.dt.from_np(a.dtype), kind="ExternalInput").ap())
    out = nc.dram_tensor("out_0_dram", (B, SEQ, D), F32, kind="ExternalOutput").ap()
    build(nc, *args, out)
    r = _run(nc, [arrays], core_ids=[0])
    return r.results[0]["out_0_dram"]
```

```python
from contextlib import ExitStack

import concourse.bass as bass
from concourse import mybir

F32 = mybir.dt.float32
F32R = mybir.dt.float32r
BF16 = mybir.dt.bfloat16
U32 = mybir.dt.uint32
ALU = mybir.AluOpType
ACT = mybir.ActivationFunctionType
AX_X = mybir.AxisListType.X

P = 128
B, SEQ, D = 8, 512, 256
TOK = B * SEQ
NT = SEQ // P
DC = D // P
H = 16
UNITS = H // 2
HD1, KV1 = 16, 4
HD2 = 64
STEPS = UNITS * NT
E, TOPK, CAP = 64, 8, 128
FS = 512
FI = 128
ROW = D + E
NROW = TOK + CAP
EPS = 1e-5
MASKED = -1e30
YS = 2
EU = 8
EARLY = 4
AHEAD = 12
PU = 4
TURNS = E // EU
FB = 4


def self_attention_timeline():
    pairs = [(g, i) for g in range(KV1) for i in range(2 * NT)]
    order, later = [], []
    for m in range(AHEAD):
        order.append(("M", pairs[m]))
        if m % 3 == 1:
            order.append(("V2", m // 3))
        if m == 2 * NT:
            order.append(("NT", 0))
    for x, (g, i) in enumerate(pairs):
        if x + AHEAD < len(pairs):
            order.append(("M", pairs[x + AHEAD]))
            if pairs[x + AHEAD][1] == 2 * NT - 1:
                later.append((x + 2, ("NT", pairs[x + AHEAD][0])))
        order.append(("X", (g, i)))
        for due in [d for d in later if d[0] <= x]:
            order.append(due[1])
            later.remove(due)
        if i % 2 == 1:
            later.append((x + 2, ("PV1", (g, i // 2))))
        if i == 2 * NT - 1:
            later += [(x + 3, ("E1", g)), (x + 5, ("SM", g)), (x + 7, ("RS", g))]
    assert {event for _, event in later} == {("PV1", (KV1 - 1, NT - 1)), ("E1", KV1 - 1), ("SM", KV1 - 1), ("RS", KV1 - 1)}
    order += [("PV1", (KV1 - 1, NT - 1)), ("E1", KV1 - 1), ("V2", 4), ("SM", KV1 - 1), ("RS", KV1 - 1), ("V2", 5)]
    return order


CROSS = {"tensor": ("SKT", "SQT", "STV", "ST"),
         "scalar": ("TSK", "TSQ", "TSV", "TS"),
         "vector": ("SRTKp", "SRTQ", "SRTp", "SRT")}


BESIDE_STEPS = {STEPS: [("xT", 1), ("xT", 0)], STEPS + 1: [("cT", 1), ("cT", 0)]}


def cross_attention_timeline(engine):
    order = [("Q2", 0)]
    for n in range(STEPS + 3):
        u = n // NT
        order += BESIDE_STEPS.get(n, [])
        for letter in CROSS[engine][n % NT]:
            if letter == "S" and n < STEPS:
                order.append(("S2", n))
            if letter == "R" and 0 <= n - 1 < STEPS:
                order.append(("R2", n - 1))
            if letter == "T" and 0 <= n - 2 < STEPS:
                order.append(("T2", n - 2))
            if letter == "K" and 1 <= u < UNITS - 1:
                order.append(("K2", u + 1))
            if letter == "Q" and u < UNITS - 1:
                order.append(("Q2", u + 1))
            if letter == "V" and u >= 1:
                order.append(("PV2", u - 1))
            if letter == "p" and n < STEPS:
                order.append(("pick", EARLY + n // 2))
    return [event for event in order if event[0] != "pick" or event[1] < CAP // 8]


def head_timeline():
    return ([("xT", c) for c in range(DC)] + [("q1", c) for c in range(DC)] + [("k1", 0), ("v1", 0)] +
            [("cT", c) for c in range(DC)])


def batch_timeline(engine):
    t = self_attention_timeline()
    fill = [("V2", 6), ("V2", 7), ("K2", 0), ("K2", 1)]
    ln1 = [("ln1", 0), ("norm1", 0)]
    t += [("o1", i) for i in range(2)] + (ln1 + fill if engine == "vector" else fill + ln1)
    t += [("x1T", c) for c in range(DC)] + cross_attention_timeline(engine)
    t += [("o2", i) for i in range(2)] + [("ln2", 0)]
    head = [("q1", 0), ("q1", 1), ("k1", 0), ("v1", 0)]
    assert sorted(head + sum(BESIDE_STEPS.values(), [])) == sorted(head_timeline())
    if engine == "vector":
        head.insert(1, ("norm2", 0))
    else:
        head.append(("norm2", 0))
    t += head + [("x2T", c) for c in range(DC)]
    t += [("gate", 0), ("up", 0), ("up", 1), ("keys", 0), ("pick", 0), ("up", 2), ("pick", 1), ("up", 3), ("pick", 2)]
    t += [("down", 0), ("pick", 3), ("down", 1)]
    return t


USES = {"xT": ["xT"], "q1": ["q1"], "k1": ["k1"], "v1": ["v1"], "cT": ["cT"], "V2": ["V2"], "NT": ["nt"],
        "SM": ["sm"], "RS": ["rs"],
        "o1": ["o1"], "x1T": ["x1T"], "Q2": ["q2"], "K2": ["k2"], "PV2": ["PV2"], "o2": ["o2"], "x2T": ["x2T"],
        "gate": ["gate"], "keys": ["keys"], "down": ["down"]}


def build(nc, x, ctx, Wq1, bq1, Wk1, bk1, Wv1, bv1, Wo1, bo1, WQ, WK, WV, WO, bQ, bK, bV, bO,
          gate_w, sgate_w, sup_w, sdown_w, eup_w, edown_w, out):
    order = batch_timeline("tensor")
    head = head_timeline()
    g_first = {}
    for kind, n in head:
        for use in USES[kind]:
            g_first[use, n] = len(g_first)
    G0 = len(g_first)
    g_index = {}
    for kind, n in order:
        for use in USES.get(kind, []):
            g_index[use, n] = len(g_index)
    NG = len(g_index)
    assert NG % 2 == 0 and G0 % 2 == 0 and all((g_first[use] - g_index[use]) % 2 == 0 for use in g_first)
    s_index = {}
    for kind, n in order:
        if kind in ("M", "X", "S2", "up"):
            s_index[kind, n] = len(s_index)
    NS = len(s_index)
    HI_PARTS = ("q1", "k1", "K2", "Q2")
    hi_first = {event: i for i, event in enumerate([event for event in head if event[0] in HI_PARTS])}
    hi_index = {event: i for i, event in enumerate([event for event in batch_timeline("scalar") if event[0] in HI_PARTS])}
    assert NS % 2 == 0

    with ExitStack() as stack:
        def sb(name, shape, dt=F32):
            return stack.enter_context(nc.sbuf_tensor(name, shape, dt))

        def psum(name, shape, dt=F32):
            return stack.enter_context(nc.psum_tensor(name, shape, dt))

        def sem(name):
            return stack.enter_context(nc.semaphore(name))

        q_parts = nc.dram_tensor("q_parts", (2, H * HD1, SEQ), F32).ap()
        k_parts = nc.dram_tensor("k_parts", (2, KV1 * HD1, SEQ), F32).ap()
        table = nc.dram_tensor("token_table", (NROW, ROW), F32).ap()
        sums = [nc.dram_tensor(f"sum_{i}", (NROW, D), F32).ap() for i in range(YS)]

        S = psum("S", [P, 2, 2, 512])
        T = psum("T", [P, 2, 512])
        G = psum("G", [P, 2, 512])

        ident = sb("ident", [P, P])
        identb = sb("identb", [P, P], BF16)
        maskb = sb("maskb", [P, P], BF16)
        wq1 = sb("wq1", [P, DC, H * HD1])
        wk1 = sb("wk1", [P, DC, KV1 * HD1])
        wv1 = sb("wv1", [P, DC, KV1 * HD1])
        wo1 = sb("wo1", [P, KV1, D])
        wq2 = sb("wq2", [P, DC, H * HD2])
        wk2 = sb("wk2", [P, DC, H * HD2])
        wv2 = sb("wv2", [P, DC, H * HD2])
        wo2 = sb("wo2", [P, UNITS, D])
        gw = sb("gw", [P, DC, E + 1])
        supw = sb("supw", [P, DC, 2 * FS])
        sdownw = sb("sdownw", [P, FS // P, D])
        bq1c = sb("bq1c", [P, DC])
        bk1c = sb("bk1c", [KV1 * HD1, 1])
        bv1r = sb("bv1r", [P, KV1 * HD1])
        bqc = sb("bqc", [P, UNITS])
        bkc = sb("bkc", [P, UNITS])
        bvc = sb("bvc", [P, UNITS])
        bo1r = sb("bo1r", [P, D])
        bo2r = sb("bo2r", [P, D])
        token_key = sb("token_key", [P, NT])
        slot_no = sb("slot_no", [P, 1])
        turned = sb("turned", [P, P])
        sum_rows = sb("sum_rows", [P, 4])

        xs = sb("xs", [P, NT, D])
        cs = sb("cs", [P, NT, D])
        xT = sb("xT", [P, DC, SEQ])
        cT = sb("cT", [P, DC, SEQ])
        x1s = sb("x1s", [P, NT, D])
        x2s = sb("x2s", [P, NT, ROW])
        parts = sb("parts", [P, 2, 2, SEQ], F32R)
        q1st = sb("q1st", [P, 4, SEQ], F32R)
        k1st = sb("k1st", [P, KV1, SEQ], F32R)
        k2z = sb("k2z", [P, 2, 2, 2, SEQ], F32R)
        q_slots = [q1st[:, :, :], parts[:, :, :, :].rearrange("p a b n -> p (a b) n"),
                   k2z[:, 0, :, :, :].rearrange("p a b n -> p (a b) n")]
        KQ = 4 * HD1 + 1
        v1s = sb("v1s", [P, NT, KV1, 32])
        v2s = sb("v2s", [P, NT, H * HD2])
        k1parts = v2s[0:KV1 * HD1, 0, :].rearrange("p (s n) -> p s n", s=2).bitcast(F32R)
        negmax1 = sb("negmax1", [P, 2, 4, NT])
        negrow = sb("negrow", [4 * NT, P], F32R)
        rsum1 = sb("rsum1", [P, 4 * NT])
        probs = sb("probs", [P, 3, 2, SEQ])
        rwide = probs[:, 0, 0, :]
        pT = sb("pT", [P, 2, 2, NT, SEQ])
        p1 = pT[:, :, :, :, :].rearrange("p a b k n -> p (a b k) n").rearrange("p (k h) n -> p k h n", k=NT)
        zT = sb("zT", [P, UNITS, SEQ])
        stats = sb("stats", [P, NT, 6])
        mv = sb("mv", [P, NT, 2])
        varps = sb("varps", [P, NT])
        minus_half = sb("minus_half", [P, NT])
        rstd = sb("rstd", [P, NT])
        negmax = sb("negmax", [P, 4, 2])
        rowsum = sb("rowsum", [P, 4, 2])
        rrow = sb("rrow", [P, 4, 2])
        gneg = sb("gneg", [P, NT])
        gsum = sb("gsum", [P, NT])
        gexp = probs[:, 0, 0, 0:NT * E].rearrange("p (t e) -> p t e", t=NT)
        gprob = probs[:, 0, 1, 0:NT * E].rearrange("p (t e) -> p t e", t=NT)
        grest = probs[:, 1, 0, 0:NT * E].rearrange("p (t e) -> p t e", t=NT)
        keyv = probs[:, 1, 1, 0:NT * E].rearrange("p (t h e) -> p t h e", t=2, h=2)
        top8 = sb("top8", [P, NT, TOPK])
        gtmp = sb("gtmp", [P, NT, 4])
        sig = sb("sig", [P, NT])
        keys = sb("keys", [P, CAP + SEQ // 2])
        found = sb("found", [P, CAP])
        hid = pT[:, 0, 0, :, :]
        tnh = pT[:, 0, 1, 0:2, :]
        y0s = pT[:, 0, 1, 2:4, :].rearrange("p a (b n) -> p (a b) n", b=2)

        found_rows = v2s[:, 3, 0:P]
        first = v2s[:, 3, P:P + E]
        idxf = v2s[:, 3, 2 * P:2 * P + 2 * E].rearrange("p (a e) -> p a e", a=2)
        idx = sb("idx", [P, E], U32)
        idx_gather = sb("idx_gather", [P, EU], U32)
        idx_add = sb("idx_add", [P, EU], U32)
        xg = v2s[:, :, :].rearrange("p a n -> p (a n)")[:, 0:EU * ROW].rearrange("p (s n) -> p s n", s=EU)
        wup = zT[:, :, :].rearrange("p u n -> p (u n)").rearrange("p (s c n) -> p s c n", s=EU, c=DC)
        wdn = pT[:, 1, 0, :, :].rearrange("p a (b n) -> p (a b) n", b=2)
        xgT = pT[:, 1, 1, 0:2, :].rearrange("p a (s n) -> p (a s) n", s=2)
        act = pT[:, 1, 1, 2, :].rearrange("p (s n) -> p s n", s=PU)
        ath = probs[:, 0, 0, :].rearrange("p (s n) -> p s n", s=PU)
        yo = xT[:, :, :].rearrange("p c (b n) -> p (c b) n", b=2)
        fin = [pT[:, 0, i // 2, i % 2 * 2:i % 2 * 2 + 2, :].rearrange("p a (b n) -> p (a b) n", b=2) for i in range(FB)]
        fin1 = [pT[:, 1, i // 2, i % 2 * 2:i % 2 * 2 + 2, :].rearrange("p a (b n) -> p (a b) n", b=2) for i in range(FB)]
        zero = sb("zero", [P, SEQ])
        zero_row = zero[0:1, :].rearrange("p (o n) -> p o n", o=1).to_broadcast([1, 4, SEQ])

        w_head = sem("w_head")
        w_values = sem("w_values")
        w_cross = sem("w_cross")
        w_ffn = sem("w_ffn")
        passed = sem("passed")
        x_in = sem("x_in")
        c_in = sem("c_in")
        consts = sem("consts")
        id_zero = sem("id_zero")
        id_done = sem("id_done")
        v1_done = sem("v1_done")
        ones_done = sem("ones_done")
        wprep = sem("wprep")
        g_ready = sem("g_ready")
        g_done = [sem("g_done0"), sem("g_done1")]
        hi_done = sem("hi_done")
        base1 = sem("base1")
        base2 = sem("base2")
        parts_out = sem("parts_out")
        kparts_out = sem("kparts_out")
        k1_in = sem("k1_in")
        q1_in = [sem(f"q1_in{i}") for i in range(3)]
        nm_in = [sem(f"nm_in{i}") for i in range(3)]
        zero_in = sem("zero_in")
        z_copied = sem("z_copied")
        rsum1_done = sem("rsum1_done")
        z_divided = sem("z_divided")
        z_ready = sem("z_ready")
        s_ready = sem("s_ready")
        s_done = [[sem(f"s_done{slot}{bank}") for bank in range(2)] for slot in range(2)]
        nm_ready = sem("nm_ready")
        rr_ready = sem("rr_ready")
        pn_ready = sem("pn_ready")
        t_ready = sem("t_ready")
        pt_ready = sem("pt_ready")
        res_done = sem("res_done")
        st_done = sem("st_done")
        ag_done = sem("ag_done")
        ve_done = sem("ve_done")
        rs_done = sem("rs_done")
        ln_done = sem("ln_done")
        gmax_done = sem("gmax_done")
        gate_step = sem("gate_step")
        keyv_done = sem("keyv_done")
        tanh_done = sem("tanh_done")
        gated = sem("gated")
        table_out = sem("table_out")
        keys_in = sem("keys_in")
        y0_done = sem("y0_done")
        y0_out = sem("y0_out")
        batch_out = sem("batch_out")
        zero_out = sem("zero_out")
        pick = sem("pick")
        kept = sem("kept")
        found_copied = sem("found_copied")
        found_turned = sem("found_turned")
        firstT = sem("firstT")
        idx_step = sem("idx_step")
        idx0_done = sem("idx0_done")
        xg_in = [sem(f"xg_in{i}") for i in range(EU)]
        we_in = [sem(f"we_in{i}") for i in range(EU)]
        e_tr = sem("e_tr")
        e_trs = sem("e_trs")
        e_up = sem("e_up")
        e_tanh = sem("e_tanh")
        e_act1 = sem("e_act1")
        e_act = sem("e_act")
        e_down = sem("e_down")
        e_yo = sem("e_yo")
        y_add = [sem(f"y_add{i}") for i in range(EU)]
        f_in = [sem(f"f_in{i}") for i in range(FB)]
        f_out = [sem(f"f_out{i}") for i in range(FB)]

        FIRST = None

        def g_uses(b, use, n):
            return g_first[use, n] + 1 if b is FIRST else G0 + b * NG + g_index[use, n] + 1

        def g_done_count(b, k):
            return 1 + k // 2 + 1 if b is FIRST else 1 + (G0 // 2) + b * (NG // 2) + k // 2 + 1

        def g_written(eng, b, use, n):
            eng.wait_ge(g_ready, g_uses(b, use, n))

        def head_no(b):
            return 0 if b is FIRST else b + 1

        def g_landed(eng, b, use, n):
            g = (g_first if b is FIRST else g_index)[use, n]
            eng.wait_ge(g_done[g % 2], g_done_count(b, g))

        def g_bank(use, n):
            return G[:, g_index[use, n] % 2, :]

        def g_sem(use, n):
            return g_done[g_index[use, n] % 2]

        def s_written(eng, b, kind, n, bank=1):
            eng.wait_ge(s_ready, 2 * (b * NS + s_index[kind, n]) + bank + 1)

        def s_landed(eng, b, *steps):
            need = {}
            for step in steps:
                k = s_index[step]
                need[k % 2] = max(need.get(k % 2, 0), k // 2 + 1)
            for k, count in sorted(need.items()):
                eng.wait_ge(s_done[k][1], 1 + b * (NS // 2) + count)

        def s_slot(kind, n):
            return S[:, s_index[kind, n] % 2, :, :]

        def s_sem(kind, n, bank):
            return s_done[s_index[kind, n] % 2][bank]

        def alone(eng):
            eng.sem_inc(passed, 1)

        def out_of(s):
            return [T, G][s % PU // 2][:, s % 2, :]

        CONSTS = 14
        W_CROSS = 13
        ROUND_STEPS = 2 * CAP // 8

        def step_no(b, n):
            return b * STEPS + n

        def turn(eng, copy, b, n):
            u, qt = n // NT, n % NT
            nk = qt + 1
            eng.wait_ge(t_ready, step_no(b, n) + 1)
            if u >= 2:
                g_written(eng, b, "PV2", u - 2)
            copy(pT[:, u % 2, :, 0:nk, qt * P:(qt + 1) * P],
                 T[:, :, 0:nk * P].rearrange("p j (k n) -> p j k n", k=nk)).then_inc(pt_ready, 1)

        block = stack.enter_context(nc.Block())

        @block.sync
        def _(sp):
            for dst, src in (
                    (wq1[:], Wq1.rearrange("(c p) n -> p c n", p=P)),
                    (bq1c[:], bq1.rearrange("(c p) -> p c", p=P)),
                    (wk1[:], Wk1.rearrange("(c p) n -> p c n", p=P)),
                    (bk1c[:], bk1.rearrange("(p o) -> p o", o=1)),
                    (wv1[:], Wv1.rearrange("(c p) n -> p c n", p=P)),
                    (bv1r[:], bv1.rearrange("(o n) -> o n", o=1).to_broadcast([P, KV1 * HD1])),
                    (bo1r[:], bo1.rearrange("(o n) -> o n", o=1).to_broadcast([P, D]))):
                sp.dma_start(dst, src, allow_slow_non_contiguous=True).then_inc(w_head, 16)

            def load_inputs(batch):
                sp.dma_start(xs[:], x[batch].rearrange("o (t p) d -> p (o t) d", p=P)).then_inc(x_in, 16)
                sp.dma_start(cs[:], ctx[batch].rearrange("o (t p) d -> p (o t) d", p=P)).then_inc(c_in, 16)

            def load_group(g):
                dst = q_slots[g % 3]
                for blk, part in enumerate((0, 1, 0, 1)):
                    sp.dma_start(dst[blk * HD1:(blk + 1) * HD1, :, :].bitcast(F32),
                                 q_parts[part, 4 * g * HD1:4 * (g + 1) * HD1, :].rearrange("(h d) n -> d h n", d=HD1)
                                 ).then_inc(q1_in[g % 3], 16)
                sp.dma_start(dst[KQ - 1:KQ, :, :].bitcast(F32), zero_row[:, :, :]).then_inc(q1_in[g % 3], 16)

            def spread_parts(b):
                for c in range(DC):
                    g_landed(sp, b, "q1", c)
                    for part in range(2):
                        sp.dma_start(q_parts[part, c * P:(c + 1) * P, :], parts[:, c, part, :].bitcast(F32)).then_inc(parts_out, 16)
                g_landed(sp, b, "k1", 0)
                sp.dma_start(k_parts.rearrange("s r n -> r s n"), k1parts.bitcast(F32)).then_inc(kparts_out, 16)
                sp.wait_ge(kparts_out, 16 * (head_no(b) + 1))
                for blk, part in enumerate((0, 0, 1, 1)):
                    sp.dma_start(k1st[blk * HD1:(blk + 1) * HD1, :, :].bitcast(F32),
                                 k_parts[part].rearrange("(h d) n -> d h n", d=HD1)).then_inc(k1_in, 16)
                sp.wait_ge(parts_out, 1 + 64 * (head_no(b) + 1))
                for g in range(3):
                    load_group(g)
                for c in range(DC):
                    g_written(sp, b, "cT", c)
                    alone(sp)
                sp.wait_ge(base1, 1 + head_no(b) + 1)
                alone(sp)

            def place_maxima(b, g):
                g_landed(sp, b, "nt", g)
                sp.dma_start(q_slots[g % 3][KQ - 1:KQ, :, :].bitcast(F32),
                             negrow[:].bitcast(F32)).then_inc(nm_in[g % 3], 16)

            load_inputs(slice(0, 1))
            sp.wait_ge(consts, CONSTS)
            sp.wait_ge(ones_done, 4)
            spread_parts(FIRST)
            with sp.Fori(0, B) as b:
                load_inputs(bass.ds((b + 1) % B, 1))
                place_maxima(b, 0)
                place_maxima(b, 1)
                s_written(sp, b, "X", (0, 2 * NT - 1))
                load_group(3)
                place_maxima(b, 2)
                place_maxima(b, 3)
                s_written(sp, b, "X", (2, 2 * NT - 1))
                sp.dma_start(q_slots[2][KQ - 1:KQ, :, :].bitcast(F32), zero_row[:, :, :]).then_inc(zero_in, 16)
                spread_parts(b)

            def weights(r, first_turn=False):
                for s in range(EU):
                    n = r * EU + s
                    if not first_turn:
                        sp.wait_ge(e_down, n + 1 - EU)
                    sp.dma_start(wup[:, s, :, :], eup_w[bass.ds(n, 1)].rearrange("o (c p) n -> p (o c) n", p=P)).then_inc(we_in[s], 16)
                    sp.dma_start(wdn[:, s, :], edown_w[bass.ds(n, 1)].rearrange("o p n -> p (o n)")).then_inc(we_in[s], 16)

            sp.wait_ge(k1_in, 64 * (B + 1))
            for g in range(3):
                sp.wait_ge(q1_in[g], 80 * (2 * B + 1 if g == 0 else B + 1))
            g_landed(sp, B - 1, "down", 1)
            sp.wait_ge(batch_out, 1 + B)
            weights(0, first_turn=True)
            with sp.Fori(1, TURNS) as r:
                weights(r)
            for s in range(EU):
                sp.wait_ge(y_add[s], 16 * TURNS)

            def load_sums(k, part):
                rows = bass.ds((FB * k + part) * SEQ, SEQ)
                for dst, src in ((fin, sums[0]), (fin1, sums[1])):
                    sp.dma_start(dst[part], src[rows, :].rearrange("(t p) n -> p t n", p=P)).then_inc(f_in[part], 16)

            for part in range(FB):
                load_sums(0, part)

            def store_results(k):
                for part in range(FB):
                    sp.wait_ge(ln_done, NT * (2 * B + FB * k + part + 1))
                    sp.dma_start(out[bass.ds(FB * k + part, 1)].rearrange("o (t p) d -> p (o t) d", p=P), fin[part]).then_inc(f_out[part], 16)

            with sp.Fori(0, B // FB - 1) as k:
                store_results(k)
                for part in range(FB):
                    sp.wait_ge(f_out[part], 16 * (k + 1))
                    load_sums(k + 1, part)
            store_results(B // FB - 1)
            for part in range(FB):
                sp.wait_ge(f_out[part], 16 * (B // FB))

        start_at_1 = [base1, *g_done, *s_done[0], *s_done[1], pt_ready, parts_out, batch_out, keyv_done, keys_in, kept, pick]

        @block.gpsimd
        def _(pool):
            for counted in start_at_1:
                pool.sem_inc(counted, 1)
            nc.gpsimd.memset(ident[:], 0.0).then_inc(id_zero, 1)
            pool.wait_ge(id_zero, 1)
            nc.gpsimd.affine_select(out=ident[:], in_=ident[:], compare_op=ALU.not_equal, fill=1.0, base=0,
                                    pattern=[[-1, P]], channel_multiplier=1).then_inc(id_done, 1)
            nc.gpsimd.memset(wo1[:], 0.0).then_inc(id_zero, 1)
            nc.gpsimd.memset(v1s[:], 0.0).then_inc(id_zero, 1)
            pool.wait_ge(id_zero, 3)
            nc.gpsimd.memset(v1s[:, :, :, HD1:HD1 + 1], 1.0).then_inc(v1_done, 1)
            pool.wait_ge(w_head, 16 * 7)
            nc.gpsimd.tensor_scalar(wq1[:], wq1[:], HD1 ** -0.5, None, ALU.mult).then_inc(wprep, 1)
            nc.gpsimd.tensor_scalar(bq1c[:], bq1c[:], HD1 ** -0.5, None, ALU.mult).then_inc(wprep, 1)
            nc.gpsimd.memset(zero[:], 0.0).then_inc(consts, 1)
            nc.gpsimd.memset(k2z[:].bitcast(F32), 0.0).then_inc(consts, 1)
            nc.gpsimd.memset(maskb[:], 0.0).then_inc(consts, 1)
            nc.gpsimd.memset(minus_half[:], -0.5).then_inc(consts, 1)
            nc.gpsimd.memset(sum_rows[:], 0.0).then_inc(consts, 1)
            nc.gpsimd.memset(keys[:], 0.0).then_inc(consts, 1)
            nc.gpsimd.memset(found[:], 0.0).then_inc(consts, 1)
            nc.gpsimd.memset(turned[:], 0.0).then_inc(consts, 1)
            pool.wait_ge(consts, 8)
            nc.gpsimd.affine_select(out=sum_rows[:], in_=sum_rows[:], compare_op=ALU.not_equal, fill=1.0, base=-HD1,
                                    pattern=[[-32, 4]], channel_multiplier=1).then_inc(consts, 1)
            nc.gpsimd.affine_select(out=turned[:], in_=turned[:], compare_op=ALU.not_equal, fill=1.0, base=1 - P,
                                    pattern=[[1, P]], channel_multiplier=1).then_inc(consts, 1)
            nc.gpsimd.iota(token_key[:], pattern=[[-P, NT]], base=TOK, channel_multiplier=-1,
                           allow_small_or_imprecise_dtypes=True).then_inc(consts, 1)
            nc.gpsimd.iota(slot_no[:], pattern=[[0, 1]], base=0, channel_multiplier=1,
                           allow_small_or_imprecise_dtypes=True).then_inc(consts, 1)
            nc.gpsimd.affine_select(out=maskb[:], in_=maskb[:], compare_op=ALU.is_ge, fill=MASKED, base=0,
                                    pattern=[[-1, P]], channel_multiplier=1).then_inc(consts, 1)
            pool.wait_ge(id_done, 1)
            nc.gpsimd.tensor_copy(identb[:], ident[:]).then_inc(consts, 1)

            def residual1(b):
                pool.wait_ge(x_in, 16 * (head_no(b) + 1))
                if b is not FIRST:
                    g_written(pool, b, "x1T", 1)
                nc.gpsimd.tensor_tensor(x1s[:], xs[:], bo1r[:].rearrange("p (o n) -> p o n", o=1).to_broadcast([P, NT, D]),
                                        ALU.add).then_inc(base1, 1)

            residual1(FIRST)
            pool.wait_ge(w_cross, 16 * W_CROSS)
            nc.gpsimd.tensor_scalar(bqc[:], bqc[:], HD2 ** -0.5, None, ALU.mult).then_inc(wprep, 1)
            nc.gpsimd.tensor_scalar(wq2[:], wq2[:], HD2 ** -0.5, None, ALU.mult).then_inc(wprep, 1)
            for i in range(4):
                pool.dma_start(sums[1][i * 1024:(i + 1) * 1024, :].rearrange("(a p) n -> p a n", p=P),
                               zero[:, 0:D].rearrange("p (o n) -> p o n", o=1).to_broadcast([P, 8, D])).then_inc(zero_out, 16)
            for i in range(2):
                pool.dma_start(sums[i][TOK:NROW, :], zero[:, 0:D]).then_inc(zero_out, 16)
            pool.dma_start(table[TOK:NROW, :], zero[:, 0:ROW]).then_inc(zero_out, 16)

            def inverse_deviation(k):
                pool.wait_ge(ag_done, NT * (k + 1))
                alone(pool)
                nc.gpsimd.tensor_scalar(varps[:], mv[:, :, 1], EPS, None, ALU.add).then_inc(ve_done, 1)
                pool.wait_ge(ve_done, k + 1)
                nc.gpsimd.tensor_tensor(rstd[:], varps[:], minus_half[:], ALU.pow).then_inc(rs_done, 1)

            with pool.Fori(0, B) as b:
                for kind, n in order:
                    if kind == "ln1":
                        inverse_deviation(2 * b)
                    elif kind == "ln2":
                        inverse_deviation(2 * b + 1)
                    if kind == "k1":
                        residual1(b)
                    elif kind == "ln1":
                        pool.wait_ge(ln_done, (2 * b + 1) * NT)
                        nc.gpsimd.tensor_tensor(x2s[:, :, 0:D], x1s[:], bo2r[:].rearrange("p (o n) -> p o n", o=1).to_broadcast([P, NT, D]),
                                                ALU.add).then_inc(base2, 1)
                    elif kind == "keys":
                        pool.wait_ge(keyv_done, 1 + b + 1)
                        pool.dma_start(table[bass.ds(b * SEQ, SEQ), :].rearrange("(t p) n -> p t n", p=P), x2s[:]).then_inc(table_out, 16)
                    elif kind == "down" and n == 1:
                        pool.wait_ge(y0_done, 2 * (b + 1))
                        pool.dma_start(sums[0][bass.ds(b * SEQ, SEQ), :].rearrange("(t p) n -> p t n", p=P), y0s).then_inc(y0_out, 16)
                        for stored in (table_out, y0_out):
                            pool.wait_ge(stored, 16 * (b + 1))
                        pool.sem_inc(batch_out, 1)

            pool.wait_ge(zero_out, 16 * 7)
            def gather(s):
                alone(pool)
                pool.indirect_dma_start(out=xg[:, s, :], out_offset=None, in_=table,
                                        in_offset=bass.IndirectOffsetOnAxis(ap=idx_gather[:, s:s + 1], axis=0)).then_inc(xg_in[s], 16)

            def add_and_gather(r, first_turn=False, last_turn=False):
                for s in range(EU):
                    pool.wait_ge(e_yo, r * EU + s + 1)
                    if s >= YS:
                        pool.wait_ge(y_add[s - YS], 16 * (r + 1))
                    elif not first_turn:
                        pool.wait_ge(y_add[s - YS], 16 * r)
                    alone(pool)
                    pool.indirect_dma_start(out=sums[s % YS], out_offset=bass.IndirectOffsetOnAxis(ap=idx_add[:, s:s + 1], axis=0),
                                            in_=yo[:, s % PU, :], in_offset=None, compute_op=ALU.add).then_inc(y_add[s], 16)
                    if not last_turn:
                        gather(s)

            pool.wait_ge(idx0_done, 1)
            pool.wait_ge(kparts_out, 16 * (B + 1))
            for s in range(EU):
                gather(s)
            add_and_gather(0, first_turn=True)
            with pool.Fori(1, TURNS - 1) as r:
                add_and_gather(r)
            add_and_gather(TURNS - 1, last_turn=True)
            with pool.Fori(0, B) as b:
                inverse_deviation(2 * B + b)

        @block.tensor
        def _(pe):
            pe.wait_ge(id_done, 1)
            pe.wait_ge(wprep, 2)

            def bank(b, use, n, *results):
                index = g_first if b is FIRST else g_index
                g = index[use, n]
                need = {g % 2: g - 2}
                for r in results:
                    need[index[r] % 2] = max(need.get(index[r] % 2, -2), index[r])
                for parity, k in sorted(need.items()):
                    if b is not FIRST or k >= 0:
                        pe.wait_ge(g_done[parity], g_done_count(b, k))
                return G[:, g % 2, :]

            def transposed(b, use, c, src):
                dst = bank(b, use, c)
                for t in range(NT):
                    i = nc.tensor.transpose(dst[:, t * P:(t + 1) * P], src[:, t, c * P:(c + 1) * P], ident[:])
                i.then_inc(g_ready, 1)

            def product(dst, lhs, rhs):
                n = len(lhs)
                for i, (a, m) in enumerate(zip(lhs, rhs)):
                    last = nc.tensor.matmul(dst, a, m, start=(i == 0), stop=(i == n - 1))
                return last

            def scores(b, kind, n, bank):
                k = s_index[kind, n]
                pe.wait_ge(s_done[k % 2][bank], 1 + b * (NS // 2) + k // 2)
                return S[:, k % 2, bank, :]

            def head_part(b, kind, n):
                if kind == "xT":
                    pe.wait_ge(x_in, 16 * (head_no(b) + 1))
                    transposed(b, "xT", n, xs)
                elif kind == "cT":
                    pe.wait_ge(c_in, 16 * (head_no(b) + 1))
                    transposed(b, "cT", n, cs)
                elif kind == "q1":
                    product(bank(b, "q1", n, ("xT", 0), ("xT", 1)), [wq1[:, c, n * P:(n + 1) * P] for c in range(DC)],
                            [xT[:, c, :] for c in range(DC)]).then_inc(g_ready, 1)
                elif kind == "k1":
                    product(bank(b, "k1", 0)[0:KV1 * HD1, :], [wk1[:, c, :] for c in range(DC)],
                            [xT[:, c, :] for c in range(DC)]).then_inc(g_ready, 1)
                elif kind == "v1":
                    dst = bank(b, "v1", 0)
                    for t in range(NT):
                        i = product(dst[:, t * 64:(t + 1) * 64], [xT[:, c, t * P:(t + 1) * P] for c in range(DC)],
                                    [wv1[:, c, :] for c in range(DC)])
                    i.then_inc(g_ready, 1)

            for kind, n in head:
                head_part(FIRST, kind, n)
            for c in range(DC):
                g_landed(pe, FIRST, "cT", c)
            pe.wait_ge(consts, CONSTS)
            pe.wait_ge(ones_done, 4)
            with pe.Fori(0, B) as b:
                for kind, n in order:
                    if (kind, n) in head:
                        head_part(b, kind, n)
                    elif kind == "V2":
                        t, half = n // 2, n % 2
                        if n == 0:
                            pe.wait_ge(w_values, 16 * DC)
                        product(bank(b, "V2", n), [cT[:, c, t * P:(t + 1) * P] for c in range(DC)],
                                [wv2[:, c, half * 512:(half + 1) * 512] for c in range(DC)]).then_inc(g_ready, 1)
                    elif kind == "M":
                        g, i = n
                        if n == (0, 0):
                            pe.wait_ge(k1_in, 64 * (b + 1))
                        if i == 0:
                            pe.wait_ge(q1_in[g % 3], 80 * (b * (2 if g % 3 == 0 else 1) + g // 3 + 1))
                        for j in range(2):
                            nc.tensor.matmul(scores(b, "M", n, j), q_slots[g % 3][:, 2 * (i % 2) + j, (i // 2) * P:(i // 2 + 1) * P],
                                             k1st[:, g, :], start=True, stop=True).then_inc(s_ready, 1)
                    elif kind == "NT":
                        s_landed(pe, b, ("M", (n, 2 * NT - 1)))
                        dst = bank(b, "nt", n)
                        alone(pe)
                        nc.tensor.transpose(dst[0:4 * NT, 0:P], negmax1[:, n % 2, :, :].rearrange("p h t -> p (h t)"), ident[:]).then_inc(g_ready, 1)
                    elif kind == "X":
                        g, i = n
                        if i == 0:
                            pe.wait_ge(nm_in[g % 3], 16 * (b * (2 if g % 3 == 0 else 1) + g // 3 + 1))
                        for j in range(2):
                            nc.tensor.matmul(scores(b, "X", n, j), k1st[:, g, (i // 2) * P:(i // 2 + 1) * P],
                                             q_slots[g % 3][:, 2 * (i % 2) + j, :], start=True, stop=True).then_inc(s_ready, 1)
                    elif kind == "PV1":
                        g, kt = n
                        s_landed(pe, b, ("X", (g, 2 * kt)), ("X", (g, 2 * kt + 1)))
                        if kt == 0 and g >= 2:
                            pe.wait_ge(z_copied, b * KV1 + g - 1)
                        for h in range(4):
                            at = nc.tensor.matmul(T[32 * h:32 * h + 32, g % 2, :], v1s[:, kt, g, :], p1[:, kt, h, :],
                                                  start=(kt == 0), stop=(kt == NT - 1), skip_group_check=True)
                        if kt == NT - 1:
                            at.then_inc(z_ready, 1)
                    elif kind == "SM":
                        pe.wait_ge(z_copied, b * KV1 + n + 1)
                        dst = bank(b, "sm", n)
                        for t in range(NT):
                            at = nc.tensor.matmul(dst[:, 4 * t:4 * t + 4], zT[:, n, t * P:(t + 1) * P], sum_rows[:], start=True, stop=True)
                        at.then_inc(g_ready, 1)
                    elif kind == "RS":
                        dst = bank(b, "rs", n, ("sm", n))
                        for t in range(NT):
                            at = nc.tensor.matmul(dst[:, t * P:(t + 1) * P],
                                                  rwide[:, t * P:(t + 1) * P],
                                                  ident[:], start=True, stop=True)
                        at.then_inc(g_ready, 1)
                    elif kind in ("o1", "o2"):
                        w, chunks = (wo1, KV1) if kind == "o1" else (wo2, UNITS)
                        if kind == "o1":
                            if n == 0:
                                pe.wait_ge(w_cross, 16 * W_CROSS)
                            pe.wait_ge(z_divided, KV1 * (b + 1))
                            dst = bank(b, "o1", n)
                        else:
                            dst = bank(b, "o2", n, *(("PV2", u) for u in range(UNITS)))
                        for t in range(2):
                            tt = 2 * n + t
                            i = product(dst[:, t * D:(t + 1) * D], [zT[:, u, tt * P:(tt + 1) * P] for u in range(chunks)],
                                        [w[:, u, :] for u in range(chunks)])
                        i.then_inc(g_ready, 1)
                    elif kind == "x1T":
                        pe.wait_ge(ln_done, (2 * b + 1) * NT)
                        transposed(b, "x1T", n, x1s)
                    elif kind == "Q2":
                        if n == 0:
                            pe.wait_ge(wprep, 4)
                        product(bank(b, "q2", n, ("x1T", 0), ("x1T", 1)), [wq2[:, c, n * P:(n + 1) * P] for c in range(DC)],
                                [xT[:, c, :] for c in range(DC)]).then_inc(g_ready, 1)
                    elif kind == "K2":
                        if n == 0:
                            pe.wait_ge(w_cross, 16 * W_CROSS)
                        product(bank(b, "k2", n), [wk2[:, c, n * P:(n + 1) * P] for c in range(DC)],
                                [cT[:, c, :] for c in range(DC)]).then_inc(g_ready, 1)
                    elif kind == "S2":
                        u, qt = n // NT, n % NT
                        w = (qt + 1) * P
                        if qt == 0:
                            g_landed(pe, b, "q2", u)
                            g_landed(pe, b, "k2", u)
                        if n == 0:
                            pe.wait_ge(zero_in, 16 * (b + 1))
                        for j in range(2):
                            bank2 = scores(b, "S2", n, j)
                            dst = bank2[:, 0:w]
                            hi = parts[:, u % 2, 0, qt * P:(qt + 1) * P]
                            lo = parts[:, u % 2, 1, qt * P:(qt + 1) * P]
                            nc.tensor.matmul(dst, hi, k2z[:, j, u % 2, 0, 0:w], start=True, stop=False)
                            nc.tensor.matmul(dst, lo, k2z[:, j, u % 2, 0, 0:w], start=False, stop=False)
                            nc.tensor.matmul(bank2[:, qt * P:w], identb[:], maskb[:], start=False, stop=False,
                                             skip_group_check=True)
                            nc.tensor.matmul(dst, hi, k2z[:, j, u % 2, 1, 0:w], start=False, stop=True).then_inc(s_ready, 1)
                    elif kind == "T2":
                        pe.wait_ge(pn_ready, step_no(b, n) + 1)
                        pe.wait_ge(pt_ready, 1 + step_no(b, n))
                        for j in range(2):
                            for kt in range(n % NT + 1):
                                i = nc.tensor.transpose(T[:, j, kt * P:(kt + 1) * P], probs[:, n % 3, j, kt * P:(kt + 1) * P], ident[:])
                        i.then_inc(t_ready, 1)
                    elif kind == "PV2":
                        pe.wait_ge(pt_ready, 1 + step_no(b, NT * n + NT))
                        dst = bank(b, "PV2", n, *(("V2", i) for i in range(2 * NT)))
                        for kt in range(NT):
                            for j in range(2):
                                h = 2 * n + j
                                i = nc.tensor.matmul(dst[64 * j:64 * j + 64, kt * P:SEQ], v2s[:, kt, h * HD2:(h + 1) * HD2],
                                                     pT[:, n % 2, j, kt, kt * P:SEQ], start=(kt == 0), stop=(kt == NT - 1),
                                                     skip_group_check=True)
                        i.then_inc(g_ready, 1)
                    elif kind == "x2T":
                        pe.wait_ge(ln_done, (2 * b + 2) * NT)
                        transposed(b, "x2T", n, x2s)
                    elif kind == "gate":
                        pe.wait_ge(w_ffn, 16 * 4)
                        dst = bank(b, "gate", 0, ("x2T", 0), ("x2T", 1))
                        for t in range(NT):
                            i = product(dst[:, t * (E + 1):(t + 1) * (E + 1)], [xT[:, c, t * P:(t + 1) * P] for c in range(DC)],
                                        [gw[:, c, :] for c in range(DC)])
                        i.then_inc(g_ready, 1)
                    elif kind == "keys":
                        pe.wait_ge(keyv_done, 1 + b + 1)
                        dst = bank(b, "keys", 0)
                        alone(pe)
                        for t in range(2):
                            i = nc.tensor.transpose(dst[:, t * P:(t + 1) * P], keyv[:, t, :, :].rearrange("p h e -> p (h e)"), ident[:])
                        i.then_inc(g_ready, 1)
                    elif kind == "up":
                        for j in range(2):
                            product(scores(b, "up", n, j), [supw[:, c, j * FS + n * P:j * FS + (n + 1) * P] for c in range(DC)],
                                    [xT[:, c, :] for c in range(DC)]).then_inc(s_ready, 1)
                    elif kind == "down":
                        s_landed(pe, b, *(("up", f) for f in range(FS // P)))
                        dst = bank(b, "down", n)
                        for t in range(2):
                            tt = 2 * n + t
                            i = product(dst[:, t * D:(t + 1) * D], [hid[:, f, tt * P:(tt + 1) * P] for f in range(FS // P)],
                                        [sdownw[:, f, :] for f in range(FS // P)])
                        i.then_inc(g_ready, 1)

            pe.wait_ge(pick, 1 + B * ROUND_STEPS + 2 * (CAP // 8 - EARLY))
            nc.tensor.transpose(T[:, 0, 0:P], found[:], ident[:]).then_inc(firstT, 1)
            pe.wait_ge(found_copied, 1)
            nc.tensor.matmul(T[:, 1, 0:E], turned[:], found_rows[:, E:2 * E], start=True, stop=True).then_inc(found_turned, 1)

            def bank_of(s):
                return S[:, s % PU // 2, s % 2, :]

            def tokens(r, s, first_turn):
                if s >= PU or not first_turn:
                    pe.wait_ge(e_act, r * EU + s + 1 - PU)
                pe.wait_ge(xg_in[s], 16 * (r + 1))
                for c in range(DC):
                    i = nc.tensor.transpose(bank_of(s)[:, c * P:(c + 1) * P], xg[:, s, c * P:(c + 1) * P], ident[:])
                i.then_inc(e_tr, 1)

            def up(r, s):
                pe.wait_ge(e_trs, r * EU + s + 1)
                pe.wait_ge(we_in[s % EU], 32 * (r + 1 if s >= 0 else r))
                for half in range(2):
                    i = product(bank_of(s % EU)[:, 256 + half * P:256 + (half + 1) * P],
                                [wup[:, s % EU, c, half * FI:(half + 1) * FI] for c in range(DC)],
                                [xgT[:, s % PU, c * P:(c + 1) * P] for c in range(DC)])
                i.then_inc(e_up, 1)

            def down(r, s, first_turn):
                pe.wait_ge(e_act, r * EU + s + 1)
                if s >= PU or not first_turn:
                    pe.wait_ge(e_yo, r * EU + s + 1 - PU)
                nc.tensor.matmul(out_of(s)[:, 0:D], act[:, s % PU, :], wdn[:, s % EU, :], start=True, stop=True).then_inc(e_down, 1)

            def experts(r, first_turn=False):
                for s in range(EU):
                    tokens(r, s, first_turn)
                    if s >= 1 or not first_turn:
                        up(r, s - 1)
                    if s >= 2 or not first_turn:
                        down(r, s - 2, first_turn)

            experts(0, first_turn=True)
            with pe.Fori(1, TURNS) as r:
                experts(r)
            down(TURNS, -2, False)
            up(TURNS, -1)
            down(TURNS, -1, False)

        @block.scalar
        def _(a):
            def evac(b, use, n, dst, bias=None):
                g_written(a, b, use, n)
                if bias is None:
                    nc.scalar.copy(dst, g_bank(use, n)).then_inc(g_sem(use, n), 1)
                else:
                    nc.scalar.activation(dst, g_bank(use, n), ACT.Identity, bias=bias).then_inc(g_sem(use, n), 1)

            def softmax(b, n):
                w = (n % NT + 1) * P
                a.wait_ge(nm_ready, step_no(b, n) + 1)
                if n >= 3:
                    a.wait_ge(t_ready, step_no(b, n - 2))
                for j in range(2):
                    nc.scalar.activation(probs[:, n % 3, j, 0:w], s_slot("S2", n)[:, j, 0:w], ACT.Exp, bias=negmax[:, n % 4, j:j + 1],
                                             accum_out=rowsum[:, n % 4, j:j + 1]).then_inc(s_sem("S2", n, j), 1)

            for c in range(DC):
                a.dma_start(wv2[:, c, :].rearrange("p (h e) -> p h e", h=H),
                            WV[:, c * P:(c + 1) * P, :].rearrange("h p e -> p h e"), allow_slow_non_contiguous=True).then_inc(w_values, 16)
            a.wait_ge(ones_done, 4)
            a.wait_ge(wprep, 2)

            def head_part(b, kind, n):
                if kind == "xT":
                    evac(b, kind, n, xT[:, n, :])
                elif kind == "cT":
                    evac(b, kind, n, cT[:, n, :])
                elif kind == "q1":
                    g_written(a, b, "q1", n)
                    a.wait_ge(parts_out, 1 + 64 * head_no(b))
                    nc.scalar.activation(parts[:, n, 0, :], g_bank("q1", n), ACT.Identity, bias=bq1c[:, n:n + 1]).then_inc(hi_done, 1)
                elif kind == "k1":
                    g_written(a, b, "k1", 0)
                    nc.scalar.activation(k1parts[:, 0, :], g_bank("k1", 0)[0:64, :], ACT.Identity, bias=bk1c[:]).then_inc(hi_done, 1)

            for kind, n in head:
                head_part(FIRST, kind, n)
            for g in range(3):
                a.wait_ge(q1_in[g], 80)
            cross_loads = [
                (bkc[:], bK.rearrange("(u j) e -> (j e) u", j=2)),
                (bqc[:], bQ.rearrange("(u j) e -> (j e) u", j=2)),
                (bvc[:], bV.rearrange("(u j) e -> (j e) u", j=2)),
                (bo2r[:], bO.rearrange("(o n) -> o n", o=1).to_broadcast([P, D])),
                (wo2[:], WO.rearrange("(u j) e d -> (j e) u d", j=2)),
            ]
            for w, src in ((wk2, WK), (wq2, WQ)):
                for c in range(DC):
                    cross_loads.append((w[:, c, :].rearrange("p (h e) -> p h e", h=H),
                                        src[:, c * P:(c + 1) * P, :].rearrange("h p e -> p h e")))
            a.wait_ge(id_zero, 2)
            for g in range(4):
                cross_loads.append((wo1[32 * g:32 * g + HD1, :, :],
                                    Wo1[4 * g * HD1:4 * (g + 1) * HD1, :].rearrange("(kv d) n -> d kv n", kv=KV1)))
            assert len(cross_loads) == W_CROSS
            for dst, src in cross_loads:
                a.dma_start(dst, src, allow_slow_non_contiguous=True).then_inc(w_cross, 16)
            for dst, src in ((gw[:, :, 0:E], gate_w), (gw[:, :, E:E + 1], sgate_w), (supw[:], sup_w), (sdownw[:], sdown_w)):
                a.dma_start(dst, src.rearrange("(c p) n -> p c n", p=P), allow_slow_non_contiguous=True).then_inc(w_ffn, 16)
            a.wait_ge(consts, CONSTS)
            with a.Fori(0, B) as b:
                for kind, n in batch_timeline("scalar"):
                    if (kind, n) in head:
                        head_part(b, kind, n)
                    elif kind in ("x1T", "x2T"):
                        evac(b, kind, n, xT[:, n, :])
                    elif kind == "V2":
                        if n >= NT or n % 2 == 0:
                            evac(b, "V2", n, v2s[:, n // 2, n % 2 * 512:(n % 2 + 1) * 512])
                    elif kind == "Q2":
                        g_written(a, b, "q2", n)
                        nc.scalar.activation(parts[:, n % 2, 0, :], g_bank("q2", n), ACT.Identity, bias=bqc[:, n:n + 1]).then_inc(hi_done, 1)
                    elif kind == "K2":
                        if n == 0:
                            a.wait_ge(w_cross, 16 * W_CROSS)
                        g_written(a, b, "k2", n)
                        for j in range(2):
                            r = slice(64 * j, 64 * j + 64)
                            i = nc.scalar.activation(k2z[r, j, n % 2, 0, :], g_bank("k2", n)[r, :], ACT.Identity, bias=bkc[r, n:n + 1])
                        i.then_inc(hi_done, 1)
                    elif kind == "NT":
                        g_written(a, b, "nt", n)
                        if n >= 1:
                            a.wait_ge(nm_in[(n - 1) % 3], 16 * (b * (2 if (n - 1) % 3 == 0 else 1) + (n - 1) // 3 + 1))
                        nc.scalar.copy(negrow[:], g_bank("nt", n)[0:4 * NT, 0:P]).then_inc(g_sem("nt", n), 1)
                    elif kind == "X":
                        g, i = n
                        if n == (0, 0):
                            a.wait_ge(batch_out, 1 + b)
                        for j in range(2):
                            s_written(a, b, "X", n, j)
                            nc.scalar.activation(p1[:, i // 2, 2 * (i % 2) + j, :], s_slot("X", n)[:, j, :], ACT.Exp).then_inc(s_sem("X", n, j), 1)
                    elif kind == "E1":
                        a.wait_ge(z_ready, b * KV1 + n + 1)
                        nc.scalar.copy(zT[:, n, :], T[:, n % 2, :]).then_inc(z_copied, 1)
                    elif kind == "S2":
                        softmax(b, n)
                    elif kind == "T2" and n % 2 == 1:
                        turn(a, nc.scalar.copy, b, n)
                    elif kind == "PV2":
                        evac(b, "PV2", n, zT[:, n, :], bvc[:, n:n + 1])
                    elif kind == "gate":
                        a.wait_ge(gmax_done, b + 1)
                        for t in range(NT):
                            nc.scalar.activation(gexp[:, t, :], g_bank("gate", 0)[:, t * (E + 1):t * (E + 1) + E], ACT.Exp,
                                                 bias=gneg[:, t:t + 1], accum_out=gsum[:, t:t + 1])
                        nc.scalar.activation(gtmp[:, :, 0], g_bank("gate", 0)[:, 0:NT * (E + 1)].rearrange("p (t e) -> p t e", t=NT)[:, :, E],
                                             ACT.Tanh, scale=0.5).then_inc(g_sem("gate", 0), 1)
                    elif kind == "keys":
                        g_written(a, b, "keys", 0)
                        nc.scalar.copy(keys[:, CAP:], g_bank("keys", 0)[:, 0:SEQ // 2]).then_inc(keys_in, 1)
                        a.wait_ge(keys_in, 1 + b + 1)
                        a.sem_inc(g_sem("keys", 0), 1)
                    elif kind == "up":
                        s_written(a, b, "up", n)
                        if n >= 2:
                            a.wait_ge(gated, b * (FS // P) + n - 1)
                        nc.scalar.activation(tnh[:, n % 2, :], s_slot("up", n)[:, 0, :], ACT.Tanh, scale=0.5).then_inc(tanh_done, 1)

            def hidden(r, s):
                a.wait_ge(e_up, r * EU + s + 1)
                nc.scalar.activation(ath[:, s % PU, :], S[:, s % PU // 2, s % 2, 256:256 + FI], ACT.Tanh, scale=0.5).then_inc(e_tanh, 1)

            def experts(r, first_turn=False):
                for s in range(EU):
                    a.wait_ge(e_tr, r * EU + s + 1)
                    if s >= PU or not first_turn:
                        a.wait_ge(e_up, r * EU + s + 1 - PU)
                    nc.scalar.copy(xgT[:, s % PU, :], S[:, s % PU // 2, s % 2, 0:D]).then_inc(e_trs, 1)
                    if s >= 1 or not first_turn:
                        hidden(r, s - 1)

            experts(0, first_turn=True)
            with a.Fori(1, TURNS) as r:
                experts(r)
            hidden(TURNS, -1)

        @block.vector
        def _(v):
            def low_part(b, event, dst, src, bias, hi):
                v.wait_ge(hi_done, hi_first[event] + 1 if b is FIRST else len(hi_first) + b * len(hi_index) + hi_index[event] + 1)
                return nc.vector.scalar_tensor_tensor(out=dst, in0=src, scalar=bias, in1=hi.bitcast(F32), op0=ALU.add, op1=ALU.subtract)

            def maxima(b, n):
                w = (n % NT + 1) * P
                s_written(v, b, "S2", n)
                nc.vector.tensor_reduce(negmax[:, n % 4, :], s_slot("S2", n)[:, :, 0:w], AX_X, ALU.max, negate=True).then_inc(nm_ready, 1)

            def divide(b, n):
                w = (n % NT + 1) * P
                s_landed(v, b, ("S2", n))
                nc.vector.reciprocal(rrow[:, n % 4, :], rowsum[:, n % 4, :]).then_inc(rr_ready, 1)
                v.wait_ge(rr_ready, step_no(b, n) + 1)
                for j in range(2):
                    i = nc.vector.tensor_scalar(probs[:, n % 3, j, 0:w], probs[:, n % 3, j, 0:w], rrow[:, n % 4, j:j + 1], None, ALU.mult)
                i.then_inc(pn_ready, 1)

            def statistics(k, tile, half):
                v.wait_ge(res_done, 2 * k + half + 1)
                for t in (2 * half, 2 * half + 1):
                    nc.vector.bn_stats(stats[:, t, :], tile[:, t, 0:D]).then_inc(st_done, 1)

            def aggregate(k):
                v.wait_ge(st_done, NT * (k + 1))
                alone(v)
                for t in range(NT):
                    nc.vector.bn_aggr(mv[:, t, :], stats[:, t, :]).then_inc(ag_done, 1)

            def normalize(k, tile):
                v.wait_ge(rs_done, k + 1)
                for t in range(NT):
                    nc.vector.tensor_scalar(tile[:, t, 0:D], tile[:, t, 0:D], mv[:, t, 0:1], rstd[:, t:t + 1],
                                            ALU.subtract, ALU.mult).then_inc(ln_done, 1)

            def search(b, r):
                at = 1 + b * ROUND_STEPS + 2 * (r - EARLY if r >= EARLY else CAP // 8 - EARLY + r)
                v.wait_ge(pick, at)
                alone(v)
                nc.vector.max(found[:, 8 * r:8 * r + 8], keys[:]).then_inc(pick, 1)
                v.wait_ge(pick, at + 1)
                alone(v)
                nc.vector.match_replace(keys[:], found[:, 8 * r:8 * r + 8], keys[:], 0.0).then_inc(pick, 1)

            nc.vector.memset(q1st[:].bitcast(F32), 0.0).then_inc(ones_done, 1)
            nc.vector.memset(parts[:].bitcast(F32), 0.0).then_inc(ones_done, 1)
            nc.vector.memset(k1st[KQ - 1:, :, :].bitcast(F32), 0.0).then_inc(ones_done, 1)
            v.wait_ge(ones_done, 3)
            nc.vector.memset(k1st[KQ - 1:KQ, :, :].bitcast(F32), 1.0).then_inc(ones_done, 1)
            v.wait_ge(wprep, 2)

            def head_part(b, kind, n):
                if kind == "q1":
                    low_part(b, ("q1", n), parts[:, n, 1, :], g_bank("q1", n), bq1c[:, n:n + 1], parts[:, n, 0, :]).then_inc(g_sem("q1", n), 1)
                elif kind == "k1":
                    low_part(b, ("k1", 0), k1parts[:, 1, :], g_bank("k1", 0)[0:64, :], bk1c[:], k1parts[:, 0, :]).then_inc(g_sem("k1", 0), 1)
                elif kind == "v1":
                    if b is FIRST:
                        v.wait_ge(v1_done, 1)
                    g_written(v, b, "v1", 0)
                    for t in range(NT):
                        i = nc.vector.tensor_tensor(v1s[:, t, :, 0:HD1], g_bank("v1", 0)[:, t * 64:(t + 1) * 64].rearrange("p (h d) -> p h d", h=KV1),
                                                    bv1r[:].rearrange("p (h d) -> p h d", h=KV1), ALU.add)
                    i.then_inc(g_sem("v1", 0), 1)

            for kind, n in head:
                head_part(FIRST, kind, n)
            v.wait_ge(consts, CONSTS)
            with v.Fori(0, B) as b:
                for kind, n in batch_timeline("vector"):
                    if (kind, n) in head:
                        head_part(b, kind, n)
                    elif kind == "V2":
                        if n < NT and n % 2 == 1:
                            g_written(v, b, "V2", n)
                            nc.vector.tensor_copy(v2s[:, n // 2, 512:1024], g_bank("V2", n)).then_inc(g_sem("V2", n), 1)
                    elif kind == "K2":
                        for j in range(2):
                            r = slice(64 * j, 64 * j + 64)
                            i = low_part(b, ("K2", n), k2z[r, j, n % 2, 1, :], g_bank("k2", n)[r, :], bkc[r, n:n + 1],
                                         k2z[r, j, n % 2, 0, :])
                        i.then_inc(g_sem("k2", n), 1)
                    elif kind == "Q2":
                        low_part(b, ("Q2", n), parts[:, n % 2, 1, :], g_bank("q2", n), bqc[:, n:n + 1], parts[:, n % 2, 0, :]).then_inc(g_sem("q2", n), 1)
                    elif kind == "pick":
                        if n == 0:
                            v.wait_ge(keys_in, 1 + b + 1)
                            v.wait_ge(kept, 1 + b + 1)
                        search(b, n)
                        if n == CAP // 8 - 1:
                            v.wait_ge(pick, 1 + b * ROUND_STEPS + 2 * (CAP // 8 - EARLY))
                            nc.vector.tensor_copy(keys[:, 0:CAP], found[:]).then_inc(kept, 1)
                    elif kind == "M":
                        g, i = n
                        for j in range(2):
                            h = 2 * (i % 2) + j
                            s_written(v, b, "M", n, j)
                            nc.vector.tensor_reduce(negmax1[:, g % 2, h:h + 1, i // 2], s_slot("M", n)[:, j, :], AX_X, ALU.max,
                                                    negate=True).then_inc(s_sem("M", n, j), 1)
                    elif kind == "SM":
                        g_written(v, b, "sm", n)
                        nc.vector.reciprocal(rsum1[:], g_bank("sm", n)[:, 0:4 * NT]).then_inc(rsum1_done, 1)
                        v.wait_ge(rsum1_done, b * KV1 + n + 1)
                        nc.vector.tensor_copy(rwide.rearrange("p (s o) -> p s o", o=32),
                                              rsum1[:].rearrange("p (s o) -> p s o", o=1).to_broadcast([P, 4 * NT, 32])).then_inc(g_sem("sm", n), 1)
                    elif kind == "RS":
                        g_written(v, b, "rs", n)
                        nc.vector.tensor_tensor(zT[:, n, :], g_bank("rs", n), zT[:, n, :], ALU.mult).then_inc(z_divided, 1)
                        v.wait_ge(z_divided, b * KV1 + n + 1)
                        v.sem_inc(g_sem("rs", n), 1)
                    elif kind == "S2":
                        maxima(b, n)
                    elif kind == "R2":
                        divide(b, n)
                    elif kind == "T2" and n % 2 == 0:
                        turn(v, nc.vector.tensor_copy, b, n)
                    elif kind in ("o1", "o2"):
                        tile = x1s if kind == "o1" else x2s
                        if n == 0:
                            v.wait_ge(*((base1, 1 + b + 1) if kind == "o1" else (base2, b + 1)))
                        g_written(v, b, kind, n)
                        dst = tile[:, 2 * n:2 * n + 2, 0:D]
                        nc.vector.tensor_tensor(dst, g_bank(kind, n).rearrange("p (t n) -> p t n", t=2), dst, ALU.add).then_inc(res_done, 1)
                        v.wait_ge(res_done, 4 * b + (0 if kind == "o1" else 2) + n + 1)
                        v.sem_inc(g_sem(kind, n), 1)
                        statistics(2 * b + (kind == "o2"), tile, n)
                    elif kind in ("ln1", "ln2"):
                        aggregate(2 * b + (kind == "ln2"))
                    elif kind in ("norm1", "norm2"):
                        normalize(2 * b + (kind == "norm2"), x1s if kind == "norm1" else x2s)
                    elif kind == "gate":
                        g_written(v, b, "gate", 0)
                        logits = g_bank("gate", 0)[:, 0:NT * (E + 1)].rearrange("p (t e) -> p t e", t=NT)[:, :, 0:E]
                        nc.vector.tensor_reduce(gneg[:], logits, AX_X, ALU.max, negate=True).then_inc(gmax_done, 1)
                        g_landed(v, b, "gate", 0)
                        v.wait_ge(keyv_done, 1 + b)
                        GS = 10
                        at = [0]

                        def link(i):
                            at[0] += 1
                            i.then_inc(gate_step, 1)
                            v.wait_ge(gate_step, b * GS + at[0])
                            alone(v)

                        def wide(t):
                            return t.rearrange("p (t o) -> p t o", o=1).to_broadcast([P, NT, E])

                        link(nc.vector.tensor_scalar(sig[:], gtmp[:, :, 0], 1.0, 0.5, ALU.add, ALU.mult))
                        link(nc.vector.reciprocal(gtmp[:, :, 1], gsum[:]))
                        link(nc.vector.tensor_tensor(gprob[:], gexp[:], wide(gtmp[:, :, 1]), ALU.mult))
                        for t in range(NT):
                            i = nc.vector.max(top8[:, t, :], gprob[:, t, :])
                        link(i)
                        for t in range(NT):
                            i = nc.vector.match_replace(grest[:, t, :], top8[:, t, :], gprob[:, t, :], -1.0)
                        link(i)
                        link(nc.vector.reduce_sum(gtmp[:, :, 2], top8[:], AX_X))
                        link(nc.vector.reciprocal(gtmp[:, :, 3], gtmp[:, :, 2]))
                        link(nc.vector.tensor_tensor(gprob[:], gprob[:], wide(gtmp[:, :, 3]), ALU.mult))
                        link(nc.vector.scalar_tensor_tensor(out=x2s[:, :, D:ROW], in0=grest[:], scalar=0.0, in1=gprob[:],
                                                            op0=ALU.is_lt, op1=ALU.mult))
                        for t in range(NT):
                            i = nc.vector.tensor_scalar(keyv[:, t % 2, t // 2, :], grest[:, t, :], 0.0, token_key[:, t:t + 1], ALU.is_lt, ALU.mult)
                        link(i)
                        nc.vector.tensor_scalar(token_key[:], token_key[:], -float(SEQ), None, ALU.add).then_inc(keyv_done, 1)
                        assert at[0] == GS, at
                    elif kind == "up":
                        v.wait_ge(tanh_done, b * (FS // P) + n + 1)
                        nc.vector.scalar_tensor_tensor(out=hid[:, n, :], in0=tnh[:, n % 2, :], scalar=1.0, in1=s_slot("up", n)[:, 0, :],
                                                       op0=ALU.add, op1=ALU.mult).then_inc(gated, 1)
                        v.wait_ge(gated, b * (FS // P) + n + 1)
                        v.sem_inc(s_sem("up", n, 0), 1)
                        nc.vector.scalar_tensor_tensor(out=hid[:, n, :], in0=hid[:, n, :], scalar=0.5, in1=s_slot("up", n)[:, 1, :],
                                                       op0=ALU.mult, op1=ALU.mult).then_inc(s_sem("up", n, 1), 1)
                    elif kind == "down":
                        if n == 0:
                            v.wait_ge(batch_out, 1 + b)
                        g_written(v, b, "down", n)
                        for t in range(2):
                            tt = 2 * n + t
                            i = nc.vector.scalar_tensor_tensor(out=y0s[:, tt, :], in0=g_bank("down", n)[:, t * D:(t + 1) * D],
                                                               scalar=sig[:, tt:tt + 1], in1=x2s[:, tt, 0:D], op0=ALU.mult, op1=ALU.add)
                        i.then_inc(y0_done, 1)
                        v.wait_ge(y0_done, 2 * b + n + 1)
                        v.sem_inc(g_sem("down", n), 1)

            for r in range(EARLY, CAP // 8):
                search(B, r)
            v.wait_ge(firstT, 1)
            nc.vector.tensor_copy(found_rows, T[:, 0, 0:P]).then_inc(found_copied, 1)
            v.wait_ge(found_copied, 1)
            v.wait_ge(found_turned, 1)
            nc.vector.tensor_tensor(first, T[:, 1, 0:E], found_rows[:, 0:E], ALU.max).then_inc(idx_step, 1)
            v.wait_ge(idx_step, 1)
            nc.vector.tensor_scalar(idxf[:, 0, :], first, 0.0, slot_no[:], ALU.is_equal, ALU.mult).then_inc(idx_step, 1)
            nc.vector.tensor_scalar(idxf[:, 1, :], first, -1.0, float(TOK), ALU.mult, ALU.add).then_inc(idx_step, 1)
            v.wait_ge(idx_step, 3)
            nc.vector.tensor_tensor(idx[:], idxf[:, 0, :], idxf[:, 1, :], ALU.add).then_inc(idx_step, 1)
            v.wait_ge(idx_step, 4)
            nc.vector.tensor_copy(idx_gather[:], idx[:, 0:EU]).then_inc(idx0_done, 1)

            def hidden(r, s, first_turn):
                v.wait_ge(e_tanh, r * EU + s + 1)
                if s >= PU or not first_turn:
                    v.wait_ge(e_down, r * EU + s + 1 - PU)
                up = S[:, s % PU // 2, s % 2, 256:512]
                nc.vector.scalar_tensor_tensor(out=act[:, s % PU, :], in0=ath[:, s % PU, :], scalar=1.0, in1=up[:, 0:FI],
                                               op0=ALU.add, op1=ALU.mult).then_inc(e_act1, 1)
                v.wait_ge(e_act1, r * EU + s + 1)
                nc.vector.scalar_tensor_tensor(out=act[:, s % PU, :], in0=act[:, s % PU, :], scalar=0.5, in1=up[:, FI:2 * FI],
                                               op0=ALU.mult, op1=ALU.mult).then_inc(e_act, 1)

            def output(r, s, first_turn, last_turn):
                slot, n = s % EU, r * EU + s
                v.wait_ge(e_down, n + 1)
                if s >= PU or not first_turn:
                    v.wait_ge(y_add[(s - PU) % EU], 16 * (r + 1 if s >= PU else r))
                nc.vector.tensor_copy(idx_add[:, slot:slot + 1], idx[:, bass.ds(n, 1)])
                if not last_turn:
                    nc.vector.tensor_copy(idx_gather[:, slot:slot + 1], idx[:, bass.ds(n + EU, 1)])
                nc.vector.tensor_scalar(yo[:, s % PU, :], out_of(s)[:, 0:D], xg[:, slot, bass.ds(n + D, 1)], None,
                                        ALU.mult).then_inc(e_yo, 1)

            def experts(r, first_turn=False, last_turn=False):
                for s in range(EU):
                    if s >= 1 or not first_turn:
                        hidden(r, s - 1, first_turn)
                    if s >= 2 or not first_turn:
                        output(r, s - 2, first_turn, last_turn and s >= 2)

            experts(0, first_turn=True)
            with v.Fori(1, TURNS - 1) as r:
                experts(r)
            experts(TURNS - 1, last_turn=True)
            output(TURNS, -2, False, True)
            hidden(TURNS, -1, False)
            output(TURNS, -1, False, True)

            with v.Fori(0, B // FB) as k:
                for part in range(FB):
                    v.wait_ge(f_in[part], 32 * (k + 1))
                    for t in range(2):
                        rows = slice(2 * t, 2 * t + 2)
                        nc.vector.tensor_tensor(fin[part][:, rows, :], fin[part][:, rows, :], fin1[part][:, rows, :],
                                                ALU.add).then_inc(res_done, 1)
                        statistics(2 * B + FB * k + part, fin[part], t)
                    aggregate(2 * B + FB * k + part)
                    normalize(2 * B + FB * k + part, fin[part])


_INS = ["x", "ctx_1024", "L0_attn_Wq", "L0_attn_bq", "L0_attn_Wk", "L0_attn_bk", "L0_attn_Wv", "L0_attn_bv",
        "L0_attn_Wo", "L0_attn_bo", "L0_xattn_W_Q", "L0_xattn_W_K", "L0_xattn_W_V", "L0_xattn_W_O",
        "L0_xattn_b_Q", "L0_xattn_b_K", "L0_xattn_b_V", "L0_xattn_b_O", "L0_ffn_gate_w", "L0_ffn_shared_gate_w",
        "L0_ffn_shared_gate_up_w", "L0_ffn_shared_down_w", "L0_ffn_expert_gate_up_w", "L0_ffn_expert_down_w"]


def kernel(**inputs):
    import numpy as _np
    import concourse.bacc as _bacc
    from concourse import mybir as _mybir
    from concourse.bass_utils import run_bass_kernel_spmd as _run

    nc = _bacc.Bacc("TRN2", target_bir_lowering=False, num_devices=1)
    arrays, args = {}, []
    for name in _INS:
        a = _np.ascontiguousarray(inputs[name])
        arrays[f"in_{name}_dram"] = a
        args.append(nc.dram_tensor(f"in_{name}_dram", a.shape, _mybir.dt.from_np(a.dtype), kind="ExternalInput").ap())
    out = nc.dram_tensor("out_0_dram", (B, SEQ, D), F32, kind="ExternalOutput").ap()
    build(nc, *args, out)
    r = _run(nc, [arrays], core_ids=[0])
    return r.results[0]["out_0_dram"]
```
